# Optimizing a Trainium2 kernel written in Bass

```python
import numpy as np
import jax
import jax.numpy as jnp

def _softmax(x, axis=-1):
    return jax.nn.softmax(x, axis=axis)

def _gelu(x):
    return jax.nn.gelu(x, approximate=True)

def _silu(x):
    return jax.nn.silu(x)

def _sigmoid(x):
    return jax.nn.sigmoid(x)

def _layernorm(x, axis=-1, eps=1e-05):
    m = jnp.mean(x, axis=axis, keepdims=True)
    v = jnp.var(x, axis=axis, keepdims=True)
    return (x - m) / jnp.sqrt(v + eps)

def _scatter_add(tgt, idx, src, axis=0):
    return tgt.at[idx].add(src)

def _segment_sum(src, seg, n):
    return jax.ops.segment_sum(src, seg, n)
kernel_name = 'mk_vit_tower_cls_d2_tok_img512_r4_72f138'

def setup_inputs(seed: int=0):
    np.random.seed(seed)
    _w = jnp.asarray

    def _rec_inputs():
        import jax
        import jax.numpy as jnp
        _rk = jax.random.key(seed)
        x = -0.000392918 + 0.999932 * jax.random.normal(jax.random.fold_in(_rk, 1), (16, 1, 128, 128), jnp.float32)
        cls_tok = 0.02 * jax.random.normal(jax.random.fold_in(_rk, 5), (1, 1, 128), jnp.float32)
        return (x, cls_tok)
    x, cls_tok = _rec_inputs()

    def _L0_tok_setup():
        import math
        import jax, jax.numpy as jnp
        import numpy as np
        PW = PH = 16
        EMB = 128
        HID = 128
        B, H, W = (64, 128, 128)
        L = H // PW * (W // PH)
        SIGMA_ZERO = 0.1

        def _f_noise(x):
            return jnp.sign(x) * jnp.sqrt(jnp.abs(x))

        def _noisy_linear(x, w, b, sw, sb, eps_in, eps_out):
            ei = _f_noise(eps_in)
            eo = _f_noise(eps_out)
            w_n = w + sw * (eo[:, None] * ei[None, :])
            b_n = b + sb * eo
            return x @ w_n.T + b_n

        def _unfold_patches(x):
            b = x.shape[0]
            p = x.reshape(b, H // PW, PW, W // PH, PH)
            p = p.transpose(0, 1, 3, 2, 4)
            return p.reshape(b, L, PW * PH)

        def _pos_encoding(x):
            pos = jnp.arange(L, dtype=jnp.float32)[:, None]
            div = jnp.exp(jnp.arange(0, EMB, 2, dtype=jnp.float32) * (-math.log(10000.0) / EMB))
            ang = pos * div
            pe = jnp.stack([jnp.sin(ang), jnp.cos(ang)], axis=-1).reshape(L, EMB)
            return x + pe[None, :, :]
        key = jax.random.key(seed)
        ks = jax.random.split(key, 12)
        in_f = PW * PH
        sig = SIGMA_ZERO / math.sqrt(in_f)
        bnd1 = 1.0 / math.sqrt(in_f)
        bnd3 = 1.0 / math.sqrt(HID)
        u = lambda k, shape, bnd: jax.random.uniform(k, shape, jnp.float32, -bnd, bnd)
        return {'inputs': jax.random.normal(ks[0], (B, 1, H, W), jnp.float32), 'W1_w': u(ks[1], (HID, in_f), bnd1), 'W1_b': u(ks[2], (HID,), bnd1), 'W1_sw': jnp.full((HID, in_f), sig, jnp.float32), 'W1_sb': jnp.full((HID,), sig, jnp.float32), 'W2_w': u(ks[3], (HID, in_f), bnd1), 'W2_b': u(ks[4], (HID,), bnd1), 'W2_sw': jnp.full((HID, in_f), sig, jnp.float32), 'W2_sb': jnp.full((HID,), sig, jnp.float32), 'W3_w': u(ks[5], (EMB, HID), bnd3), 'W3_b': u(ks[6], (EMB,), bnd3), 'eps_in1': jax.random.normal(ks[7], (in_f,), jnp.float32), 'eps_out1': jax.random.normal(ks[8], (HID,), jnp.float32), 'eps_in2': jax.random.normal(ks[9], (in_f,), jnp.float32), 'eps_out2': jax.random.normal(ks[10], (HID,), jnp.float32)}
    _L0_tok_all = _L0_tok_setup()
    _L0_tok_in = {k: v for k, v in _L0_tok_all.items() if k in ('W1_w', 'W1_b', 'W1_sw', 'W1_sb', 'W2_w', 'W2_b', 'W2_sw', 'W2_sb', 'W3_w', 'W3_b', 'eps_in1', 'eps_out1', 'eps_in2', 'eps_out2')}
    del _L0_tok_all

    def _L0_attn_setup():
        import jax, jax.numpy as jnp
        import numpy as np
        D_MODEL = 128
        N_PAIRS = D_MODEL // 2
        B, T = (8, 1024)

        def _givens_ssm(x_seq, W_angle, b_angle, W_decay, b_decay, W_input, b_input):
            Bb, Tt, D = x_seq.shape
            P = D // 2
            angles = jnp.einsum('btd,dp->btp', x_seq, W_angle) + b_angle
            decays = jax.nn.sigmoid(jnp.einsum('btd,dk->btk', x_seq, W_decay) + b_decay)[..., 0]
            inj = jnp.einsum('btd,de->bte', x_seq, W_input) + b_input
            inj = inj.reshape(Bb, Tt, P, 2)

            def step(h, inp):
                a, d, u = inp
                c, s = (jnp.cos(a), jnp.sin(a))
                he = c * h[..., 0] - s * h[..., 1]
                ho = s * h[..., 0] + c * h[..., 1]
                h_new = d[:, None, None] * jnp.stack([he, ho], axis=-1) + u
                return (h_new, h_new)
            h0 = jnp.zeros((Bb, P, 2), x_seq.dtype)
            xs = (jnp.swapaxes(angles, 0, 1), jnp.swapaxes(decays, 0, 1), jnp.swapaxes(inj, 0, 1))
            _, states = jax.lax.scan(step, h0, xs)
            return jnp.swapaxes(states, 0, 1).reshape(Bb, Tt, D)
        key = jax.random.key(seed)
        ks = jax.random.split(key, 7)
        scale = 1.0 / np.sqrt(D_MODEL)
        return {'x_seq': jax.random.normal(ks[0], (B, T, D_MODEL), dtype=jnp.float32), 'W_angle': jax.random.uniform(ks[1], (D_MODEL, N_PAIRS), jnp.float32, -scale, scale), 'b_angle': jnp.zeros((N_PAIRS,), jnp.float32), 'W_decay': jax.random.uniform(ks[2], (D_MODEL, 1), jnp.float32, -scale, scale), 'b_decay': jnp.full((1,), 1.4, jnp.float32), 'W_input': jax.random.uniform(ks[3], (D_MODEL, D_MODEL), jnp.float32, -scale, scale), 'b_input': jax.random.uniform(ks[4], (D_MODEL,), jnp.float32, -scale, scale)}
    _L0_attn_all = _L0_attn_setup()
    _L0_attn_in = {k: v for k, v in _L0_attn_all.items() if k in ('W_angle', 'b_angle', 'W_decay', 'b_decay', 'W_input', 'b_input')}
    del _L0_attn_all

    def _L0_ffn_setup():
        import jax, jax.numpy as jnp
        import numpy as np
        B, L, H, E, F, C = (8, 2048, 128, 8, 256, 2)
        key = jax.random.key(seed)
        ks = jax.random.split(key, 4)
        x = jax.random.normal(ks[0], (B, L, H), jnp.float32)
        Wg = jax.random.normal(ks[1], (H, E), jnp.float32) * H ** (-0.5)
        W1 = jax.random.normal(ks[2], (E, H, F), jnp.float32) * H ** (-0.5)
        b1 = jnp.zeros((E, F), jnp.float32)
        W2 = jax.random.normal(ks[3], (E, F, H), jnp.float32) * F ** (-0.5)
        b2 = jnp.zeros((E, H), jnp.float32)
        return {'x': x, 'Wg': Wg, 'W1': W1, 'b1': b1, 'W2': W2, 'b2': b2}
    _L0_ffn_all = _L0_ffn_setup()
    _L0_ffn_in = {k: v for k, v in _L0_ffn_all.items() if k in ('Wg', 'W1', 'b1', 'W2', 'b2')}
    del _L0_ffn_all

    def _L1_attn_setup():
        import jax, jax.numpy as jnp
        import numpy as np
        BATCH, SEQ_L, H, N = (16, 512, 128, 64)
        DT_MIN, DT_MAX = (0.001, 0.1)
        key = jax.random.key(seed)
        ks = jax.random.split(key, 6)
        u = jax.random.normal(ks[0], (BATCH, SEQ_L, H), dtype=jnp.float32)
        Lambda_real = -0.5 * jnp.ones((N,), dtype=jnp.float32)
        Lambda_imag = jnp.pi * jnp.arange(N, dtype=jnp.float32)
        B_real = jax.random.normal(ks[1], (H, N), dtype=jnp.float32) * N ** (-0.5)
        B_imag = jnp.zeros((H, N), dtype=jnp.float32)
        C_real = jax.random.normal(ks[2], (H, N), dtype=jnp.float32) * 0.5
        C_imag = jax.random.normal(ks[3], (H, N), dtype=jnp.float32) * 0.5
        log_dt = jax.random.uniform(ks[4], (H,), dtype=jnp.float32) * (np.float32(np.log(DT_MAX)) - np.float32(np.log(DT_MIN))) + np.float32(np.log(DT_MIN))
        D = jax.random.normal(ks[5], (H,), dtype=jnp.float32) * 0.01
        return {'u': u, 'Lambda_real': Lambda_real, 'Lambda_imag': Lambda_imag, 'B_real': B_real, 'B_imag': B_imag, 'C_real': C_real, 'C_imag': C_imag, 'log_dt': log_dt, 'D': D}
    _L1_attn_all = _L1_attn_setup()
    _L1_attn_in = {k: v for k, v in _L1_attn_all.items() if k in ('Lambda_real', 'Lambda_imag', 'B_real', 'B_imag', 'C_real', 'C_imag', 'log_dt', 'D')}
    del _L1_attn_all

    def _L1_ffn_setup():
        import jax, jax.numpy as jnp
        import numpy as np
        D, E, DR, K, DFF, DSH = (128, 64, 64, 2, 512, 256)
        TEMP = 0.7
        SHARED_SCALE = 0.25
        EPS = 1e-05

        def _ln(x, g, b):
            m = jnp.mean(x, axis=-1, keepdims=True)
            v = jnp.mean(jnp.square(x - m), axis=-1, keepdims=True)
            return (x - m) * jax.lax.rsqrt(v + EPS) * g + b
        key = jax.random.key(seed)
        ks = jax.random.split(key, 16)
        s = 0.02
        return {'x': jax.random.normal(ks[0], (1, 128, D), dtype=jnp.float32), 'ln1_g': jnp.ones((D,), jnp.float32), 'ln1_b': jnp.zeros((D,), jnp.float32), 'Wr': jax.random.normal(ks[1], (D, DR), jnp.float32) * s, 'codebook': jax.random.normal(ks[2], (E, DR), jnp.float32), 'W1': jax.random.normal(ks[3], (E, D, DFF), jnp.float32) * s, 'b1': jnp.zeros((E, DFF), jnp.float32), 'W2': jax.random.normal(ks[4], (E, DFF, D), jnp.float32) * s, 'b2': jnp.zeros((E, D), jnp.float32), 'Ws1': jax.random.normal(ks[5], (D, DSH), jnp.float32) * s, 'bs1': jnp.zeros((DSH,), jnp.float32), 'Ws2': jax.random.normal(ks[6], (DSH, D), jnp.float32) * s, 'bs2': jnp.zeros((D,), jnp.float32), 'ffln_g': jnp.ones((D,), jnp.float32), 'ffln_b': jnp.zeros((D,), jnp.float32), 'Wf1': jax.random.normal(ks[7], (D, DFF), jnp.float32) * s, 'bf1': jnp.zeros((DFF,), jnp.float32), 'Wf2': jax.random.normal(ks[8], (DFF, D), jnp.float32) * s, 'bf2': jnp.zeros((D,), jnp.float32)}
    _L1_ffn_all = _L1_ffn_setup()
    _L1_ffn_in = {k: v for k, v in _L1_ffn_all.items() if k in ('ln1_g', 'ln1_b', 'Wr', 'codebook', 'W1', 'b1', 'W2', 'b2', 'Ws1', 'bs1', 'Ws2', 'bs2', 'ffln_g', 'ffln_b', 'Wf1', 'bf1', 'Wf2', 'bf2')}
    del _L1_ffn_all
    return {'x': x, 'cls_tok': cls_tok, 'L0_tok_W1_w': _L0_tok_in['W1_w'], 'L0_tok_W1_b': _L0_tok_in['W1_b'], 'L0_tok_W1_sw': _L0_tok_in['W1_sw'], 'L0_tok_W1_sb': _L0_tok_in['W1_sb'], 'L0_tok_W2_w': _L0_tok_in['W2_w'], 'L0_tok_W2_b': _L0_tok_in['W2_b'], 'L0_tok_W2_sw': _L0_tok_in['W2_sw'], 'L0_tok_W2_sb': _L0_tok_in['W2_sb'], 'L0_tok_W3_w': _L0_tok_in['W3_w'], 'L0_tok_W3_b': _L0_tok_in['W3_b'], 'L0_tok_eps_in1': _L0_tok_in['eps_in1'], 'L0_tok_eps_out1': _L0_tok_in['eps_out1'], 'L0_tok_eps_in2': _L0_tok_in['eps_in2'], 'L0_tok_eps_out2': _L0_tok_in['eps_out2'], 'L0_attn_W_angle': _L0_attn_in['W_angle'], 'L0_attn_b_angle': _L0_attn_in['b_angle'], 'L0_attn_W_decay': _L0_attn_in['W_decay'], 'L0_attn_b_decay': _L0_attn_in['b_decay'], 'L0_attn_W_input': _L0_attn_in['W_input'], 'L0_attn_b_input': _L0_attn_in['b_input'], 'L0_ffn_Wg': _L0_ffn_in['Wg'], 'L0_ffn_W1': _L0_ffn_in['W1'], 'L0_ffn_b1': _L0_ffn_in['b1'], 'L0_ffn_W2': _L0_ffn_in['W2'], 'L0_ffn_b2': _L0_ffn_in['b2'], 'L1_attn_Lambda_real': _L1_attn_in['Lambda_real'], 'L1_attn_Lambda_imag': _L1_attn_in['Lambda_imag'], 'L1_attn_B_real': _L1_attn_in['B_real'], 'L1_attn_B_imag': _L1_attn_in['B_imag'], 'L1_attn_C_real': _L1_attn_in['C_real'], 'L1_attn_C_imag': _L1_attn_in['C_imag'], 'L1_attn_log_dt': _L1_attn_in['log_dt'], 'L1_attn_D': _L1_attn_in['D'], 'L1_ffn_ln1_g': _L1_ffn_in['ln1_g'], 'L1_ffn_ln1_b': _L1_ffn_in['ln1_b'], 'L1_ffn_Wr': _L1_ffn_in['Wr'], 'L1_ffn_codebook': _L1_ffn_in['codebook'], 'L1_ffn_W1': _L1_ffn_in['W1'], 'L1_ffn_b1': _L1_ffn_in['b1'], 'L1_ffn_W2': _L1_ffn_in['W2'], 'L1_ffn_b2': _L1_ffn_in['b2'], 'L1_ffn_Ws1': _L1_ffn_in['Ws1'], 'L1_ffn_bs1': _L1_ffn_in['bs1'], 'L1_ffn_Ws2': _L1_ffn_in['Ws2'], 'L1_ffn_bs2': _L1_ffn_in['bs2'], 'L1_ffn_ffln_g': _L1_ffn_in['ffln_g'], 'L1_ffn_ffln_b': _L1_ffn_in['ffln_b'], 'L1_ffn_Wf1': _L1_ffn_in['Wf1'], 'L1_ffn_bf1': _L1_ffn_in['bf1'], 'L1_ffn_Wf2': _L1_ffn_in['Wf2'], 'L1_ffn_bf2': _L1_ffn_in['bf2']}

def reference(x, cls_tok, L0_tok_W1_w, L0_tok_W1_b, L0_tok_W1_sw, L0_tok_W1_sb, L0_tok_W2_w, L0_tok_W2_b, L0_tok_W2_sw, L0_tok_W2_sb, L0_tok_W3_w, L0_tok_W3_b, L0_tok_eps_in1, L0_tok_eps_out1, L0_tok_eps_in2, L0_tok_eps_out2, L0_attn_W_angle, L0_attn_b_angle, L0_attn_W_decay, L0_attn_b_decay, L0_attn_W_input, L0_attn_b_input, L0_ffn_Wg, L0_ffn_W1, L0_ffn_b1, L0_ffn_W2, L0_ffn_b2, L1_attn_Lambda_real, L1_attn_Lambda_imag, L1_attn_B_real, L1_attn_B_imag, L1_attn_C_real, L1_attn_C_imag, L1_attn_log_dt, L1_attn_D, L1_ffn_ln1_g, L1_ffn_ln1_b, L1_ffn_Wr, L1_ffn_codebook, L1_ffn_W1, L1_ffn_b1, L1_ffn_W2, L1_ffn_b2, L1_ffn_Ws1, L1_ffn_bs1, L1_ffn_Ws2, L1_ffn_bs2, L1_ffn_ffln_g, L1_ffn_ffln_b, L1_ffn_Wf1, L1_ffn_bf1, L1_ffn_Wf2, L1_ffn_bf2):
    import jax
    import jax.numpy as jnp

    def _L0_tok_ref(inputs, W1_w, W1_b, W1_sw, W1_sb, W2_w, W2_b, W2_sw, W2_sb, W3_w, W3_b, eps_in1, eps_out1, eps_in2, eps_out2):
        import math
        import jax, jax.numpy as jnp
        import numpy as np
        PW = PH = 16
        EMB = 128
        HID = 128
        B, H, W = (64, 128, 128)
        L = H // PW * (W // PH)
        SIGMA_ZERO = 0.1

        def _f_noise(x):
            return jnp.sign(x) * jnp.sqrt(jnp.abs(x))

        def _noisy_linear(x, w, b, sw, sb, eps_in, eps_out):
            ei = _f_noise(eps_in)
            eo = _f_noise(eps_out)
            w_n = w + sw * (eo[:, None] * ei[None, :])
            b_n = b + sb * eo
            return x @ w_n.T + b_n

        def _unfold_patches(x):
            b = x.shape[0]
            p = x.reshape(b, H // PW, PW, W // PH, PH)
            p = p.transpose(0, 1, 3, 2, 4)
            return p.reshape(b, L, PW * PH)

        def _pos_encoding(x):
            pos = jnp.arange(L, dtype=jnp.float32)[:, None]
            div = jnp.exp(jnp.arange(0, EMB, 2, dtype=jnp.float32) * (-math.log(10000.0) / EMB))
            ang = pos * div
            pe = jnp.stack([jnp.sin(ang), jnp.cos(ang)], axis=-1).reshape(L, EMB)
            return x + pe[None, :, :]
        x = _unfold_patches(inputs)
        g = _noisy_linear(x, W1_w, W1_b, W1_sw, W1_sb, eps_in1, eps_out1)
        x_gate = g * jnp.tanh(jax.nn.softplus(g))
        x_inner = _noisy_linear(x, W2_w, W2_b, W2_sw, W2_sb, eps_in2, eps_out2)
        x = x_gate * x_inner
        x = x @ W3_w.T + W3_b
        return _pos_encoding(x)

    def _L0_attn_ref(x_seq, W_angle, b_angle, W_decay, b_decay, W_input, b_input):
        import jax, jax.numpy as jnp
        import numpy as np
        D_MODEL = 128
        N_PAIRS = D_MODEL // 2
        B, T = (8, 1024)

        def _givens_ssm(x_seq, W_angle, b_angle, W_decay, b_decay, W_input, b_input):
            Bb, Tt, D = x_seq.shape
            P = D // 2
            angles = jnp.einsum('btd,dp->btp', x_seq, W_angle) + b_angle
            decays = jax.nn.sigmoid(jnp.einsum('btd,dk->btk', x_seq, W_decay) + b_decay)[..., 0]
            inj = jnp.einsum('btd,de->bte', x_seq, W_input) + b_input
            inj = inj.reshape(Bb, Tt, P, 2)

            def step(h, inp):
                a, d, u = inp
                c, s = (jnp.cos(a), jnp.sin(a))
                he = c * h[..., 0] - s * h[..., 1]
                ho = s * h[..., 0] + c * h[..., 1]
                h_new = d[:, None, None] * jnp.stack([he, ho], axis=-1) + u
                return (h_new, h_new)
            h0 = jnp.zeros((Bb, P, 2), x_seq.dtype)
            xs = (jnp.swapaxes(angles, 0, 1), jnp.swapaxes(decays, 0, 1), jnp.swapaxes(inj, 0, 1))
            _, states = jax.lax.scan(step, h0, xs)
            return jnp.swapaxes(states, 0, 1).reshape(Bb, Tt, D)
        return _givens_ssm(x_seq, W_angle, b_angle, W_decay, b_decay, W_input, b_input)

    def _L0_ffn_ref(x, Wg, W1, b1, W2, b2):
        import jax, jax.numpy as jnp
        import numpy as np
        B, L, H, E, F, C = (8, 2048, 128, 8, 256, 2)
        b, l, h = x.shape
        e = Wg.shape[1]
        k = min(max(int(l * C / e), 1), l)
        S = jax.nn.softmax(x @ Wg, axis=-1)
        St = jnp.swapaxes(S, 1, 2)
        G, I = jax.lax.top_k(St, k)
        ex = jnp.take_along_axis(x[:, None], I[..., None], axis=2)
        hmid = jax.nn.gelu(jnp.einsum('bekh,ehf->bekf', ex, W1) + b1[None, :, None, :], approximate=False)
        out = jnp.einsum('bekf,efh->bekh', hmid, W2) + b2[None, :, None, :]
        vals = G[..., None] * out
        new_x = jnp.zeros_like(x).at[jnp.arange(b)[:, None, None], I].add(vals)
        return new_x

    def _L1_attn_ref(u, Lambda_real, Lambda_imag, B_real, B_imag, C_real, C_imag, log_dt, D):
        import jax, jax.numpy as jnp
        import numpy as np
        BATCH, SEQ_L, H, N = (16, 512, 128, 64)
        DT_MIN, DT_MAX = (0.001, 0.1)
        Lseq = u.shape[1]
        Lam = Lambda_real + 1j * Lambda_imag
        Bc = B_real + 1j * B_imag
        Cc = C_real + 1j * C_imag
        dt = jnp.exp(log_dt)
        dtA = dt[:, None] * Lam[None, :]
        Ab = jnp.exp(dtA)
        Bb = Bc * (Ab - 1.0) / (Lam[None, :] + 1e-08)
        ell = jnp.arange(Lseq, dtype=jnp.float32)
        V = jnp.exp(dtA[:, :, None] * ell[None, None, :])
        K = jnp.einsum('hn,hnl->hl', Cc * Bb, V).real
        x = jnp.swapaxes(u, -1, -2)
        nfft = 2 * Lseq
        Xf = jnp.fft.rfft(x, n=nfft)
        Kf = jnp.fft.rfft(K, n=nfft)
        y = jnp.fft.irfft(Xf * Kf[None], n=nfft)[..., :Lseq]
        y = y + x * D[None, :, None]
        return jnp.swapaxes(y, -1, -2)

    def _L1_ffn_ref(x, ln1_g, ln1_b, Wr, codebook, W1, b1, W2, b2, Ws1, bs1, Ws2, bs2, ffln_g, ffln_b, Wf1, bf1, Wf2, bf2):
        import jax, jax.numpy as jnp
        import numpy as np
        D, E, DR, K, DFF, DSH = (128, 64, 64, 2, 512, 256)
        TEMP = 0.7
        SHARED_SCALE = 0.25
        EPS = 1e-05

        def _ln(x, g, b):
            m = jnp.mean(x, axis=-1, keepdims=True)
            v = jnp.mean(jnp.square(x - m), axis=-1, keepdims=True)
            return (x - m) * jax.lax.rsqrt(v + EPS) * g + b
        B, S, _ = x.shape
        T = B * S
        h = _ln(x, ln1_g, ln1_b).reshape(T, D)
        r = h @ Wr
        logits = r @ codebook.T / TEMP
        probs = jax.nn.softmax(logits, axis=-1)
        vals, idx = jax.lax.top_k(probs, K)
        w = vals / jnp.sum(vals, axis=-1, keepdims=True)
        combine = jnp.zeros((T, E), x.dtype).at[jnp.arange(T)[:, None], idx].set(w)
        eh = jax.nn.silu(jnp.einsum('td,edf->tef', h, W1) + b1)
        eo = jnp.einsum('tef,efd->ted', eh, W2) + b2
        moe = jnp.einsum('te,ted->td', combine, eo)
        shared = (jax.nn.silu(h @ Ws1 + bs1) @ Ws2 + bs2) * SHARED_SCALE
        hmoe = (moe + shared).reshape(B, S, D)
        f = _ln(hmoe, ffln_g, ffln_b)
        f = jax.nn.silu(f @ Wf1 + bf1) @ Wf2 + bf2
        return x + hmoe + f
    h = _L0_tok_ref(x, L0_tok_W1_w, L0_tok_W1_b, L0_tok_W1_sw, L0_tok_W1_sb, L0_tok_W2_w, L0_tok_W2_b, L0_tok_W2_sw, L0_tok_W2_sb, L0_tok_W3_w, L0_tok_W3_b, L0_tok_eps_in1, L0_tok_eps_out1, L0_tok_eps_in2, L0_tok_eps_out2)
    h = jnp.concatenate([jnp.broadcast_to(cls_tok, (h.shape[0], 1, h.shape[2])), h], axis=1)
    h = h + _L0_attn_ref(_layernorm(h, axis=-1), L0_attn_W_angle, L0_attn_b_angle, L0_attn_W_decay, L0_attn_b_decay, L0_attn_W_input, L0_attn_b_input)
    h = h + _L0_ffn_ref(_layernorm(h, axis=-1), L0_ffn_Wg, L0_ffn_W1, L0_ffn_b1, L0_ffn_W2, L0_ffn_b2)
    h = h + _L1_attn_ref(_layernorm(h, axis=-1), L1_attn_Lambda_real, L1_attn_Lambda_imag, L1_attn_B_real, L1_attn_B_imag, L1_attn_C_real, L1_attn_C_imag, L1_attn_log_dt, L1_attn_D)
    h = h + _L1_ffn_ref(_layernorm(h, axis=-1), L1_ffn_ln1_g, L1_ffn_ln1_b, L1_ffn_Wr, L1_ffn_codebook, L1_ffn_W1, L1_ffn_b1, L1_ffn_W2, L1_ffn_b2, L1_ffn_Ws1, L1_ffn_bs1, L1_ffn_Ws2, L1_ffn_bs2, L1_ffn_ffln_g, L1_ffn_ffln_b, L1_ffn_Wf1, L1_ffn_bf1, L1_ffn_Wf2, L1_ffn_bf2)
    return h

_drawn_inputs = setup_inputs


def setup_inputs(seed=0):
    import zlib

    import numpy as np

    out = dict(_drawn_inputs(seed))
    spreads = {'L0_tok_W1_sw': (0.0062500000931322575, 0.6),
     'L0_tok_W1_sb': (0.0062500000931322575, 0.6),
     'L0_tok_W2_sw': (0.0062500000931322575, 0.6),
     'L0_tok_W2_sb': (0.0062500000931322575, 0.6),
     'L0_attn_b_angle': (0.0, 0.1),
     'L0_ffn_b1': (0.0, 0.498),
     'L0_ffn_b2': (0.0, 0.315),
     'L1_attn_Lambda_real': (-0.5, 0.6),
     'L1_attn_B_imag': (0.0, 0.487),
     'L1_ffn_ln1_g': (1.0, 0.6),
     'L1_ffn_ln1_b': (0.0, 0.505),
     'L1_ffn_b1': (0.0, 0.8),
     'L1_ffn_b2': (0.0, 0.299),
     'L1_ffn_bs1': (0.0, 0.8),
     'L1_ffn_bs2': (0.0, 0.8),
     'L1_ffn_ffln_g': (1.0, 0.6),
     'L1_ffn_ffln_b': (0.0, 0.8),
     'L1_ffn_bf1': (0.0, 0.8),
     'L1_ffn_bf2': (0.0, 0.1)}
    factors = {'L0_tok_W1_b': 3.214,
     'L0_tok_W2_b': 2.9,
     'L1_attn_B_real': 2.715,
     'L1_attn_C_real': 2.972,
     'L1_attn_C_imag': 3.334,
     'L1_attn_D': 8.0,
     'L1_ffn_W1': 3.44,
     'L1_ffn_W2': 3.017,
     'L1_ffn_Ws1': 8.0,
     'L1_ffn_Ws2': 8.0,
     'L1_ffn_Wf1': 3.149,
     'L1_ffn_Wf2': 2.752}
    for name, (base, spread) in spreads.items():
        noise = np.random.default_rng([zlib.crc32(name.encode()), seed]).standard_normal(out[name].shape)
        drawn = base * np.exp(spread * noise) if base else spread * noise
        out[name] = jnp.asarray(drawn.astype(out[name].dtype))
    for name, factor in factors.items():
        out[name] = (out[name] * factor).astype(out[name].dtype)
    return out
```

```python
from contextlib import ExitStack
import math

import numpy as np

import concourse.bass as bass
from concourse import mybir

F32 = mybir.dt.float32
BF16 = mybir.dt.bfloat16
I32 = mybir.dt.int32
U32 = mybir.dt.uint32
ALU = mybir.AluOpType
ACT = mybir.ActivationFunctionType
AX = mybir.AxisListType.X

NI, GP, PW, D = 16, 8, 16, 128
L = GP * GP
T = L + 1
N = NI * T
CI = 4
NC = NI // CI
CT = CI * T
E0, K0, F0 = 8, 2 * T // 8, 256
SL = NI * K0
NS = 64
PB, PA = 8, 9
E1, F1, FS = 64, 512, 256
CAP = 128
NBLK = E1 + 2 * N // CAP
U = 3
NCOL = (NBLK // U + 2) * U
BIG = 1.0e6
MAGIC = 12582912.0
TWO_PI = 6.2831850
EPS = 1e-5
NJ = 2 * NI

C_ID, C_CEN, C_ONE, C_PA, C_PB = 0, 128, 256, 384, 512
C_PE = 640
C_TRI = C_PE + L
C_EX = C_TRI + E1
C_IOTA = C_EX + CI * 128
C_K16 = C_IOTA + 128
C_PWR = C_K16 + K0
C_VEC = C_PWR + PA + PB
V_SLOT, V_E, V_EPS, V_HPI, V_SGN, V_T, V_ONE = range(7)
C_ALL = C_VEC + 7


def shape_constants():
    c = np.zeros((128, C_ALL), np.float32)
    eye = np.eye(128, dtype=np.float32)
    c[:, C_ID:C_ID + 128] = eye
    c[:, C_CEN:C_CEN + 128] = eye - 1.0 / D
    c[:, C_ONE:C_ONE + 128] = 1.0 / D
    for p in range(64):
        c[p, C_PA + 2 * p] = 1.0
        c[64 + p, C_PA + 2 * p + 1] = 1.0
        c[64 + p, C_PB + 2 * p] = -1.0
        c[p, C_PB + 2 * p + 1] = 1.0
    pos = np.arange(L, dtype=np.float32)[:, None]
    div = np.exp(np.arange(0, D, 2, dtype=np.float32) * np.float32(-math.log(10000.0) / D)).astype(np.float32)
    ang = pos * div
    c[:, C_PE:C_PE + L] = np.stack([np.sin(ang), np.cos(ang)], axis=-1).reshape(L, D).T
    c[:E1, C_TRI:C_TRI + E1] = np.triu(np.ones((E1, E1), np.float32), 1)
    for r in range(128):
        for b in range(CI):
            if (r // E0) % CI == b:
                c[r, C_EX + b * 128 + (r % E0) * K0:C_EX + b * 128 + (r % E0 + 1) * K0] = 1.0
    c[:, C_IOTA:C_IOTA + 128] = np.arange(128)
    c[:, C_K16:C_K16 + K0] = np.arange(1, K0 + 1)
    c[:, C_PWR:C_PWR + PB] = np.arange(PB)
    c[:, C_PWR + PB:C_PWR + PB + PA] = PB * np.arange(PA)
    c[:, C_VEC + V_SLOT] = np.arange(128) % K0 + 1
    c[:, C_VEC + V_E] = np.arange(128)
    c[:, C_VEC + V_EPS] = EPS
    c[:, C_VEC + V_HPI] = math.pi / 2
    c[:, C_VEC + V_SGN] = np.where(np.arange(128) < 64, 1.0, -1.0)
    c[:, C_VEC + V_T] = np.arange(128)
    c[:, C_VEC + V_ONE] = 1.0
    return c


SEMAPHORES = """
cst_in x_in tokw_in misc_in attw_in ssm_in ffn0_in moe_in moe2_in
feps_f wn wt_ps wt_sb misc_ps misc_sb xr xt_ps xt_sb gi_ps gmn mexp gated tok_ps h0s
xc sqr var sdv xnr pj_ps attw tdec decs frac sc rot out_ps h1s
lg0_ps smx smx_e sms st_ps route0 pt_ps sels xtm_ps xtms gx_ps gxc ga_ps exts px_ps selg
hid_ps gelu y0_ps y0s yt_ps ybs h2_ps h2s xs_ps xss h2t_ps cv_ps h3s
dt_e dtl args fracs trg vv qrec prods kpads kp_out toep_in
st4 sdv4 y4s yn5s x_out h5_ps h5s r_ps rts lg_ps w12a w12e w12 ohss ohs_ps ohts nblks base_ps slts slt_ps
s1_ps s1s cmbs cmb_ps cmb_sb sh_ps b2s tabs_in blk_ps blks tab_ps tabs iots
w_in0 w_in1 w_in2 g_in0 g_in1 g_in2 t_ps t_sb h_ps hps hss y_ps ysbs sc_out0 sc_out1 sc_out2 ix_cp p_rd sp_rd p_io
yl_in0 yl_in1 yl_in2 yl_in3 hms st6 sd6 xfs xf_ps ffs f1_ps fss f2_ps fos fo_ps fins out_in res
a_ch d_ch p_ch
""".split()


def build(nc, a, out):
    xrow_dram = nc.dram_tensor("moe_rows", [N, D], F32, kind="Internal").ap()
    yrow_dram = nc.dram_tensor("moe_out_rows", [2 * N, D], F32, kind="Internal").ap()
    kpad_dram = nc.dram_tensor("ssm_kernel", [128, 2 * T - 1], F32, kind="Internal").ap()

    ctx = ExitStack()
    with ctx:
        def sb(name, shape, dt=F32):
            return ctx.enter_context(nc.sbuf_tensor(name, shape, dt))[:]

        s = {n: ctx.enter_context(nc.semaphore(n)) for n in SEMAPHORES}
        PS = ctx.enter_context(nc.psum_tensor("PS", [128, 8, 512], F32))[:]

        def carve(region, shapes):
            views, at = [], 0
            for shape in shapes:
                n = math.prod(shape)
                v = region[:, at:at + n]
                if len(shape) == 2:
                    v = v.rearrange("p (a b) -> p a b", a=shape[0])
                elif len(shape) == 3:
                    v = v.rearrange("p (a b c) -> p a b c", a=shape[0], b=shape[1])
                views.append(v)
                at += n
            assert at <= region.shape[1], (at, region.shape)
            return views

        R1 = sb("R1", [128, 8448])
        R2 = sb("R2", [128, 12400])
        R3 = sb("R3", [128, 7680])
        R4 = sb("R4", [128, 26 * CT])
        R5 = sb("R5", [128, 4096])
        RF = sb("RF", [128, 6 * N])

        cst = sb("cst", [128, C_ALL])
        ident = cst[:, C_ID:C_ID + 128]
        cen = cst[:, C_CEN:C_CEN + 128]
        onesd = cst[:, C_ONE:C_ONE + 128]
        perm_a = cst[:, C_PA:C_PA + 128]
        perm_b = cst[:, C_PB:C_PB + 128]

        def vec(k, rows=128):
            return cst[0:rows, C_VEC + k:C_VEC + k + 1]

        h0, h1, h2, xn, sq, sd = carve(RF, [[N]] * 6)

        xin, xr, xT, gmin, emis, gate = carve(R2, [[2048], [2048], [2, 1024], [1024], [1024], [1024]])
        feps, fabs, fsgn, wsrc, swsrc, w3, win, b1rows, b2rows, cb = carve(
            R4, [[514], [514], [514], [2, 256], [2, 256], [128], [128], [F0], [D], [64]])
        bcol, sbcol, cols = sb("bcol", [128, 2]), sb("sbcol", [128, 2]), sb("cols", [128, 16])
        wT, w3T = sb("wT", [128, 4, 128]), sb("w3T", [128, 128])
        peb = sb("peb", [128, L])
        B3, CLS, BANG, BDEC, BI, BISW, LDT, DD, G1, B1, GF, BF, BF2, WDEC = range(14)

        def col(k):
            return cols[:, k:k + 1]

        wang = sb("wang", [128, 2, 64])
        wdec = sb("wdec", [128, 128])
        winp, winsw = sb("winp", [128, 2, 64]), sb("winsw", [128, 2, 64])
        mask = sb("mask", [128, CI, T])
        ring4 = carve(R4, [[13, CT], [13, CT]])
        wg = sb("wg", [128, E0])
        w1a, w2a = carve(R5, [[E0, F0], [E0, 2, D]])
        bT = sb("bT", [128, 3, E0])
        xtm, sel, exT, yT, Yb, gxs, selG = carve(
            R2, [[NI, D], [128, K0], [E0, NI, K0], [NI, E0, K0], [NI, D], [NC, CT], [NC, CT]])
        sm = sb("sm", [T, 4, 128])
        smr = sb("smr", [T, 2, NI])
        rt0 = sb("rt0", [128, 6, T])
        top8 = sb("top8", [128, 2, 8])
        lam = sb("lam", [128, 2, NS])
        bc4 = sb("bc4", [128, 4, NS])
        NPW = PB + PA
        pAR, pTI, pE, pS, pC, UU, q64 = carve(R3, [[NPW, NS]] * 5 + [[PA, 2, NS], [14, NS]])
        VV, = carve(R3, [[NPW, 2, NS]])
        prod, = carve(R1, [[T, 2 * NS]])
        kpad = sb("kpad", [128, 2 * T - 1])
        toep, = carve(R1, [[D, T]])
        xs, h2t, h3 = carve(R4[0:T, :], [[NI, D]] * 3)
        y4 = h2t
        lnst = sb("lnst", [T, NI, 6])
        mv = sb("mv", [T, NI, 2])
        lnv = sb("lnv", [T, 8, NI])
        yn5, h5, rT, lg, oh, ohs, ohT, inc, slT = carve(
            R2, [[NI, D], [N], [N], [NI, E1], [2, NI * E1], [NI, E1], [N], [N], [N]])
        base2 = yn5
        wr, cbT = sb("wr", [128, 64]), sb("cbT", [64, 64])
        mx8, ix8 = sb("mx8", [T, NI, 8]), sb("ix8", [T, NI, 8], U32)
        ef = sb("ef", [T, 2, NI])
        wk = sb("wk", [T, 6, NI])
        wts = sb("wts", [T, 2, NI])
        esm = sb("esm", [E1, 8])
        obk = sb("obk", [E1, 2, NCOL])
        b1all, b2all = sb("b1all", [E1, F1]), sb("b2all", [E1, D])
        ws1, ws2, bs1 = sb("ws1", [128, FS]), sb("ws2", [128, 2, D]), sb("bs1", [128, 2])
        bs2 = sb("bs2", [T, D])
        s1, = carve(RF, [[2, N]])
        cmb, cmbT = carve(sq[0:T, :], [[NI, E1]])[0], sd
        sprod, ohAf, ohBf = carve(R1, [[2, NI * E1], [CAP * NJ // 2], [3 * NCOL * NJ // 2]])
        ohA = ohAf.bitcast(BF16).rearrange("p (a j) -> p a j", a=CAP)
        ohB = ohBf.bitcast(BF16).rearrange("p (q i j) -> p q i j", q=3, i=NCOL)
        iotb = R4[0:T, 0:CAP * NJ // 2].bitcast(BF16).rearrange("p (a j) -> p a j", a=CAP)
        slot = sb("slot", [T, 4, NJ])
        slotb = sb("slotb", [T, 2, NJ], BF16)
        cvb = sb("cvb", [T, NJ], BF16)
        tabf, = carve(xn, [[5, NCOL]])
        tabx, taby = sb("tabx", [128, NCOL], U32), sb("taby", [128, NCOL + 1], U32)
        bexp, trips = sb("bexp", [1, NCOL], I32), sb("trips", [1, 1], I32)
        b1blk = sb("b1blk", [128, 4, NCOL])
        w1r, w2r, hs = carve(R3, [[U, F1], [U, 4 * D], [U, 4 * CAP]])
        hpre, xg, xsr, ysb = carve(R5, [[U, 4 * CAP], [U, D], [U, CAP], [U, D]])
        ixg, ixs = sb("ixg", [128, U], U32), sb("ixs", [128, U], U32)
        yl, xf, fs = carve(R2[:, 2048:], [[2, NI * D], [NI, D], [4, N]])
        wf1, wf2 = carve(h2, [[F1], [4, D]])
        bf1 = sb("bf1", [128, 4])
        ff, fo, hm, fin = xn, h0, base2, h3
        s1, = carve(RF, [[2, N]])
        hid, = carve(R2, [[2, 2 * SL]])
        y_dst = yT

        def cs(c):
            return slice(c * CT, (c + 1) * CT)

        def im(b):
            return slice(b * T, (b + 1) * T)

        def tile4(b):
            return slice((b % CI) * T, (b % CI + 1) * T)

        def tok4(b):
            return slice((b % CI) * D, (b % CI + 1) * D)

        def spread(ap, axis, n):
            shape = list(ap.shape)
            return ap.unsqueeze(axis).to_broadcast(shape[:axis] + [n] + shape[axis:])

        LN_XC = [[2, 3, 0, 1], [0, 1, 2, 3], [4, 5, 6, 7]]
        LN_VAR = [[4, 5, 6, 7], [4, 5, 6, 7], [0, 1, 2, 3]]
        PJ = [[2, 3, 4, 5], [0, 1, 6, 7]]
        TD, DEC, AN, TH, RM, FR, AF, SN, CS_, CU, SU, GI, GS = range(13)

        block = ctx.enter_context(nc.Block())

        @block.sync
        def _(sp):
            sp.dma_start(xin, a["x"].rearrange("b o (i r) w -> (b o i) (r w)", i=GP)).then_inc(s["x_in"], 16)
            for k in range(2):
                eps_in = a[f"L0_tok_eps_in{k + 1}"].rearrange("(o n) -> o n", o=1)
                sp.dma_start(feps[:, k * 256:(k + 1) * 256], eps_in.to_broadcast([128, 256])).then_inc(s["tokw_in"], 16)
                for dst, name in ((feps[:, 512 + k:513 + k], "eps_out"), (bcol[:, k:k + 1], "W{}_b"),
                                  (sbcol[:, k:k + 1], "W{}_sb")):
                    name = f"L0_tok_{name.format(k + 1)}" if "{" in name else f"L0_tok_{name}{k + 1}"
                    sp.dma_start(dst, a[name].rearrange("(p o) -> p o", o=1)).then_inc(s["tokw_in"], 16)
                sp.dma_start(wsrc[:, k, :], a[f"L0_tok_W{k + 1}_w"]).then_inc(s["tokw_in"], 16)
                sp.dma_start(swsrc[:, k, :], a[f"L0_tok_W{k + 1}_sw"]).then_inc(s["tokw_in"], 16)
            sp.dma_start(w1a, a["L0_ffn_W1"].rearrange("e h f -> h e f")).then_inc(s["ffn0_in"], 16)
            sp.dma_start(w2a, a["L0_ffn_W2"].rearrange("e (p c) h -> p e c h", c=2)).then_inc(s["ffn0_in"], 16)
            sp.dma_start(wg, a["L0_ffn_Wg"]).then_inc(s["ffn0_in"], 16)
            moe = [(wr, "Wr", None), (b1all, "b1", None), (b2all, "b2", None), (ws1, "Ws1", None),
                   (ws2, "Ws2", "(p c) d -> p c d"), (bs1, "bs1", "(p c) -> p c"),
                   (bf1, "bf1", "(p c) -> p c")]
            for dst, name, how in moe:
                src = a["L1_ffn_" + name]
                if how:
                    src = src.rearrange(how, p=128)
                sp.dma_start(dst, src).then_inc(s["moe_in"], 16)
            sp.dma_start(bs2, a["L1_ffn_bs2"].rearrange("(o n) -> o n", o=1).to_broadcast([T, D])).then_inc(s["moe_in"], 16)
            for k, name in ((G1, "ln1_g"), (B1, "ln1_b"), (GF, "ffln_g"), (BF, "ffln_b"), (BF2, "bf2")):
                sp.dma_start(col(k), a["L1_ffn_" + name].rearrange("(p o) -> p o", o=1)).then_inc(s["moe_in"], 16)
            sp.wait_ge(s["kpads"], 1)
            sp.dma_start(kpad_dram, kpad[:, :]).then_inc(s["kp_out"], 16)
            sp.wait_ge(s["kp_out"], 16)
            skewed = bass.AP(kpad_dram.tensor, 0, [[1, T], [2 * T - 1, D], [1, T]])
            sp.dma_start(toep[0:T], skewed).then_inc(s["toep_in"], 16)
            sp.wait_ge(s["yn5s"], 1)
            sp.dma_start(xrow_dram.rearrange("(b t) d -> t b d", b=NI), yn5[0:T]).then_inc(s["x_out"], 16)
            sp.wait_ge(s["cmbs"], 1)
            sp.dma_start(wf1, a["L1_ffn_Wf1"]).then_inc(s["moe2_in"], 16)
            sp.dma_start(wf2, a["L1_ffn_Wf2"].rearrange("(p c) d -> p c d", p=128)).then_inc(s["moe2_in"], 16)

            sp.wait_ge(s["blks"], 2)
            n_trips = sp.value_load(trips[0:1, 0:1], min_val=1, max_val=NCOL // U - 1)

            def load_block(j, at):
                e = sp.value_load(bexp[0:1, at], min_val=0, max_val=E1 - 1)
                sp.dma_start(w1r[:, j, :], a["L1_ffn_W1"][bass.ds(e, 1)].rearrange("o h f -> (o h) f"))\
                    .then_inc(s[f"w_in{j}"], 16)
                sp.dma_start(w2r[:, j, :], a["L1_ffn_W2"][bass.ds(e, 1)].rearrange("o (p c) d -> (o p) (c d)", p=128))\
                    .then_inc(s[f"w_in{j}"], 16)

            sp.wait_ge(s["p_io"], 1)
            for j in range(U):
                if j == U - 1:
                    sp.wait_ge(s["y_ps"], 1)
                load_block(j, slice(j, j + 1))
            with sp.Fori(1, n_trips) as it:
                for j in range(U):
                    sp.wait_ge(s["y_ps"], it * U + (j - 1))
                    sp.sem_inc(s["sp_rd"], 1)
                    load_block(j, bass.ds(it * U + j, 1))
            for j in range(U):
                sp.wait_ge(s[f"sc_out{j}"], n_trips * 16 + (16 if j == U - 1 else 0))
                sp.sem_inc(s["sp_rd"], 1)
            for c in range(NC):
                src = yrow_dram.rearrange("(k b t) d -> t k b d", k=2, b=NI)[:, :, c * CI:(c + 1) * CI]
                dst = yl[0:T].rearrange("p k (b d) -> p k b d", b=NI)[:, :, c * CI:(c + 1) * CI]
                for k in range(2):
                    sp.dma_start(dst[:, k], src[:, k]).then_inc(s[f"yl_in{c}"], 16)
            for c in range(NC):
                sp.wait_ge(s["fins"], c + 1)
                sp.dma_start(out.rearrange("b t d -> t b d")[:, c * CI:(c + 1) * CI],
                             fin[:, c * CI:(c + 1) * CI]).then_inc(s["out_in"], 16)
            sp.wait_ge(s["out_in"], 16 * NC)

        @block.tensor
        def _(pe):
            mm, tr = nc.tensor.matmul, nc.tensor.transpose
            pe.wait_ge(s["cst_in"], 16)
            pe.wait_ge(s["wn"], 1)
            for k in range(2):
                for h in range(2):
                    q = 2 * k + h
                    last = tr(PS[:, 6, q * 128:(q + 1) * 128], wsrc[:, k, h * 128:(h + 1) * 128], ident)
            last.then_inc(s["wt_ps"], 1)
            pe.wait_ge(s["misc_in"], 16 * 6)
            tr(PS[:, 7, 0:128], w3, ident)
            for c in range(2):
                tr(PS[:, 7, 128 + E0 * c:128 + E0 * (c + 1)], b1rows[0:E0, c:F0:2], ident[0:E0, 0:E0])
            tr(PS[:, 7, 144:144 + E0], b2rows[0:E0, :], ident[0:E0, 0:E0])
            tr(PS[0:64, 7, 160:224], cb[0:64, :], ident[0:64, 0:64]).then_inc(s["misc_ps"], 1)
            pe.wait_ge(s["xr"], 2)
            for h in range(2):
                for j in range(GP):
                    last = tr(PS[:, 2 * h + j // 4, (j % 4) * 128:(j % 4 + 1) * 128],
                              xr[:, j * 256 + h * 128:j * 256 + (h + 1) * 128], ident)
                    if j % 4 == 3:
                        last.then_inc(s["xt_ps"], 1)
            pe.wait_ge(s["wt_sb"], 1)
            pe.wait_ge(s["misc_sb"], 1)
            pe.wait_ge(s["xt_sb"], 4)
            for n in range(2):
                for k in range(2):
                    for h in range(2):
                        last = mm(PS[:, 4 + 2 * n + k, :], wT[:, 2 * k + h, :], xT[:, h, n * 512:(n + 1) * 512],
                                  start=h == 0, stop=h == 1)
                last.then_inc(s["gi_ps"], 1)
            for n in range(2):
                pe.wait_ge(s["gated"], n + 1)
                mm(PS[:, n, :], w3T[:, :], gate[:, n * 512:(n + 1) * 512], start=True, stop=True).then_inc(s["tok_ps"], 1)

            def centre(k, c, src):
                mm(PS[:, LN_XC[k][c], 0:CT], cen, src[:, cs(c)], start=True, stop=True).then_inc(s["xc"], 1)

            def variance(k, c):
                pe.wait_ge(s["sqr"], 4 * k + c + 1)
                mm(PS[:, LN_VAR[k][c], 0:CT], onesd, sq[:, cs(c)], start=True, stop=True).then_inc(s["var"], 1)

            for c in range(NC):
                pe.wait_ge(s["h0s"], 1 + c // 2)
                centre(0, c, h0)
                if c:
                    variance(0, c - 1)
            variance(0, NC - 1)

            def project(c):
                bk = PJ[c % 2]
                pe.wait_ge(s["xnr"], 2 if c == 0 else 4)
                if c >= 2:
                    pe.wait_ge(s["h1s"], c - 1)
                x = xn[:, cs(c)]
                mm(PS[:, bk[0], 0:CT], wang[:, :, :].rearrange("p a b -> p (a b)"), x, start=True, stop=True)
                mm(PS[:, bk[1], 0:CT], wdec[:, :], x, start=True, stop=True)
                mm(PS[:, bk[2], 0:CT], winp[:, :, :].rearrange("p a b -> p (a b)"), x, start=True, stop=True)
                mm(PS[:, bk[3], 0:CT], winsw[:, :, :].rearrange("p a b -> p (a b)"), x, start=True, stop=True)\
                    .then_inc(s["pj_ps"], 1)

            def rotate_back(c):
                r = ring4[c % 2]
                pe.wait_ge(s["rot"], c + 1)
                bank = PS[:, PJ[c % 2][0], 0:CT]
                mm(bank, ident, h0[:, cs(c)], start=True, stop=False)
                mm(bank, perm_a, r[:, RM], start=False, stop=False)
                mm(bank, perm_b, r[:, AN], start=False, stop=True).then_inc(s["out_ps"], 1)

            pe.wait_ge(s["attw"], 1)
            pe.wait_ge(s["attw_in"], 16 * 11)
            project(0)
            project(1)
            rotate_back(0)
            project(2)
            rotate_back(1)
            project(3)
            rotate_back(2)
            rotate_back(3)

            pe.wait_ge(s["h1s"], 4)
            for c in range(NC):
                centre(1, c, h1)
                if c:
                    variance(1, c - 1)
            variance(1, NC - 1)

            pe.wait_ge(s["ffn0_in"], 48)
            pe.wait_ge(s["xnr"], 8)
            for b in range(NI):
                last = mm(PS[0:T, 4, b * E0:(b + 1) * E0], xn[:, im(b)], wg[:, :], start=True, stop=True)
            last.then_inc(s["lg0_ps"], 1)
            for b in range(NI):
                last = tr(PS[0:T, b // CI, tok4(b)], xn[:, im(b)], ident)
                if b % CI == CI - 1:
                    last.then_inc(s["xtm_ps"], 1)
            pe.wait_ge(s["sms"], 1)
            tr(PS[:, 5, 0:T], sm[:, 2, :], ident[0:T, 0:T]).then_inc(s["st_ps"], 1)
            pe.wait_ge(s["route0"], 1)
            pe.wait_ge(s["xtms"], 4)
            tr(PS[0:T, 0, 0:128], rt0[:, 5, :], ident).then_inc(s["pt_ps"], 1)
            for b in range(NI):
                g = b // CI
                last = mm(PS[:, 4 + g, tile4(b)],
                          cst[32 * g:32 * g + 32, C_EX + (b % CI) * 128:C_EX + (b % CI + 1) * 128],
                          rt0[32 * g:32 * g + 32, 1, :], start=True, stop=True)
                if b % CI == CI - 1:
                    last.then_inc(s["gx_ps"], 1)
            pe.wait_ge(s["sels"], 1)
            for b in range(NI):
                last = mm(PS[:, b // CI, tok4(b)], xtm[0:T, b, :],
                          sel[0:T, b * E0:(b + 1) * E0, :].rearrange("p e k -> p (e k)"), start=True, stop=True)
                if b % CI == CI - 1:
                    last.then_inc(s["ga_ps"], 1)
            for b in range(NI):
                g = b // CI
                if b % CI == 0:
                    pe.wait_ge(s["gxc"], g + 1)
                last = mm(PS[:, 4 + g, tile4(b)],
                          cst[32 * g:32 * g + 32, C_EX + (b % CI) * 128:C_EX + (b % CI + 1) * 128],
                          rt0[32 * g:32 * g + 32, 5, :], start=True, stop=True)
                if b % CI == CI - 1:
                    last.then_inc(s["px_ps"], 1)

            def hidden0(e):
                if e == 0:
                    pe.wait_ge(s["exts"], 4)
                if e >= 2:
                    pe.wait_ge(s["gelu"], e - 1)
                for c in range(2):
                    last = mm(PS[:, e % 2, c * SL:(c + 1) * SL], w1a[:, e, c:F0:2],
                              exT[:, e].rearrange("p b k -> p (b k)"), start=True, stop=True)
                last.then_inc(s["hid_ps"], 1)

            hidden0(0)
            for e in range(E0):
                if e + 1 < E0:
                    hidden0(e + 1)
                pe.wait_ge(s["gelu"], e + 1)
                if e >= 2:
                    pe.wait_ge(s["y0s"], e - 1)
                for c in range(2):
                    last = mm(PS[:, 2 + e % 2, 0:SL], w2a[:, e, c, :], hid[:, e % 2, c * SL:(c + 1) * SL],
                              start=c == 0, stop=c == 1)
                last.then_inc(s["y0_ps"], 1)
            pe.wait_ge(s["selg"], 4)
            pe.wait_ge(s["y0s"], 8)
            for b in range(NI):
                last = tr(PS[:, 4 + b // CI, tok4(b)], yT[:, b].rearrange("p e k -> p (e k)"), ident)
                if b % CI == CI - 1:
                    last.then_inc(s["yt_ps"], 1)
            pe.wait_ge(s["ybs"], 4)
            for g in range(NC):
                mm(PS[:, g, 0:CT], ident, h1[:, cs(g)], start=True, stop=False, skip_group_check=True)
                for b in range(g * CI, g * CI + CI):
                    last = mm(PS[:, g, tile4(b)], Yb[:, b, :], selG[:, g, tile4(b)], start=False,
                              stop=b % CI == CI - 1, skip_group_check=True)
                last.then_inc(s["h2_ps"], 1)

            for c in range(NC):
                pe.wait_ge(s["h2s"], c + 1)
                centre(2, c, h2)
                if c:
                    variance(2, c - 1)
            variance(2, NC - 1)
            pe.wait_ge(s["xnr"], 12)
            for b in range(NI):
                last = tr(PS[0:T, b // CI, tok4(b)], xn[:, im(b)], ident)
                if b % CI == CI - 1:
                    last.then_inc(s["xs_ps"], 1)
            for b in range(NI):
                last = tr(PS[0:T, 4 + b // CI, tok4(b)], h2[:, im(b)], ident)
                if b % CI == CI - 1:
                    last.then_inc(s["h2t_ps"], 1)
            pe.wait_ge(s["xss"], 4)
            pe.wait_ge(s["toep_in"], 16)
            for h in range(D):
                last = mm(PS[0:T, h // 32, (h % 32) * NI:(h % 32 + 1) * NI], toep[0:T, h, :], xs[:, :, h],
                          start=True, stop=True)
                if h % 32 == 31:
                    last.then_inc(s["cv_ps"], 1)

            pe.wait_ge(s["yn5s"], 1)
            pe.wait_ge(s["moe_in"], 16 * 13)
            for b in range(NI):
                last = tr(PS[:, 4 + b // CI, tile4(b)], yn5[0:T, b, :], ident[0:T, 0:T])
                if b % CI == CI - 1:
                    last.then_inc(s["h5_ps"], 1)
            for c in range(NC):
                pe.wait_ge(s["h5s"], c + 1)
                mm(PS[0:64, c, 0:CT], wr[:, :], h5[:, cs(c)], start=True, stop=True).then_inc(s["r_ps"], 1)
            pe.wait_ge(s["rts"], 4)
            for b in range(NI):
                last = mm(PS[0:T, 4 + b // 8, (b % 8) * E1:(b % 8 + 1) * E1], rT[0:64, im(b)], cbT[:, :],
                          start=True, stop=True)
                if b % 8 == 7:
                    last.then_inc(s["lg_ps"], 1)
            for k in range(2 * NC):
                if k >= 2:
                    pe.wait_ge(s["s1s"], k - 1)
                mm(PS[:, 6 + k % 2, 0:CT], ws1[:, k % 2:FS:2], h5[:, cs(k // 2)], start=True, stop=True)\
                    .then_inc(s["s1_ps"], 1)
            pe.wait_ge(s["ohss"], 1)
            for b in range(NI):
                last = tr(PS[0:E1, b // CI, tile4(b)], ohs[0:T, b, :], ident[0:T, 0:T])
                if b % CI == CI - 1:
                    last.then_inc(s["ohs_ps"], 1)
            pe.wait_ge(s["s1s"], 8)
            pe.wait_ge(s["nblks"], 1)
            mm(PS[0:E1, 6, 0:1], cst[0:E1, C_TRI:C_TRI + E1], esm[:, 1:2], start=True, stop=True)
            mm(PS[0:1, 6, 8:9], esm[:, 1:2], vec(V_ONE, E1), start=True, stop=True).then_inc(s["base_ps"], 1)
            pe.wait_ge(s["slts"], 1)
            for b in range(NI):
                last = tr(PS[0:T, 4 + b // 8, (b % 8) * E1:(b % 8 + 1) * E1], slT[0:E1, im(b)], ident[0:E1, 0:E1])
            last.then_inc(s["slt_ps"], 1)
            mm(PS[0:1, 6, 16:16 + NCOL], vec(V_E, E1), obk[:, 1, :], start=True, stop=True)
            for c in range(4):
                last = mm(PS[:, 7, c * NCOL:(c + 1) * NCOL], b1all[:, c:F1:4], obk[:, 1, :], start=True, stop=True)
            last.then_inc(s["blk_ps"], 1)
            pe.wait_ge(s["cmbs"], 1)
            pe.wait_ge(s["ohts"], 4)
            for b in range(NI):
                last = tr(PS[0:E1, b // CI, tile4(b)], cmb[:, b, :], ident[0:T, 0:T])
                if b % CI == CI - 1:
                    last.then_inc(s["cmb_ps"], 1)
            pe.wait_ge(s["tabs_in"], 1)
            for j in range(NJ):
                last = mm(PS[:, 5, 0:3 * NCOL], ohA[0:T, :, j], ohB[0:T, :, :, j].rearrange("p q i -> p (q i)"),
                          start=j == 0, stop=j == NJ - 1)
            last.then_inc(s["tab_ps"], 1)
            pe.wait_ge(s["cmb_sb"], 4)
            for b in range(NI):
                bank = PS[0:T, b // CI, tok4(b)]
                for c in range(2):
                    mm(bank, s1[:, c, im(b)], ws2[:, c, :], start=c == 0, stop=False)
                last = mm(bank, cmbT[0:E1, im(b)], b2all[:, :], start=False, stop=True)
                if b % CI == CI - 1:
                    last.then_inc(s["sh_ps"], 1)

            def turn(j):
                tr(PS[:, 3 + j, 0:CAP], xg[:, j, :], ident).then_inc(s["t_ps"], 1)

            def second(j):
                for c in range(4):
                    last = mm(PS[:, 3 + j, 128:256], hs[:, j, c * CAP:(c + 1) * CAP], w2r[:, j, c * D:(c + 1) * D],
                              start=c == 0, stop=c == 3)
                last.then_inc(s["y_ps"], 1)

            pe.wait_ge(s["b2s"], 4)
            pe.wait_ge(s["tabs"], 1)
            pe.wait_ge(s["p_io"], 1)
            pe.wait_ge(s["blks"], 2)
            pe_trips = pe.value_load(trips[0:1, 0:1], min_val=1, max_val=NCOL // U - 1)
            pe.wait_ge(s["g_in0"], 16)
            turn(0)

            def pe_body(it, first):
                for j in range(U):
                    nxt, prev = (j + 1) % U, (j - 1) % U
                    pe.wait_ge(s[f"g_in{nxt}"], it * 16 + (16 if j < U - 1 else 32))
                    if not (first and j == 0):
                        pe.wait_ge(s["ysbs"], it * U + j)
                    turn(nxt)
                    pe.wait_ge(s[f"w_in{j}"], it * 32 + 32)
                    pe.wait_ge(s["t_sb"], it * U + (j + 1))
                    for c in range(4):
                        last = mm(PS[:, j, c * CAP:(c + 1) * CAP], w1r[:, j, c:F1:4], xsr[:, j, :], start=True, stop=True)
                    last.then_inc(s["h_ps"], 1)
                    pe.wait_ge(s["hss"], it * U + (j + U))
                    second(prev)

            pe_body(0, True)
            with pe.Fori(1, pe_trips) as it:
                pe_body(it, False)
            pe.wait_ge(s["hss"], pe_trips * U + U)
            second(U - 1)

            pe.wait_ge(s["moe2_in"], 32)
            for c in range(NC):
                pe.wait_ge(s["xfs"], c + 1)
                if c == 0:
                    pe.wait_ge(s["ysbs"], pe_trips * U + 1)
                for b in range(c * CI, c * CI + CI):
                    last = tr(PS[:, c, tile4(b)], xf[0:T, b, :], ident[0:T, 0:T])
                last.then_inc(s["xf_ps"], 1)
            for c in range(NC):
                pe.wait_ge(s["ffs"], c + 1)
                for f in range(4):
                    if c:
                        pe.wait_ge(s["fss"], 4 * (c - 1) + f + 1)
                    mm(PS[:, 4 + f, 0:CT], wf1[:, f:F1:4], ff[:, cs(c)], start=True, stop=True).then_inc(s["f1_ps"], 1)
                for f in range(4):
                    pe.wait_ge(s["fss"], 4 * c + f + 1)
                    last = mm(PS[:, c, 0:CT], wf2[:, f, :], fs[:, f, cs(c)], start=f == 0, stop=f == 3)
                last.then_inc(s["f2_ps"], 1)
                pe.wait_ge(s["fos"], c + 1)
                for b in range(c * CI, c * CI + CI):
                    last = tr(PS[0:T, c, tok4(b)], fo[:, im(b)], ident)
                last.then_inc(s["fo_ps"], 1)

        @block.scalar
        def _(act):
            act.dma_start(cst[:, :], a["constants"]).then_inc(s["cst_in"], 16)
            act.dma_start(w3, a["L0_tok_W3_w"]).then_inc(s["misc_in"], 16)
            act.dma_start(col(B3), a["L0_tok_W3_b"].rearrange("(p o) -> p o", o=1)).then_inc(s["misc_in"], 16)
            act.dma_start(col(CLS), a["cls_tok"].rearrange("o q d -> d (o q)")).then_inc(s["misc_in"], 16)
            act.dma_start(b1rows[0:E0, :], a["L0_ffn_b1"]).then_inc(s["misc_in"], 16)
            act.dma_start(b2rows[0:E0, :], a["L0_ffn_b2"]).then_inc(s["misc_in"], 16)
            act.dma_start(cb[0:64, :], a["L1_ffn_codebook"]).then_inc(s["misc_in"], 16)
            act.dma_start(lam[:, 0, :], a["L1_attn_Lambda_real"].rearrange("(o n) -> o n", o=1).to_broadcast([128, NS])).then_inc(s["ssm_in"], 16)
            act.dma_start(lam[:, 1, :], a["L1_attn_Lambda_imag"].rearrange("(o n) -> o n", o=1).to_broadcast([128, NS])).then_inc(s["ssm_in"], 16)
            act.dma_start(col(LDT), a["L1_attn_log_dt"].rearrange("(p o) -> p o", o=1)).then_inc(s["ssm_in"], 16)
            for k, name in enumerate(("B_real", "B_imag", "C_real", "C_imag")):
                act.dma_start(bc4[:, k, :], a["L1_attn_" + name]).then_inc(s["ssm_in"], 16)
            act.dma_start(col(DD), a["L1_attn_D"].rearrange("(p o) -> p o", o=1)).then_inc(s["ssm_in"], 16)
            for k in range(2):
                act.dma_start(wang[:, k, :], a["L0_attn_W_angle"]).then_inc(s["attw_in"], 16)
                act.dma_start(col(BANG)[64 * k:64 * k + 64], a["L0_attn_b_angle"].rearrange("(p o) -> p o", o=1))\
                    .then_inc(s["attw_in"], 16)
            act.dma_start(col(WDEC), a["L0_attn_W_decay"]).then_inc(s["attw_in"], 16)
            act.dma_start(col(BDEC), a["L0_attn_b_decay"].rearrange("(p o) -> p o", o=1).to_broadcast([128, 1])).then_inc(s["attw_in"], 16)
            act.dma_start(win, a["L0_attn_W_input"]).then_inc(s["attw_in"], 16)
            pairs = a["L0_attn_b_input"].rearrange("(p two) -> p two", two=2)
            with nc.allow_non_contiguous_dma(reason="a bias of 128 values, split into pairs"):
                for dst, lo in ((BI, 0), (BISW, 1)):
                    for k in range(2):
                        act.dma_start(col(dst)[64 * k:64 * k + 64], pairs[:, (lo + k) % 2:(lo + k) % 2 + 1])\
                            .then_inc(s["attw_in"], 16)

            n_link = [0]

            def link(ins):
                n_link[0] += 1
                ins.then_inc(s["a_ch"], 1)
                act.wait_ge(s["a_ch"], n_link[0])

            act.wait_ge(s["tokw_in"], 16 * 12)
            link(nc.scalar.activation(fabs, feps, ACT.Abs))
            nc.scalar.activation(fabs, fabs, ACT.Sqrt)
            nc.scalar.activation(fsgn, feps, ACT.Sign).then_inc(s["feps_f"], 1)
            act.wait_ge(s["x_in"], 16)
            nc.scalar.activation(xr.rearrange("p (j r c) -> p j r c", j=GP, r=PW)[:, 4:8],
                                 xin.rearrange("p (r j c) -> p j r c", j=GP, r=PW)[:, 4:8], ACT.Copy).then_inc(s["xr"], 1)
            act.wait_ge(s["ssm_in"], 16 * 8)
            link(nc.scalar.activation(col(LDT), col(LDT), ACT.Exp))
            nc.scalar.activation(col(LDT), col(LDT), ACT.Copy).then_inc(s["dt_e"], 1)

            def turned(k):
                return (xT[:, k // 2, :].rearrange("p (q j) -> p j q", j=GP)[:, 4 * (k % 2):4 * (k % 2) + 4],
                        PS[:, k, :].rearrange("p (j q) -> p j q", j=4))

            for k in (0, 2):
                act.wait_ge(s["xt_ps"], k + 1)
                dst, src = turned(k)
                nc.scalar.activation(dst, src, ACT.Copy).then_inc(s["xt_sb"], 1)
            for n in range(2):
                act.wait_ge(s["gmn"], n + 1)
                nc.scalar.activation(emis[:, n * 512:(n + 1) * 512], gmin[:, n * 512:(n + 1) * 512], ACT.Exp)\
                    .then_inc(s["mexp"], 1)
            act.wait_ge(s["args"], 2)
            nc.scalar.activation(pE, pAR, ACT.Exp).then_inc(s["trg"], 1)

            def squares(k, c):
                act.wait_ge(s["xc"], 4 * k + c + 1)
                if k:
                    act.wait_ge(s["var"], 4 * k)
                nc.scalar.activation(sq[:, cs(c)], PS[:, LN_XC[k][c], 0:CT], ACT.Square).then_inc(s["sqr"], 1)

            def deviation(k, c):
                act.wait_ge(s["var"], 4 * k + c + 1)
                if k:
                    act.wait_ge(s["xnr"], 4 * k)
                nc.scalar.activation(sd[:, cs(c)], PS[:, LN_VAR[k][c], 0:CT], ACT.Sqrt, bias=vec(V_EPS)).then_inc(s["sdv"], 1)

            for c in range(NC):
                squares(0, c)
                if c:
                    deviation(0, c - 1)
            deviation(0, NC - 1)

            act.wait_ge(s["fracs"], 1)
            link(nc.scalar.activation(pC, pTI, ACT.Abs))
            nc.scalar.activation(pS, pTI, ACT.Sin, scale=TWO_PI).then_inc(s["trg"], 1)
            nc.scalar.activation(pC, pC, ACT.Sin, scale=-TWO_PI, bias=vec(V_HPI)).then_inc(s["trg"], 1)

            def decay(c):
                act.wait_ge(s["pj_ps"], c + 1)
                if c >= 2:
                    act.wait_ge(s["decs"], c - 1)
                nc.scalar.activation(ring4[c % 2][:, TD], PS[:, PJ[c % 2][1], 0:CT], ACT.Tanh, scale=0.5,
                                     bias=col(BDEC)).then_inc(s["tdec"], 1)

            def sincos(c):
                r = ring4[c % 2]
                act.wait_ge(s["frac"], c + 1)
                link(nc.scalar.activation(r[:, AF], r[:, FR], ACT.Abs))
                nc.scalar.activation(r[:, SN], r[:, FR], ACT.Sin, scale=TWO_PI)
                nc.scalar.activation(r[:, CS_], r[:, AF], ACT.Sin, scale=-TWO_PI, bias=vec(V_HPI)).then_inc(s["sc"], 1)

            def residual1(c):
                act.wait_ge(s["out_ps"], c + 1)
                nc.scalar.activation(h1[:, cs(c)], PS[:, PJ[c % 2][0], 0:CT], ACT.Copy).then_inc(s["h1s"], 1)

            act.wait_ge(s["attw"], 1)
            for c in range(NC):
                decay(c)
                sincos(c)
                if c:
                    residual1(c - 1)
            residual1(NC - 1)

            for c in range(NC):
                squares(1, c)
                if c:
                    deviation(1, c - 1)
            deviation(1, NC - 1)

            act.wait_ge(s["smx"], 1)
            nc.scalar.activation(sm[:, 1, :], sm[:, 0, :], ACT.Exp).then_inc(s["smx_e"], 1)
            for g in range(NC):
                act.wait_ge(s["xtm_ps"], g + 1)
                nc.scalar.activation(xtm[0:T, CI * g:CI * g + CI, :],
                                     PS[0:T, g, :].rearrange("p (b d) -> p b d", b=CI), ACT.Copy).then_inc(s["xtms"], 1)
            for g in range(NC):
                act.wait_ge(s["gx_ps"], g + 1)
                nc.scalar.activation(gxs[:, g, :], PS[:, 4 + g, 0:CT], ACT.Copy).then_inc(s["gxc"], 1)
            for g in range(NC):
                act.wait_ge(s["ga_ps"], g + 1)
                nc.scalar.activation(exT[:, :, CI * g:CI * g + CI, :].rearrange("p e b k -> p b e k"),
                                     PS[:, g, :].rearrange("p (b e k) -> p b e k", b=CI, e=E0), ACT.Copy)\
                    .then_inc(s["exts"], 1)
            for e in range(E0):
                act.wait_ge(s["hid_ps"], e + 1)
                if e >= 2:
                    act.wait_ge(s["y0_ps"], e - 1)
                for c in range(2):
                    last = nc.scalar.activation(hid[:, e % 2, c * SL:(c + 1) * SL], PS[:, e % 2, c * SL:(c + 1) * SL],
                                                ACT.Gelu, bias=bT[:, c, e:e + 1])
                last.then_inc(s["gelu"], 1)
            for g in (0, 2):
                act.wait_ge(s["yt_ps"], g + 1)
                nc.scalar.activation(Yb[:, CI * g:CI * g + CI, :], PS[:, 4 + g, :].rearrange("p (b d) -> p b d", b=CI),
                                     ACT.Copy).then_inc(s["ybs"], 1)
            for g in range(NC):
                act.wait_ge(s["h2_ps"], g + 1)
                nc.scalar.activation(h2[:, cs(g)], PS[:, g, 0:CT], ACT.Copy).then_inc(s["h2s"], 1)
                squares(2, g)
                if g:
                    deviation(2, g - 1)
            deviation(2, NC - 1)
            for g in range(NC):
                act.wait_ge(s["xs_ps"], g + 1)
                nc.scalar.activation(xs[:, CI * g:CI * g + CI, :], PS[0:T, g, :].rearrange("p (b d) -> p b d", b=CI),
                                     ACT.Copy).then_inc(s["xss"], 1)
            act.wait_ge(s["st4"], 1)
            nc.scalar.activation(lnv[:, 1, :], mv[:, :, 1], ACT.Sqrt, bias=vec(V_EPS, T)).then_inc(s["sdv4"], 1)
            act.wait_ge(s["st4"], 2)
            nc.scalar.activation(lnv[:, 4, :], lnv[:, 3, :], ACT.Sqrt, bias=vec(V_EPS, T)).then_inc(s["sdv4"], 1)
            for c in range(NC):
                act.wait_ge(s["r_ps"], c + 1)
                nc.scalar.activation(rT[0:64, cs(c)], PS[0:64, c, 0:CT], ACT.Copy).then_inc(s["rts"], 1)
            act.wait_ge(s["h1s"], 4)
            for k in range(2 * NC):
                act.wait_ge(s["s1_ps"], k + 1)
                nc.scalar.activation(s1[:, k % 2, cs(k // 2)], PS[:, 6 + k % 2, 0:CT], ACT.Silu,
                                     bias=bs1[:, k % 2:k % 2 + 1]).then_inc(s["s1s"], 1)
            act.wait_ge(s["w12a"], 1)
            nc.scalar.activation(wk[:, 1, :], wk[:, 0, :], ACT.Tanh, scale=0.5 / 0.7).then_inc(s["w12e"], 1)
            for g in range(NC):
                act.wait_ge(s["ohs_ps"], g + 1)
                nc.scalar.activation(ohT[0:E1, cs(g)], PS[0:E1, g, 0:CT], ACT.Copy).then_inc(s["ohts"], 1)
            act.wait_ge(s["blk_ps"], 1)
            nc.scalar.activation(b1blk[:, :, :].rearrange("p c i -> p (c i)"), PS[:, 7, 0:4 * NCOL], ACT.Copy)
            nc.scalar.activation(bexp[:, :], PS[0:1, 6, 16:16 + NCOL], ACT.Copy).then_inc(s["blks"], 1)
            for g in range(NC):
                act.wait_ge(s["cmb_ps"], g + 1)
                nc.scalar.activation(cmbT[0:E1, cs(g)], PS[0:E1, g, 0:CT], ACT.Copy).then_inc(s["cmb_sb"], 1)

            act.wait_ge(s["blks"], 2)
            act_trips = act.value_load(trips[0:1, 0:1], min_val=1, max_val=NCOL // U - 1)
            act.wait_ge(s["p_io"], 1)

            def leave(j, seen):
                act.wait_ge(s["y_ps"], seen)
                nc.scalar.activation(ysb[:, j, :], PS[:, 3 + j, 128:256], ACT.Copy).then_inc(s["ysbs"], 1)

            def act_body(it, first):
                for j in range(U):
                    act.wait_ge(s["hps"], it * U + (j + 1))
                    nc.scalar.activation(hs[:, j, :], hpre[:, j, :], ACT.Silu).then_inc(s["hss"], 1)
                    if not first:
                        act.wait_ge(s[f"sc_out{(j - 1) % U}"], it * 16)
                    leave((j - 1) % U, it * U + (j + 1))

            act_body(0, True)
            with act.Fori(1, act_trips) as it:
                act_body(it, False)
            act.wait_ge(s[f"sc_out{U - 1}"], act_trips * 16)
            leave(U - 1, act_trips * U + 1)

            for c in range(NC):
                act.wait_ge(s["st6"], c + 1)
                nc.scalar.activation(lnv[:, 1, CI * c:CI * c + CI], mv[:, CI * c:CI * c + CI, 1], ACT.Sqrt,
                                     bias=vec(V_EPS, T)).then_inc(s["sd6"], 1)
            for c in range(NC):
                for f in range(4):
                    act.wait_ge(s["f1_ps"], 4 * c + f + 1)
                    nc.scalar.activation(fs[:, f, cs(c)], PS[:, 4 + f, 0:CT], ACT.Silu, bias=bf1[:, f:f + 1])\
                        .then_inc(s["fss"], 1)
                act.wait_ge(s["f2_ps"], c + 1)
                nc.scalar.activation(fo[:, cs(c)], PS[:, c, 0:CT], ACT.Identity, bias=col(BF2)).then_inc(s["fos"], 1)

        @block.vector
        def _(dve):
            v = nc.vector
            n_link = [0]

            def link(ins):
                n_link[0] += 1
                ins.then_inc(s["d_ch"], 1)
                dve.wait_ge(s["d_ch"], n_link[0])

            v.memset(kpad[:, 0:T - 1], 0.0)
            link(v.memset(mask[:, :, :], 1.0))
            link(v.memset(mask[:, :, 0:1], 0.0))
            dve.wait_ge(s["x_in"], 16)
            v.tensor_copy(xr.rearrange("p (j r c) -> p j r c", j=GP, r=PW)[:, 0:4],
                          xin.rearrange("p (r j c) -> p j r c", j=GP, r=PW)[:, 0:4]).then_inc(s["xr"], 1)
            dve.wait_ge(s["feps_f"], 1)
            link(v.tensor_tensor(feps, fabs, fsgn, ALU.mult))
            v.tensor_tensor(sbcol[:, :], sbcol[:, :], feps[:, 512:514], ALU.mult)
            link(v.tensor_tensor(swsrc, swsrc, feps[:, 0:512].rearrange("p (a b) -> p a b", a=2), ALU.mult))
            for k in range(2):
                last = v.scalar_tensor_tensor(wsrc[:, k, :], swsrc[:, k, :], feps[:, 512 + k:513 + k], wsrc[:, k, :],
                                              ALU.mult, ALU.add)
            last.then_inc(s["wn"], 1)
            link(v.tensor_tensor(bcol[:, :], bcol[:, :], sbcol[:, :], ALU.add))
            dve.wait_ge(s["wt_ps"], 1)
            v.tensor_copy(wT[:, :, :].rearrange("p a b -> p (a b)"), PS[:, 6, :]).then_inc(s["wt_sb"], 1)
            dve.wait_ge(s["misc_ps"], 1)
            v.tensor_copy(w3T[:, :], PS[:, 7, 0:128])
            v.tensor_copy(bT[:, :, :].rearrange("p a b -> p (a b)"), PS[:, 7, 128:128 + 3 * E0])
            v.tensor_copy(cbT[:, :], PS[0:64, 7, 160:224]).then_inc(s["misc_sb"], 1)
            v.tensor_scalar(peb[:, :], cst[:, C_PE:C_PE + L], col(B3), None, ALU.add)
            h0v = h0.rearrange("p (b t) -> p b t", b=NI)
            link(v.tensor_copy(h0v[:, :, 0], col(CLS).to_broadcast([128, NI])))
            for k in (1, 3):
                dve.wait_ge(s["xt_ps"], k + 1)
                v.tensor_copy(xT[:, k // 2, :].rearrange("p (q j) -> p j q", j=GP)[:, 4 * (k % 2):4 * (k % 2) + 4],
                              PS[:, k, :].rearrange("p (j q) -> p j q", j=4)).then_inc(s["xt_sb"], 1)
            dve.wait_ge(s["dt_e"], 1)
            v.tensor_scalar(q64[:, 0, :], lam[:, 0, :], col(LDT), None, ALU.mult)
            v.tensor_scalar(q64[:, 1, :], lam[:, 1, :], col(LDT), 1.0 / (2.0 * math.pi), ALU.mult, ALU.mult)\
                .then_inc(s["dtl"], 1)
            dve.wait_ge(s["attw_in"], 16 * 11)
            v.tensor_copy(wdec[:, :], col(WDEC).to_broadcast([128, 128]))
            v.tensor_copy(winp[:, 0, :], win[:, 0:D:2])
            v.tensor_copy(winp[:, 1, :], win[:, 1:D:2])
            v.tensor_copy(winsw[:, 0, :], win[:, 1:D:2])
            v.tensor_scalar(winsw[:, 1, :], win[:, 0:D:2], -1.0, None, ALU.mult)
            v.tensor_scalar(col(BANG), col(BANG), 1.0 / (2.0 * math.pi), None, ALU.mult)
            v.tensor_scalar(col(BDEC), col(BDEC), 0.5, None, ALU.mult)
            v.tensor_tensor(col(BISW), col(BISW), vec(V_SGN), ALU.mult).then_inc(s["attw"], 1)

            hf = [slice(0, 512), slice(512, 1024)]
            for n in range(2):
                dve.wait_ge(s["gi_ps"], n + 1)
                v.tensor_scalar(gmin[:, hf[n]], PS[:, 4 + 2 * n, :], bcol[:, 0:1], 20.0, ALU.add, ALU.min)\
                    .then_inc(s["gmn"], 1)
            for n in range(2):
                h = hf[n]
                dve.wait_ge(s["mexp"], n + 1)
                link(v.scalar_tensor_tensor(gate[:, h], emis[:, h], 2.0, emis[:, h], ALU.add, ALU.mult))
                link(v.tensor_scalar(gmin[:, h], gate[:, h], 2.0, None, ALU.add))
                link(v.reciprocal(gmin[:, h], gmin[:, h]))
                link(v.tensor_tensor(gate[:, h], gate[:, h], gmin[:, h], ALU.mult))
                link(v.scalar_tensor_tensor(gate[:, h], PS[:, 4 + 2 * n, :], bcol[:, 0:1], gate[:, h], ALU.add, ALU.mult))
                v.scalar_tensor_tensor(gate[:, h], PS[:, 5 + 2 * n, :], bcol[:, 1:2], gate[:, h], ALU.add, ALU.mult)\
                    .then_inc(s["gated"], 1)
            for n in range(2):
                dve.wait_ge(s["tok_ps"], n + 1)
                v.tensor_tensor(h0v[:, 8 * n:8 * n + 8, 1:T], PS[:, n, :].rearrange("p (b l) -> p b l", b=8),
                                spread(peb[:, :], 1, 8), ALU.add).then_inc(s["h0s"], 1)

            dve.wait_ge(s["args"], 2)
            link(v.tensor_scalar(pS, pTI, MAGIC, -MAGIC, ALU.add, ALU.add))
            v.tensor_tensor(pTI, pTI, pS, ALU.subtract).then_inc(s["fracs"], 1)

            def normalise(k, c):
                dve.wait_ge(s["sdv"], 4 * k + c + 1)
                link(v.reciprocal(sd[:, cs(c)], sd[:, cs(c)]))
                dst, xc, rec = xn[:, cs(c)], PS[:, LN_XC[k][c], 0:CT], sd[:, cs(c)]
                if k == 2:
                    dst, xc, rec = [z.rearrange("p (b t) -> p b t", b=CI) for z in (dst, xc, rec)]
                    dst = dst[:, :, ::-1]
                v.tensor_tensor(dst, xc, rec, ALU.mult).then_inc(s["xnr"], 1)

            for c in range(NC):
                normalise(0, c)

            flat_mask = mask[:, :, :].rearrange("p a b -> p (a b)")

            def phases(c):
                r = ring4[c % 2]
                dve.wait_ge(s["pj_ps"], c + 1)
                if c >= 2:
                    dve.wait_ge(s["out_ps"], c - 1)
                link(v.tensor_scalar(r[:, AN], PS[:, PJ[c % 2][0], 0:CT], 1.0 / (2.0 * math.pi), col(BANG), ALU.mult, ALU.add))
                link(v.tensor_tensor_scan(r[:, TH], flat_mask, r[:, AN], 0.0, ALU.mult, ALU.add))
                link(v.tensor_scalar(r[:, RM], r[:, TH], MAGIC, -MAGIC, ALU.add, ALU.add))
                v.tensor_tensor(r[:, FR], r[:, TH], r[:, RM], ALU.subtract).then_inc(s["frac"], 1)

            def recur(c):
                r = ring4[c % 2]
                dve.wait_ge(s["sc"], c + 1)
                v.scalar_tensor_tensor(r[:, CU], PS[:, PJ[c % 2][2], 0:CT], col(BI), r[:, CS_], ALU.add, ALU.mult)
                link(v.scalar_tensor_tensor(r[:, SU], PS[:, PJ[c % 2][3], 0:CT], col(BISW), r[:, SN], ALU.add, ALU.mult))
                link(v.tensor_tensor(r[:, GI], r[:, CU], r[:, SU], ALU.add))
                dve.wait_ge(s["decs"], c + 1)
                link(v.tensor_tensor_scan(r[:, GS], r[:, DEC], r[:, GI], 0.0, ALU.mult, ALU.add))
                v.tensor_tensor(r[:, RM], r[:, CS_], r[:, GS], ALU.mult)
                v.tensor_tensor(r[:, AN], r[:, SN], r[:, GS], ALU.mult).then_inc(s["rot"], 1)

            phases(0)
            phases(1)
            recur(0)
            phases(2)
            recur(1)
            phases(3)
            recur(2)
            recur(3)

            def q(k):
                return q64[:, k, :]

            def tt(o, x, y, op):
                link(v.tensor_tensor(o, x, y, op))

            dve.wait_ge(s["vv"], 1)
            v1r, v1i = VV[:, 1, 0, :], VV[:, 1, 1, :]
            v.tensor_scalar(q(0), v1r, -1.0, None, ALU.add)
            link(v.tensor_scalar(q(2), lam[:, 0, :], 1e-8, None, ALU.add))
            tt(q(3), q(2), q(2), ALU.mult)
            tt(q(4), lam[:, 1, :], lam[:, 1, :], ALU.mult)
            tt(q(3), q(3), q(4), ALU.add)
            link(v.reciprocal(q(3), q(3)))
            tt(q(4), q(0), q(2), ALU.mult)
            tt(q(5), v1i, lam[:, 1, :], ALU.mult)
            tt(q(4), q(4), q(5), ALU.add)
            tt(q(4), q(4), q(3), ALU.mult)
            tt(q(5), v1i, q(2), ALU.mult)
            tt(q(6), q(0), lam[:, 1, :], ALU.mult)
            tt(q(5), q(5), q(6), ALU.subtract)
            tt(q(5), q(5), q(3), ALU.mult)

            def cmul(re, im_, ar, ai, br, bi, t):
                tt(t, ai, bi, ALU.mult)
                tt(re, ar, br, ALU.mult)
                tt(re, re, t, ALU.subtract)
                tt(t, ar, bi, ALU.mult)
                tt(im_, ai, br, ALU.mult)
                tt(im_, im_, t, ALU.add)

            cmul(q(6), q(7), bc4[:, 0, :], bc4[:, 1, :], q(4), q(5), q(10))
            cmul(q(8), q(9), bc4[:, 2, :], bc4[:, 3, :], q(6), q(7), q(10))
            v.tensor_scalar(q(10), q(8), -1.0, None, ALU.mult).then_inc(s["qrec"], 1)

            for c in range(NC):
                normalise(1, c)

            dve.wait_ge(s["lg0_ps"], 1)
            lg0 = PS[0:T, 4, 0:128].rearrange("p (b e) -> p b e", b=NI)
            smv = [sm[:, k, :].rearrange("p (b e) -> p b e", b=NI) for k in range(3)]
            link(v.tensor_reduce(smr[:, 0, :], lg0, AX, ALU.max))
            v.tensor_tensor(smv[0], lg0, spread(smr[:, 0, :], 2, E0), ALU.subtract).then_inc(s["smx"], 1)
            dve.wait_ge(s["smx_e"], 1)
            link(v.tensor_reduce(smr[:, 1, :], smv[1], AX, ALU.add))
            link(v.reciprocal(smr[:, 1, :], smr[:, 1, :]))
            v.tensor_tensor(smv[2], smv[1], spread(smr[:, 1, :], 2, E0), ALU.mult).then_inc(s["sms"], 1)
            dve.wait_ge(s["st_ps"], 1)
            link(v.tensor_copy(rt0[:, 0, :], PS[:, 5, 0:T]))
            link(v.max(top8[:, 0, :], rt0[:, 0, :]))
            link(v.match_replace(rt0[:, 1, :], top8[:, 0, :], rt0[:, 0, :], -1.0))
            link(v.max(top8[:, 1, :], rt0[:, 1, :]))
            link(v.match_replace(rt0[:, 2, :], top8[:, 1, :], rt0[:, 1, :], -1.0))
            link(v.tensor_scalar(rt0[:, 3, :], rt0[:, 2, :], 0.0, None, ALU.is_lt))
            link(v.tensor_tensor_scan(rt0[:, 4, :], rt0[:, 3, :], rt0[:, 3, :], 0.0, ALU.add, ALU.max))
            v.tensor_tensor(rt0[:, 5, :], rt0[:, 4, :], rt0[:, 3, :], ALU.mult)
            v.tensor_tensor(rt0[:, 1, :], rt0[:, 0, :], rt0[:, 3, :], ALU.mult).then_inc(s["route0"], 1)
            dve.wait_ge(s["pt_ps"], 1)
            v.tensor_tensor(sel[0:T], spread(PS[0:T, 0, 0:128], 2, K0),
                            spread(cst[0:T, C_K16:C_K16 + K0], 1, 128), ALU.is_equal).then_inc(s["sels"], 1)
            for g in range(NC):
                dve.wait_ge(s["px_ps"], g + 1)
                v.scalar_tensor_tensor(selG[:, g, :], PS[:, 4 + g, 0:CT], vec(V_SLOT), gxs[:, g, :], ALU.is_equal, ALU.mult)\
                    .then_inc(s["selg"], 1)
            dve.wait_ge(s["prods"], 1)
            link(v.tensor_reduce(kpad[:, T - 1:2 * T - 1], prod, AX, ALU.add))
            v.tensor_tensor(kpad[:, T - 1:T], kpad[:, T - 1:T], col(DD), ALU.add).then_inc(s["kpads"], 1)
            for e in range(E0):
                dve.wait_ge(s["y0_ps"], e + 1)
                v.tensor_scalar(yT[:, :, e, :], PS[:, 2 + e % 2, 0:SL].rearrange("p (b k) -> p b k", b=NI),
                                bT[:, 2, e:e + 1], None, ALU.add).then_inc(s["y0s"], 1)
            for g in (1, 3):
                dve.wait_ge(s["yt_ps"], g + 1)
                v.tensor_copy(Yb[:, CI * g:CI * g + CI, :], PS[:, 4 + g, :].rearrange("p (b d) -> p b d", b=CI))\
                    .then_inc(s["ybs"], 1)
            for c in range(NC):
                normalise(2, c)
            for g in range(NC):
                dve.wait_ge(s["h2t_ps"], g + 1)
                link(v.tensor_copy(h2t[:, CI * g:CI * g + CI, :], PS[0:T, 4 + g, :].rearrange("p (b d) -> p b d", b=CI)))
            for g in range(NC):
                dve.wait_ge(s["cv_ps"], g + 1)
                v.tensor_tensor(h3[:, :, 32 * g:32 * g + 32], PS[0:T, g, :].rearrange("p (h b) -> p b h", b=NI),
                                h2t[:, :, 32 * g:32 * g + 32], ALU.add).then_inc(s["h3s"], 1)
            dve.wait_ge(s["h3s"], 4)

            for b in range(NI):
                last = v.bn_stats(lnst[:, b, :], h3[:, b, :])
            link(last)
            for b in range(NI):
                last = v.bn_aggr(mv[:, b, :], lnst[:, b, :])
            last.then_inc(s["st4"], 1)
            dve.wait_ge(s["sdv4"], 1)
            link(v.reciprocal(lnv[:, 2, :], lnv[:, 1, :]))
            link(v.tensor_tensor(lnv[:, 3, :], lnv[:, 2, :], lnv[:, 2, :], ALU.mult))
            v.tensor_tensor(lnv[:, 3, :], lnv[:, 3, :], mv[:, :, 1], ALU.mult).then_inc(s["st4"], 1)
            for b in range(NI):
                last = v.tensor_scalar(y4[:, b, :], h3[:, b, :], mv[:, b, 0:1], lnv[:, 2, b:b + 1], ALU.subtract, ALU.mult)
            last.then_inc(s["y4s"], 1)
            dve.wait_ge(s["sdv4"], 2)
            link(v.reciprocal(lnv[:, 5, :], lnv[:, 4, :]))
            link(v.tensor_tensor(lnv[:, 6, :], lnv[:, 5, :], lnv[:, 2, :], ALU.mult))
            for b in range(NI):
                last = v.tensor_scalar(yn5[0:T, b, :], h3[:, b, :], mv[:, b, 0:1], lnv[:, 6, b:b + 1], ALU.subtract, ALU.mult)
            last.then_inc(s["yn5s"], 1)
            dve.wait_ge(s["moe_in"], 16 * 13)
            for c in range(NC):
                dve.wait_ge(s["h5_ps"], c + 1)
                v.tensor_scalar(h5[:, cs(c)], PS[:, 4 + c, 0:CT], col(G1), col(B1), ALU.mult, ALU.add).then_inc(s["h5s"], 1)
            v.tensor_scalar(ws2[:, :, :], ws2[:, :, :], 0.25, None, ALU.mult)
            link(v.tensor_scalar(bs2[:, :], bs2[:, :], 0.25, None, ALU.mult))
            dve.wait_ge(s["lg_ps"], 2)

            def scores(b):
                return PS[0:T, 4 + b // 8, (b % 8) * E1:(b % 8 + 1) * E1]

            for b in range(NI):
                last = v.max(mx8[:, b, :], scores(b))
            link(last)
            for b in range(NI):
                last = v.max_index(ix8[:, b, :], mx8[:, b, :], scores(b))
            link(last)
            v.tensor_tensor(wk[:, 0, :], mx8[:, :, 1], mx8[:, :, 0], ALU.subtract).then_inc(s["w12a"], 1)
            link(v.tensor_copy(ef[:, :, :].rearrange("p k b -> p b k"), ix8[:, :, 0:2]))
            ohv = [oh[0:T, k, :].rearrange("p (b e) -> p b e", b=NI) for k in range(2)]
            for k in range(2):
                last = v.tensor_tensor(ohv[k], spread(cst[0:T, C_IOTA:C_IOTA + E1], 1, NI), spread(ef[:, k, :], 2, E1),
                                       ALU.is_equal)
            link(last)
            v.tensor_tensor(ohs[0:T], ohv[0], ohv[1], ALU.add).then_inc(s["ohss"], 1)
            dve.wait_ge(s["w12e"], 1)
            v.tensor_scalar(wts[:, 0, :], wk[:, 1, :], -0.5, 0.5, ALU.mult, ALU.add)
            v.tensor_scalar(wts[:, 1, :], wk[:, 1, :], 0.5, 0.5, ALU.mult, ALU.add).then_inc(s["w12"], 1)
            dve.wait_ge(s["ohts"], 4)
            link(v.tensor_tensor_scan(inc[0:E1, :], ohT[0:E1, :], ohT[0:E1, :], 0.0, ALU.add, ALU.max))
            cnt = inc[0:E1, N - 1:N]
            link(v.tensor_scalar(esm[:, 0:1], cnt, 1.0 / CAP, (CAP - 1.0) / CAP - 0.498, ALU.mult, ALU.add))
            v.tensor_scalar(esm[:, 1:2], esm[:, 0:1], MAGIC, -MAGIC, ALU.add, ALU.add).then_inc(s["nblks"], 1)
            dve.wait_ge(s["base_ps"], 1)
            v.tensor_scalar(esm[:, 3:4], PS[0:E1, 6, 0:1], float(CAP), -1.0, ALU.mult, ALU.add)
            v.tensor_scalar(esm[0:1, 6:7], PS[0:1, 6, 8:9], 1.0 / U, (U - 1.0) / U - 0.4, ALU.mult, ALU.add)
            v.tensor_tensor(esm[:, 4:5], PS[0:E1, 6, 0:1], esm[:, 1:2], ALU.add)
            link(v.tensor_copy(esm[:, 2:3], PS[0:E1, 6, 0:1]))
            v.tensor_scalar(trips[:, :], esm[0:1, 6:7], MAGIC, -MAGIC, ALU.add, ALU.add).then_inc(s["blks"], 1)
            link(v.tensor_scalar(obk[:, 0, :], cst[0:E1, C_IOTA:C_IOTA + NCOL], esm[:, 4:5], None, ALU.is_lt))
            v.scalar_tensor_tensor(obk[:, 1, :], cst[0:E1, C_IOTA:C_IOTA + NCOL], esm[:, 2:3], obk[:, 0, :], ALU.is_ge, ALU.mult)
            v.tensor_scalar(slT[0:E1, :], inc[0:E1, :], esm[:, 3:4], None, ALU.add).then_inc(s["slts"], 1)
            dve.wait_ge(s["slt_ps"], 1)
            slt = PS[0:T, 4:6, :].rearrange("p a b -> p (a b)")
            for k in range(2):
                last = v.tensor_tensor(sprod[0:T, k, :], oh[0:T, k, :], slt, ALU.mult)
            link(last)
            link(v.tensor_reduce(slot[:, 0, :], sprod[0:T].rearrange("p k (b e) -> p (k b) e", e=E1), AX, ALU.add))
            link(v.tensor_scalar(slot[:, 1, :], slot[:, 0, :], 1.0 / CAP, -0.498, ALU.mult, ALU.add))
            link(v.tensor_scalar(slot[:, 2, :], slot[:, 1, :], MAGIC, -MAGIC, ALU.add, ALU.add))
            v.tensor_copy(slotb[:, 1, :], slot[:, 2, :])
            link(v.scalar_tensor_tensor(slotb[:, 0, :], slot[:, 2, :], -float(CAP), slot[:, 0, :], ALU.mult, ALU.add))
            dve.wait_ge(s["iots"], 2)
            v.tensor_tensor(ohA[0:T], iotb, spread(slotb[:, 0, :], 1, CAP), ALU.is_equal)
            link(v.tensor_tensor(ohB[0:T, 0], iotb[:, 0:NCOL, :], spread(slotb[:, 1, :], 1, NCOL), ALU.is_equal))
            v.tensor_scalar(ohB[0:T, 1], ohB[0:T, 0], vec(V_T, T), None, ALU.mult)
            v.tensor_tensor(ohB[0:T, 2], ohB[0:T, 0], spread(cvb[:, :], 1, NCOL), ALU.mult).then_inc(s["tabs_in"], 1)
            dve.wait_ge(s["tab_ps"], 1)
            link(v.tensor_copy(tabf[:, 0:3, :].rearrange("p a b -> p (a b)"), PS[:, 5, 0:3 * NCOL]))
            v.scalar_tensor_tensor(tabf[:, 3, :], tabf[:, 2, :], float(T), tabf[:, 1, :], ALU.mult, ALU.add)
            link(v.tensor_scalar(tabf[:, 4, :], tabf[:, 0, :], -BIG, BIG, ALU.mult, ALU.add))
            v.tensor_scalar(taby[:, 0:1], vec(V_ONE), BIG, None, ALU.mult)
            v.tensor_tensor(taby[:, 1:NCOL + 1], tabf[:, 3, :], tabf[:, 4, :], ALU.add)
            link(v.tensor_scalar(tabf[:, 0, :], tabf[:, 3, :], float(N), -float(N), ALU.is_ge, ALU.mult))
            link(v.tensor_tensor(tabf[:, 0, :], tabf[:, 0, :], tabf[:, 3, :], ALU.add))
            v.tensor_tensor(tabx[:, :], tabf[:, 0, :], tabf[:, 4, :], ALU.add).then_inc(s["tabs"], 1)
            dve.wait_ge(s["x_out"], 16)
            for g in range(NC):
                dve.wait_ge(s["sh_ps"], g + 1)
                v.tensor_tensor(base2[0:T, CI * g:CI * g + CI, :], PS[0:T, g, :].rearrange("p (b d) -> p b d", b=CI),
                                spread(bs2[:, :], 1, CI), ALU.add).then_inc(s["b2s"], 1)

            dve.wait_ge(s["blks"], 2)
            dve_trips = dve.value_load(trips[0:1, 0:1], min_val=1, max_val=NCOL // U - 1)
            dve.wait_ge(s["p_io"], 1)

            def tokens(j, seen):
                dve.wait_ge(s["t_ps"], seen)
                v.tensor_scalar(xsr[:, j, :], PS[:, 3 + j, 0:CAP], col(G1), col(B1), ALU.mult, ALU.add).then_inc(s["t_sb"], 1)

            tokens(0, 1)
            with dve.Fori(0, dve_trips) as it:
                for j in range(U):
                    tokens((j + 1) % U, it * U + (j + 2))
                    dve.wait_ge(s["hss"], it * U + (j + 1))
                    dve.wait_ge(s["h_ps"], it * U + (j + 1))
                    bias = b1blk[:, :, bass.ds(it * U + j, 1)].to_broadcast([128, 4, CAP])
                    v.tensor_tensor(hpre[:, j, :].rearrange("p (c q) -> p c q", c=4),
                                    PS[:, j, :].rearrange("p (c q) -> p c q", c=4), bias, ALU.add).then_inc(s["hps"], 1)

            dve.wait_ge(s["w12"], 1)
            dve.wait_ge(s["b2s"], 4)
            for c in range(NC):
                bs = range(c * CI, c * CI + CI)
                dve.wait_ge(s[f"yl_in{c}"], 32)
                for k in range(2):
                    for b in bs:
                        last = v.scalar_tensor_tensor(base2[0:T, b, :], yl[0:T, k, b * D:(b + 1) * D], wts[:, k, b:b + 1],
                                                      base2[0:T, b, :], ALU.mult, ALU.add)
                    if k == 0:
                        link(last)
                last.then_inc(s["hms"], 1)
                dve.wait_ge(s["hms"], c + 1)
                for b in bs:
                    last = v.bn_stats(lnst[:, b, :], base2[0:T, b, :])
                link(last)
                for b in bs:
                    last = v.bn_aggr(mv[:, b, :], lnst[:, b, :])
                last.then_inc(s["st6"], 1)
                dve.wait_ge(s["sd6"], c + 1)
                link(v.reciprocal(lnv[:, 2, CI * c:CI * c + CI], lnv[:, 1, CI * c:CI * c + CI]))
                for b in bs:
                    last = v.tensor_scalar(xf[0:T, b, :], base2[0:T, b, :], mv[:, b, 0:1], lnv[:, 2, b:b + 1],
                                           ALU.subtract, ALU.mult)
                last.then_inc(s["xfs"], 1)
            for c in range(NC):
                dve.wait_ge(s["xf_ps"], c + 1)
                v.tensor_scalar(ff[:, cs(c)], PS[:, c, 0:CT], col(GF), col(BF), ALU.mult, ALU.add).then_inc(s["ffs"], 1)
            for c in range(NC):
                dve.wait_ge(s["fo_ps"], c + 1)
                dve.wait_ge(s["res"], c + 2)
                v.tensor_tensor(fin[:, CI * c:CI * c + CI, :], PS[0:T, c, :].rearrange("p (b d) -> p b d", b=CI),
                                h3[:, CI * c:CI * c + CI, :], ALU.add).then_inc(s["fins"], 1)

        @block.gpsimd
        def _(pool):
            p = nc.gpsimd
            n_link = [0]

            def link(ins):
                n_link[0] += 1
                ins.then_inc(s["p_ch"], 1)
                pool.wait_ge(s["p_ch"], n_link[0])

            pool.wait_ge(s["cst_in"], 16)
            pool.wait_ge(s["dtl"], 1)
            powers = spread(cst[:, C_PWR:C_PWR + NPW], 2, NS)
            for k, dst in enumerate((pAR, pTI)):
                p.tensor_tensor(dst, powers, spread(q64[:, k, :], 1, NPW), ALU.mult).then_inc(s["args"], 1)
            pool.wait_ge(s["trg"], 3)
            p.tensor_tensor(VV[:, :, 0, :], pE, pC, ALU.mult)
            p.tensor_tensor(VV[:, :, 1, :], pE, pS, ALU.mult).then_inc(s["vv"], 1)

            def decays(c):
                r = ring4[c % 2]
                if c < 2:
                    link(p.memset(r[:, DEC], 0.0))
                else:
                    pool.wait_ge(s["rot"], c - 1)
                pool.wait_ge(s["tdec"], c + 1)
                td = r[:, TD].rearrange("p (b t) -> p b t", b=CI)[:, :, 1:T]
                de = r[:, DEC].rearrange("p (b t) -> p b t", b=CI)[:, :, 1:T]
                p.tensor_scalar(de, td, 0.5, 0.5, ALU.mult, ALU.add).then_inc(s["decs"], 1)

            for c in range(NC):
                decays(c)

            pool.wait_ge(s["vv"], 1)
            pool.wait_ge(s["qrec"], 1)
            va = [VV[:, PB:NPW, k, :] for k in range(2)]
            t0, t1 = pE[:, 0:PA, :], pS[:, 0:PA, :]

            def fac(k):
                return spread(q64[:, k, :], 1, PA)

            p.tensor_tensor(t0, va[0], fac(8), ALU.mult)
            link(p.tensor_tensor(t1, va[1], fac(9), ALU.mult))
            link(p.tensor_tensor(UU[:, :, 0, :], t0, t1, ALU.subtract))
            p.tensor_tensor(t0, va[1], fac(10), ALU.mult)
            link(p.tensor_tensor(t1, va[0], fac(9), ALU.mult))
            link(p.tensor_tensor(UU[:, :, 1, :], t0, t1, ALU.subtract))
            uf = UU.rearrange("p a c n -> p a (c n)")
            vf = VV.rearrange("p a c n -> p a (c n)")
            for q in range(PA - 1):
                p.tensor_tensor(prod[:, PB * q:PB * q + PB, :], spread(uf[:, q, :], 1, PB), vf[:, 0:PB, :], ALU.mult)
            p.tensor_tensor(prod[:, T - 1, :], uf[:, PA - 1, :], vf[:, 0, :], ALU.mult).then_inc(s["prods"], 1)

            pool.wait_ge(s["cv_ps"], 4)
            p.iota(iotb, [[1, CAP], [0, NJ]], base=0, channel_multiplier=0, allow_small_or_imprecise_dtypes=True)\
                .then_inc(s["iots"], 1)
            p.iota(cvb[:, :], [[1, NJ]], base=0, channel_multiplier=0, allow_small_or_imprecise_dtypes=True)\
                .then_inc(s["iots"], 1)
            pool.wait_ge(s["yn5s"], 1)
            for g in range(1):
                p.tensor_tensor(h3, h3, y4, ALU.add).then_inc(s["res"], 1)
            pool.wait_ge(s["w12"], 1)
            ohv = [oh[0:T, k, :].rearrange("p (b e) -> p b e", b=NI) for k in range(2)]
            tmp = carve(h2[0:T, :], [[NI, E1]])[0]
            p.tensor_tensor(cmb, ohv[0], spread(wts[:, 0, :], 2, E1), ALU.mult)
            link(p.tensor_tensor(tmp, ohv[1], spread(wts[:, 1, :], 2, E1), ALU.mult))
            p.tensor_tensor(cmb, cmb, tmp, ALU.add).then_inc(s["cmbs"], 1)
            p.memset(xg, 0.0)
            p.memset(hs[:, U - 1, :], 0.0).then_inc(s["hss"], U)
            p.memset(w2r[:, U - 1, :], 0.0).then_inc(s["p_io"], 1)

            pool.wait_ge(s["blks"], 2)
            pool_trips = pool.value_load(trips[0:1, 0:1], min_val=1, max_val=NCOL // U - 1)
            last_x = pool.to_reg(N - 1)
            last_y = pool.to_reg(2 * N - 1)
            pool.wait_ge(s["tabs"], 1)
            pool.wait_ge(s["x_out"], 16)
            pool.wait_ge(s["p_io"], 1)

            def gather(j):
                pool.indirect_dma_start(out=xg[:, j, :], out_offset=None, in_=xrow_dram,
                                        in_offset=bass.IndirectOffsetOnAxis(ap=ixg[:, j:j + 1], axis=0),
                                        bounds_check=last_x, oob_is_err=False).then_inc(s[f"g_in{j}"], 16)

            def scatter(j):
                pool.indirect_dma_start(out=yrow_dram, out_offset=bass.IndirectOffsetOnAxis(ap=ixs[:, j:j + 1], axis=0),
                                        in_=ysb[:, j, :], in_offset=None,
                                        bounds_check=last_y, oob_is_err=False).then_inc(s[f"sc_out{j}"], 16)

            p.tensor_copy(ixg[:, 0:2], tabx[:, 0:2]).then_inc(s["ix_cp"], 1)
            pool.wait_ge(s["ix_cp"], 1)
            gather(0)
            gather(1)

            def pool_body(it, first):
                for j in range(U):
                    far, prev = (j + 2) % U, (j - 1) % U
                    if not (first and j == 0):
                        pool.wait_ge(s["t_ps"], it * U + j)
                        pool.sem_inc(s["p_rd"], 1)
                    p.tensor_copy(ixg[:, far:far + 1], tabx[:, bass.ds(it * U + (j + 2), 1)])
                    if not first:
                        pool.wait_ge(s[f"sc_out{prev}"], it * 16)
                        pool.sem_inc(s["p_rd"], 1)
                    p.tensor_copy(ixs[:, prev:prev + 1], taby[:, bass.ds(it * U + j, 1)]).then_inc(s["ix_cp"], 1)
                    pool.wait_ge(s["ix_cp"], it * U + (j + 2))
                    pool.sem_inc(s["p_rd"], 1)
                    gather(far)
                    pool.wait_ge(s["ysbs"], it * U + (j + 1))
                    pool.sem_inc(s["p_rd"], 1)
                    scatter(prev)

            pool_body(0, True)
            with pool.Fori(1, pool_trips) as it:
                pool_body(it, False)
            pool.wait_ge(s[f"sc_out{U - 1}"], pool_trips * 16)
            pool.sem_inc(s["p_rd"], 1)
            p.tensor_copy(ixs[:, U - 1:U], taby[:, bass.ds(pool_trips * U, 1)]).then_inc(s["ix_cp"], 1)
            pool.wait_ge(s["ix_cp"], pool_trips * U + 2)
            pool.sem_inc(s["p_rd"], 1)
            pool.wait_ge(s["ysbs"], pool_trips * U + 1)
            pool.sem_inc(s["p_rd"], 1)
            scatter(U - 1)

            pool.wait_ge(s["res"], 1)
            for c in range(NC):
                pool.wait_ge(s["hms"], c + 1)
                p.tensor_tensor(h3[:, CI * c:CI * c + CI, :], h3[:, CI * c:CI * c + CI, :],
                                base2[0:T, CI * c:CI * c + CI, :], ALU.add).then_inc(s["res"], 1)


def kernel(**inputs):
    import concourse.bacc as _bacc
    from concourse.bass_utils import run_bass_kernel_spmd as _run

    nc = _bacc.Bacc("TRN2", target_bir_lowering=False, num_devices=1)
    arrays, args = {}, {}
    inputs = dict(inputs, constants=shape_constants())
    for name, value in inputs.items():
        v = np.ascontiguousarray(value)
        arrays[f"in_{name}"] = v
        args[name] = nc.dram_tensor(f"in_{name}", v.shape, mybir.dt.from_np(v.dtype), kind="ExternalInput").ap()
    out = nc.dram_tensor("out", (NI, T, D), F32, kind="ExternalOutput").ap()
    build(nc, args, out)
    r = _run(nc, [arrays], core_ids=[0])
    return r.results[0]["out"]
```

```python
from contextlib import ExitStack
import math

import numpy as np

import concourse.bass as bass
from concourse import mybir

F32 = mybir.dt.float32
BF16 = mybir.dt.bfloat16
I32 = mybir.dt.int32
U32 = mybir.dt.uint32
ALU = mybir.AluOpType
ACT = mybir.ActivationFunctionType
AX = mybir.AxisListType.X

NI, GP, PW, D = 16, 8, 16, 128
L = GP * GP
T = L + 1
N = NI * T
CI = 4
NC = NI // CI
CT = CI * T
E0, K0, F0 = 8, 2 * T // 8, 256
SL = NI * K0
NS = 64
PB, PA = 8, 9
E1, F1, FS = 64, 512, 256
CAP = 128
NBLK = E1 + 2 * N // CAP
U = 4
NCOL = (NBLK // U + 2) * U
NOUT = (NBLK // U + 1) * U + 1
BIG = 1.0e6
MAGIC = 12582912.0
TWO_PI = 6.2831850
EPS = 1e-5
NG = -(-N // 128)
NP = NG * 128
NJ = 2 * NG
TAIL = [(g, min(g + 2, NG)) for g in range(0, NG, 2)]
SQRT_GUESS = 1597463007.0

C_ID, C_CEN, C_ONE, C_PA, C_PB = 0, 128, 256, 384, 512
C_PE = 640
C_TRI = C_PE + L
C_EX = C_TRI + E1
C_IOTA = C_EX + CI * 128
C_K16 = C_IOTA + 128
C_PWR = C_K16 + K0
C_VEC = C_PWR + PA + PB
V_SLOT, V_E, V_EPS, V_HPI, V_SGN, V_T, V_ONE = range(7)
C_ALL = C_VEC + 7


def shape_constants():
    c = np.zeros((128, C_ALL), np.float32)
    eye = np.eye(128, dtype=np.float32)
    c[:, C_ID:C_ID + 128] = eye
    c[:, C_CEN:C_CEN + 128] = eye - 1.0 / D
    c[:, C_ONE:C_ONE + 128] = 1.0 / D
    for p in range(64):
        c[p, C_PA + 2 * p] = 1.0
        c[64 + p, C_PA + 2 * p + 1] = 1.0
        c[64 + p, C_PB + 2 * p] = -1.0
        c[p, C_PB + 2 * p + 1] = 1.0
    pos = np.arange(L, dtype=np.float32)[:, None]
    div = np.exp(np.arange(0, D, 2, dtype=np.float32) * np.float32(-math.log(10000.0) / D)).astype(np.float32)
    ang = pos * div
    c[:, C_PE:C_PE + L] = np.stack([np.sin(ang), np.cos(ang)], axis=-1).reshape(L, D).T
    c[:E1, C_TRI:C_TRI + E1] = np.triu(np.ones((E1, E1), np.float32), 1)
    for r in range(128):
        for b in range(CI):
            if (r // E0) % CI == b:
                c[r, C_EX + b * 128 + (r % E0) * K0:C_EX + b * 128 + (r % E0 + 1) * K0] = 1.0
    c[:, C_IOTA:C_IOTA + 128] = np.arange(128)
    c[:, C_K16:C_K16 + K0] = np.arange(1, K0 + 1)
    c[:, C_PWR:C_PWR + PB] = np.arange(PB)
    c[:, C_PWR + PB:C_PWR + PB + PA] = PB * np.arange(PA)
    c[:, C_VEC + V_SLOT] = np.arange(128) % K0 + 1
    c[:, C_VEC + V_E] = np.arange(128)
    c[:, C_VEC + V_EPS] = EPS
    c[:, C_VEC + V_HPI] = math.pi / 2
    c[:, C_VEC + V_SGN] = np.where(np.arange(128) < 64, 1.0, -1.0)
    c[:, C_VEC + V_T] = np.arange(128)
    c[:, C_VEC + V_ONE] = 1.0
    return c

(B3, CLS, BANG, BDEC, BI, BISW, LDT, DD, G1, B1, GF, BF) = range(12)
S_B1 = 12
S_WG = S_B1 + 3 * E0
S_BS1 = S_WG + E0
S_BF1 = S_BS1 + FS // 128
S_ALL = S_BF1 + F1 // 128


def packed(a):
    f = {k: np.asarray(v) for k, v in a.items()}

    def wide(v):
        return np.broadcast_to(v, (128, v.size))

    tok = [f[f"L0_tok_{n}"] for n in ("eps_in1", "eps_in2", "eps_out1", "eps_out2")]
    eps = [e.reshape(2, 128).T for e in tok[:2]] + [wide(e) for e in tok[2:]] + [e[:, None] for e in tok[2:]]
    eps += [f[f"L0_tok_W{k}_{n}"][:, None] for n in ("b", "sb") for k in (1, 2)]
    weights = np.stack([np.stack([f[f"L0_tok_W{k}_{n}"] for k in (1, 2)]) for n in ("w", "sw")])
    patches = f["x"].reshape(NI, GP, PW, GP, PW).transpose(0, 1, 3, 2, 4).reshape(2, NI * L // 2, 2, 128)
    w_in, b_in = f["L0_attn_W_input"], f["L0_attn_b_input"]
    attw = [f["L0_tok_W3_w"].T, f["L0_attn_W_angle"], f["L0_attn_W_angle"],
            np.broadcast_to(f["L0_attn_W_decay"], (D, 128)), w_in[:, 0::2], w_in[:, 1::2], w_in[:, 1::2], w_in[:, 0::2]]
    small = [f["L0_tok_W3_b"], f["cls_tok"].reshape(D), np.tile(f["L0_attn_b_angle"], 2), wide(f["L0_attn_b_decay"])[:, 0],
             np.concatenate([b_in[0::2], b_in[1::2]]), np.concatenate([b_in[1::2], b_in[0::2]]), f["L1_attn_log_dt"],
             f["L1_attn_D"], f["L1_ffn_ln1_g"], f["L1_ffn_ln1_b"], f["L1_ffn_ffln_g"], f["L1_ffn_ffln_b"]]
    b1 = f["L0_ffn_b1"].reshape(E0, 128, 2)
    small = [v[:, None] for v in small] + [b1[:, :, 0].T, b1[:, :, 1].T, f["L0_ffn_b2"].T, f["L0_ffn_Wg"],
                                           f["L1_ffn_bs1"].reshape(128, -1), f["L1_ffn_bf1"].reshape(128, -1)]
    ssm = [wide(f[f"L1_attn_Lambda_{n}"]) for n in ("real", "imag")]
    ssm += [f[f"L1_attn_{n}"] for n in ("B_real", "B_imag", "C_real", "C_imag")]
    moe = [f["L1_ffn_Ws1"], f["L1_ffn_Ws2"].reshape(128, -1), wide(f["L1_ffn_bs2"]), wide(f["L1_ffn_bf2"])]
    rest = ("L0_ffn_W1", "L0_ffn_W2", "L1_ffn_W1", "L1_ffn_W2", "L1_ffn_Wf1", "L1_ffn_Wf2")
    return {
        "eps": np.concatenate(eps, 1),
        "tok_weights": weights.reshape(2, 2, 128, 2, 128).transpose(4, 0, 1, 3, 2).reshape(128, 8, 128),
        "patches": patches.transpose(0, 3, 2, 1),
        "attn_weights": np.concatenate(attw, 1),
        "small": np.concatenate(small, 1),
        "ssm": np.concatenate(ssm, 1),
        "moe": np.concatenate(moe, 1),
        "experts_b": np.concatenate([f["L1_ffn_b1"], f["L1_ffn_b2"], f["L1_ffn_codebook"].T, f["L1_ffn_Wr"].T], 1),
        "constants": shape_constants(),
        **{k: f[k] for k in rest},
    }


SEMAPHORES = """
zero y_clear cst_in x_in0 x_in1 eps_in tokw_in attw_in small_in ssm_in ffn0_in moe_in moe2_in
feps_f wn wc_ps wcs gi_ps gmn mexp numer gated tok_ps h0s
xc sqr var sdv xnr pj_ps attw tdec decs frac sc rot out_ps h1s
lg0_ps smx smx_e sms st_ps route0 pt_ps sels xtm_ps xtms gx_ps gxc ga_ps exts px_ps selg
hid_ps gelu y0_ps y0s yt_ps ybs h2_ps h2s xs_ps xss h2t_ps cv_ps h3s
dtl args fracs trg vv qrec prods kpads kp_out toep_in
st4 sdv4 yn5s x_out yn5a h5_ps h5s lg_ps w12a w12e w12 ohss ohs_ps ohts nblks base_ps slts slt_ps rr_out rr_in
s1_ps s1s cmbs cmb_ps cmb_sb sh_ps b2s tabs_in blk_ps blks tab_ps tabs iots
w1_in0 w1_in1 w1_in2 w1_in3 w2_in0 w2_in1 w2_in2 w2_in3
g_in0 g_in1 g_in2 g_in3 yr_out0 yr_out1 yr_out2 yr_out3 t_ps t_sb h_ps hps hss y_ps ysbs resb ix_cp p_rd sp_rd p_io
yl_in0 yl_in1 yl_in2 yl_in3 yl_in4 hms xfs xf_ps ffs f1_ps fss f2_ps fins out_in res
a_ch d_ch p_ch
""".split()


def build(nc, a, out):
    xrow_dram = nc.dram_tensor("moe_rows", [N, D], F32, kind="Internal").ap()
    yrow_dram = nc.dram_tensor("moe_out_rows", [NOUT * CAP, D], F32, kind="Internal").ap()
    rrow_dram = nc.dram_tensor("residual_rows", [N, D], F32, kind="Internal").ap()
    kpad_dram = nc.dram_tensor("ssm_kernel", [128, 2 * T - 1], F32, kind="Internal").ap()

    ctx = ExitStack()
    with ctx:
        def sb(name, shape, dt=F32):
            return ctx.enter_context(nc.sbuf_tensor(name, shape, dt))[:]

        s = {n: ctx.enter_context(nc.semaphore(n)) for n in SEMAPHORES}
        PS = ctx.enter_context(nc.psum_tensor("PS", [128, 8, 512], F32))[:]

        def carve(region, shapes):
            views, at = [], 0
            for shape in shapes:
                n = math.prod(shape)
                v = region[:, at:at + n]
                if len(shape) == 2:
                    v = v.rearrange("p (a b) -> p a b", a=shape[0])
                elif len(shape) == 3:
                    v = v.rearrange("p (a b c) -> p a b c", a=shape[0], b=shape[1])
                views.append(v)
                at += n
            assert at <= region.shape[1], (at, region.shape)
            return views

        R1 = sb("R1", [128, 8448])
        R2 = sb("R2", [128, 12400])
        R3 = sb("R3", [128, 7680])
        R4 = sb("R4", [128, 26 * CT])
        R5 = sb("R5", [128, 4096])
        RF = sb("RF", [128, 6 * N])

        cst = sb("cst", [128, C_ALL])
        ident = cst[:, C_ID:C_ID + 128]
        cen = cst[:, C_CEN:C_CEN + 128]
        onesd = cst[:, C_ONE:C_ONE + 128]
        perm_a = cst[:, C_PA:C_PA + 128]
        perm_b = cst[:, C_PB:C_PB + 128]

        def vec(k, rows=128):
            return cst[0:rows, C_VEC + k:C_VEC + k + 1]

        h0, h1, h2, xn, sq, sd = carve(RF, [[N]] * 6)

        xT, gmin, emis, gate = carve(R2, [[2, 2, 512], [1024], [1024], [1024]])
        feps, fabs, fsgn, tokw = carve(R4, [[266], [262], [262], [8, 128]])
        bcol = sb("bcol", [128, 2])
        peb = sb("peb", [128, L])
        two, dt = sb("two", [128, 1]), sb("dt", [128, 1])
        small = sb("small", [128, S_ALL])
        attw = sb("attw", [128, 5, 128])
        w3T, wang, wdec, winp, winsw = [attw[:, k, :] for k in range(5)]

        def col(k):
            return small[:, k:k + 1]

        mask = sb("mask", [128, CI, T])
        ring4 = carve(R4, [[13, CT], [13, CT]])
        wg = small[:, S_WG:S_WG + E0]
        w1a, w2a = carve(R5, [[E0, F0], [E0, 2, D]])
        bT = small[:, S_B1:S_B1 + 3 * E0].rearrange("p (c e) -> p c e", c=3)
        xtm, sel, exT, yT, Yb, gxs, selG = carve(
            R2, [[NI, D], [128, K0], [E0, NI, K0], [NI, E0, K0], [NI, D], [NC, CT], [NC, CT]])
        sm = sb("sm", [T, 4, 128])
        smr = sb("smr", [T, 2, NI])
        rt0 = sb("rt0", [128, 6, T])
        top8 = sb("top8", [128, 2, 8])
        ssm = sb("ssm", [128, 6, NS])
        lam, bc4 = ssm[:, 0:2, :], ssm[:, 2:6, :]
        NPW = PB + PA
        pAR, pTI, pE, pS, pC, UU, q64 = carve(R3, [[NPW, NS]] * 5 + [[PA, 2, NS], [14, NS]])
        VV, = carve(R3, [[NPW, 2, NS]])
        prod, = carve(R1, [[T, 2 * NS]])
        kpad = sb("kpad", [128, 2 * T - 1])
        toep, = carve(R1, [[D, T]])
        xs, h2t, h3 = carve(R4[0:T, :], [[NI, D]] * 3)
        hres = h2t
        lnst = sb("lnst", [T, NI, 6])
        mv = sb("mv", [T, NI, 2])
        lnv = sb("lnv", [T, 8, NI])
        yn5, h5, oh, ohs, ohT, inc, slT = carve(
            R2, [[NI, D], [NP], [2, NG * E1], [NG * E1], [N], [N], [NP]])
        base2 = carve(R2, [[NG, D]])[0]
        wc = sb("wc", [128, E1])
        mx8, ix8 = sb("mx8", [128, NG, 8]), sb("ix8", [128, NG, 8], U32)
        ef = sb("ef", [128, 2, NG])
        wk = sb("wk", [128, 2, NG])
        wts = sb("wts", [128, 2, NG])
        esm = sb("esm", [E1, 8])
        obk = sb("obk", [E1, 2, NCOL])
        experts_b = sb("experts_b", [E1, F1 + D + E1 + D])
        b1all, b2all = experts_b[:, 0:F1], experts_b[:, F1:F1 + D]
        cbT, wrT = experts_b[:, F1 + D:F1 + D + E1], experts_b[:, F1 + D + E1:F1 + D + E1 + D]
        moe = sb("moe", [128, 2 * FS + 2 * D])
        ws1, ws2 = moe[:, 0:FS], moe[:, FS:2 * FS].rearrange("p (c d) -> p c d", c=2)
        bs2, bf2 = moe[:, 2 * FS:2 * FS + D], moe[:, 2 * FS + D:2 * FS + 2 * D]
        bs1, bf1 = small[:, S_BS1:S_BF1], small[:, S_BF1:S_ALL]
        s1, = carve(RF, [[2, N]])
        cmb, cmbT = carve(sq, [[NG, E1]])[0], sd
        sprod, ohAf, ohBf = carve(R1, [[2, NG * E1], [CAP * NJ // 2], [3 * NCOL * NJ // 2]])
        ohA = ohAf.bitcast(BF16).rearrange("p (a j) -> p a j", a=CAP)
        ohB = ohBf.bitcast(BF16).rearrange("p (q i j) -> p q i j", q=3, i=NCOL)
        iotb = R4[:, 0:CAP * NJ // 2].bitcast(BF16).rearrange("p (a j) -> p a j", a=CAP)
        slot = sb("slot", [128, 3, NJ])
        slotb = sb("slotb", [128, 2, NJ], BF16)
        cvb = sb("cvb", [128, NJ], BF16)
        tabf, = carve(xn, [[5, NCOL]])
        tabx, yix = sb("tabx", [128, NCOL], U32), sb("yix", [128, NJ], U32)
        bexp, trips = sb("bexp", [1, NCOL], I32), sb("trips", [1, 1], I32)
        b1blk = sb("b1blk", [128, 4, NCOL])
        zeros = sb("zeros", [128, D])
        w1r, w2r, hs = carve(R3, [[U, F1], [U, 4 * D], [U, 4 * CAP]])
        hpre, xg, xsr, ysb = carve(R5, [[U, 4 * CAP], [U, D], [U, CAP], [U, D]])
        ixg = sb("ixg", [128, U], U32)
        yl, xf, fs = carve(R2[:, 2048:], [[NJ, D], [NG, D], [4, N]])
        resg, = carve(R4, [[NG, D]])
        st6, mv6 = sb("st6", [128, NG, 6]), sb("mv6", [128, NG, 2])
        nw = sb("nw", [128, 4, NG])
        nwi = sb("nwi", [128, NG], I32)
        wf1, wf2 = carve(h2, [[F1], [4, D]])
        ff = xn
        hid, = carve(R2, [[2, 2 * SL]])
        y_dst = yT

        def cs(c):
            return slice(c * CT, (c + 1) * CT)

        def im(b):
            return slice(b * T, (b + 1) * T)

        def tile4(b):
            return slice((b % CI) * T, (b % CI + 1) * T)

        def tok4(b):
            return slice((b % CI) * D, (b % CI + 1) * D)

        def rows(g):
            return min(128, N - 128 * g)

        def gc(g):
            return slice(128 * g, 128 * g + rows(g))

        def spread(ap, axis, n):
            shape = list(ap.shape)
            return ap.unsqueeze(axis).to_broadcast(shape[:axis] + [n] + shape[axis:])

        LN_XC = [[2, 3, 0, 1], [0, 1, 2, 3], [4, 5, 6, 7]]
        LN_VAR = [[4, 5, 6, 7], [4, 5, 6, 7], [0, 1, 2, 3]]
        PJ = [[2, 3, 4, 5], [0, 1, 6, 7]]
        TD, DEC, AN, TH, RM, FR, AF, SN, CS_, CU, SU, GI, GS = range(13)

        block = ctx.enter_context(nc.Block())

        @block.sync
        def _(sp):
            sp.dma_start(feps, a["eps"]).then_inc(s["eps_in"], 16)
            sp.dma_start(xT[:, 0], a["patches"][0]).then_inc(s["x_in0"], 16)
            sp.dma_start(xT[:, 1], a["patches"][1]).then_inc(s["x_in1"], 16)
            sp.dma_start(cst, a["constants"]).then_inc(s["cst_in"], 16)
            sp.dma_start(w1a, a["L0_ffn_W1"].rearrange("e h f -> h e f")).then_inc(s["ffn0_in"], 16)
            sp.dma_start(w2a, a["L0_ffn_W2"].rearrange("e (p c) h -> p e c h", c=2)).then_inc(s["ffn0_in"], 16)
            sp.dma_start(experts_b, a["experts_b"]).then_inc(s["moe_in"], 16)
            sp.dma_start(moe, a["moe"]).then_inc(s["moe_in"], 16)
            sp.wait_ge(s["zero"], 1)
            sp.dma_start(yrow_dram.rearrange("(n p) d -> p n d", p=CAP), spread(zeros[:, :], 1, NOUT)).then_inc(s["y_clear"], 16)
            sp.wait_ge(s["kpads"], 1)
            sp.dma_start(kpad_dram, kpad[:, :]).then_inc(s["kp_out"], 16)
            sp.wait_ge(s["kp_out"], 16)
            skewed = bass.AP(kpad_dram.tensor, 0, [[1, T], [2 * T - 1, D], [1, T]])
            sp.dma_start(toep[0:T], skewed).then_inc(s["toep_in"], 16)
            sp.wait_ge(s["yn5s"], NC)
            sp.wait_ge(s["yn5a"], NC)
            sp.dma_start(xrow_dram.rearrange("(b t) d -> t b d", b=NI), yn5[0:T]).then_inc(s["x_out"], 16)
            sp.wait_ge(s["res"], 1)
            sp.dma_start(rrow_dram.rearrange("(b t) d -> t b d", b=NI), hres).then_inc(s["rr_out"], 16)
            sp.wait_ge(s["cmbs"], 1)
            sp.dma_start(wf1, a["L1_ffn_Wf1"]).then_inc(s["moe2_in"], 16)
            sp.dma_start(wf2, a["L1_ffn_Wf2"].rearrange("(p c) d -> p c d", p=128)).then_inc(s["moe2_in"], 16)

            sp.wait_ge(s["rr_out"], 16)
            sp.wait_ge(s["tabs_in"], 1)
            full = NG - 1 if rows(NG - 1) < 128 else NG
            sp.dma_start(resg[:, 0:full, :], rrow_dram[0:128 * full].rearrange("(g p) d -> p g d", p=128)).then_inc(s["rr_in"], 16)
            if full < NG:
                sp.dma_start(resg[0:rows(full), full, :], rrow_dram[128 * full:N]).then_inc(s["rr_in"], 16)

            sp.wait_ge(s["blks"], 2)
            n_trips = sp.value_load(trips[0:1, 0:1], min_val=1, max_val=NCOL // U - 1)

            def expert(at):
                return sp.value_load(bexp[0:1, at], min_val=0, max_val=E1 - 1)

            def load_first(j, e):
                sp.dma_start(w1r[:, j, :], a["L1_ffn_W1"][bass.ds(e, 1)].rearrange("o h f -> (o h) f"))\
                    .then_inc(s[f"w1_in{j}"], 16)

            def load_second(j, e):
                sp.dma_start(w2r[:, j, :], a["L1_ffn_W2"][bass.ds(e, 1)].rearrange("o (p c) d -> (o p) (c d)", p=128))\
                    .then_inc(s[f"w2_in{j}"], 16)

            sp.wait_ge(s["p_io"], 1)
            for j in range(U):
                e = expert(slice(j, j + 1))
                load_first(j, e)
                if j == U - 1:
                    sp.wait_ge(s["y_ps"], 1)
                load_second(j, e)
            with sp.Fori(1, n_trips) as it:
                for j in range(U):
                    sp.wait_ge(s["h_ps"], it * U + (j - U + 1))
                    sp.sem_inc(s["sp_rd"], 1)
                    e = expert(bass.ds(it * U + j, 1))
                    load_first(j, e)
                    sp.wait_ge(s["y_ps"], it * U + (j - U + 2))
                    load_second(j, e)
            for c, (lo, hi) in enumerate(TAIL):
                sp.wait_ge(s["fins"], c + 1)
                dst = out.rearrange("b t d -> (b t) d")[128 * lo:min(N, 128 * hi)]
                if rows(lo) == 128:
                    dst = dst.rearrange("(g p) d -> p g d", p=128)
                    sp.dma_start(dst, resg[:, lo:hi, :]).then_inc(s["out_in"], 16)
                else:
                    sp.dma_start(dst, resg[0:rows(lo), lo, :]).then_inc(s["out_in"], 16)
            sp.wait_ge(s["out_in"], 16 * len(TAIL))

        @block.tensor
        def _(pe):
            mm, tr = nc.tensor.matmul, nc.tensor.transpose
            pe.wait_ge(s["wn"], 1)
            for n in range(2):
                pe.wait_ge(s[f"x_in{n}"], 16)
                for k in range(2):
                    for h in range(2):
                        last = mm(PS[:, 4 + 2 * n + k, :], tokw[:, 2 * k + h, :], xT[:, n, h, :], start=h == 0, stop=h == 1)
                last.then_inc(s["gi_ps"], 1)
            pe.wait_ge(s["attw_in"], 16)
            for n in range(2):
                pe.wait_ge(s["gated"], n + 1)
                mm(PS[:, n, :], w3T, gate[:, n * 512:(n + 1) * 512], start=True, stop=True).then_inc(s["tok_ps"], 1)
            pe.wait_ge(s["cst_in"], 16)

            def centre(k, c, src):
                mm(PS[:, LN_XC[k][c], 0:CT], cen, src[:, cs(c)], start=True, stop=True).then_inc(s["xc"], 1)

            def variance(k, c):
                pe.wait_ge(s["sqr"], 4 * k + c + 1)
                mm(PS[:, LN_VAR[k][c], 0:CT], onesd, sq[:, cs(c)], start=True, stop=True).then_inc(s["var"], 1)

            for c in range(NC):
                pe.wait_ge(s["h0s"], 1 + c // 2)
                centre(0, c, h0)
                if c:
                    variance(0, c - 1)
            variance(0, NC - 1)

            def project(c):
                bk = PJ[c % 2]
                pe.wait_ge(s["xnr"], 2 if c == 0 else 4)
                if c >= 2:
                    pe.wait_ge(s["h1s"], c - 1)
                x = xn[:, cs(c)]
                mm(PS[:, bk[0], 0:CT], wang, x, start=True, stop=True)
                mm(PS[:, bk[1], 0:CT], wdec, x, start=True, stop=True)
                mm(PS[:, bk[2], 0:CT], winp, x, start=True, stop=True)
                mm(PS[:, bk[3], 0:CT], winsw, x, start=True, stop=True)\
                    .then_inc(s["pj_ps"], 1)

            def rotate_back(c):
                r = ring4[c % 2]
                pe.wait_ge(s["rot"], c + 1)
                bank = PS[:, PJ[c % 2][0], 0:CT]
                mm(bank, ident, h0[:, cs(c)], start=True, stop=False)
                mm(bank, perm_a, r[:, RM], start=False, stop=False)
                mm(bank, perm_b, r[:, AN], start=False, stop=True).then_inc(s["out_ps"], 1)

            pe.wait_ge(s["attw"], 1)
            project(0)
            project(1)
            rotate_back(0)
            project(2)
            rotate_back(1)
            project(3)
            rotate_back(2)
            rotate_back(3)

            pe.wait_ge(s["h1s"], 4)
            for c in range(NC):
                centre(1, c, h1)
                if c:
                    variance(1, c - 1)
            variance(1, NC - 1)

            pe.wait_ge(s["ffn0_in"], 32)
            pe.wait_ge(s["xnr"], 8)
            for b in range(NI):
                last = mm(PS[0:T, 4, b * E0:(b + 1) * E0], xn[:, im(b)], wg, start=True, stop=True)
            last.then_inc(s["lg0_ps"], 1)
            for b in range(NI):
                last = tr(PS[0:T, b // CI, tok4(b)], xn[:, im(b)], ident)
                if b % CI == CI - 1:
                    last.then_inc(s["xtm_ps"], 1)
            pe.wait_ge(s["sms"], 1)
            tr(PS[:, 5, 0:T], sm[:, 2, :], ident[0:T, 0:T]).then_inc(s["st_ps"], 1)
            pe.wait_ge(s["route0"], 1)
            pe.wait_ge(s["xtms"], 4)
            tr(PS[0:T, 0, 0:128], rt0[:, 5, :], ident).then_inc(s["pt_ps"], 1)
            for b in range(NI):
                g = b // CI
                last = mm(PS[:, 4 + g, tile4(b)],
                          cst[32 * g:32 * g + 32, C_EX + (b % CI) * 128:C_EX + (b % CI + 1) * 128],
                          rt0[32 * g:32 * g + 32, 1, :], start=True, stop=True)
                if b % CI == CI - 1:
                    last.then_inc(s["gx_ps"], 1)
            pe.wait_ge(s["sels"], 1)
            for b in range(NI):
                last = mm(PS[:, b // CI, tok4(b)], xtm[0:T, b, :],
                          sel[0:T, b * E0:(b + 1) * E0, :].rearrange("p e k -> p (e k)"), start=True, stop=True)
                if b % CI == CI - 1:
                    last.then_inc(s["ga_ps"], 1)
            for b in range(NI):
                g = b // CI
                if b % CI == 0:
                    pe.wait_ge(s["gxc"], g + 1)
                last = mm(PS[:, 4 + g, tile4(b)],
                          cst[32 * g:32 * g + 32, C_EX + (b % CI) * 128:C_EX + (b % CI + 1) * 128],
                          rt0[32 * g:32 * g + 32, 5, :], start=True, stop=True)
                if b % CI == CI - 1:
                    last.then_inc(s["px_ps"], 1)

            def hidden0(e):
                if e == 0:
                    pe.wait_ge(s["exts"], 4)
                if e >= 2:
                    pe.wait_ge(s["gelu"], e - 1)
                for c in range(2):
                    last = mm(PS[:, e % 2, c * SL:(c + 1) * SL], w1a[:, e, c:F0:2],
                              exT[:, e].rearrange("p b k -> p (b k)"), start=True, stop=True)
                last.then_inc(s["hid_ps"], 1)

            hidden0(0)
            for e in range(E0):
                if e + 1 < E0:
                    hidden0(e + 1)
                pe.wait_ge(s["gelu"], e + 1)
                if e >= 2:
                    pe.wait_ge(s["y0s"], e - 1)
                for c in range(2):
                    last = mm(PS[:, 2 + e % 2, 0:SL], w2a[:, e, c, :], hid[:, e % 2, c * SL:(c + 1) * SL],
                              start=c == 0, stop=c == 1)
                last.then_inc(s["y0_ps"], 1)
            pe.wait_ge(s["selg"], 4)
            pe.wait_ge(s["y0s"], 8)
            for b in range(NI):
                last = tr(PS[:, 4 + b // CI, tok4(b)], yT[:, b].rearrange("p e k -> p (e k)"), ident)
                if b % CI == CI - 1:
                    last.then_inc(s["yt_ps"], 1)
            pe.wait_ge(s["ybs"], 4)
            for g in range(NC):
                mm(PS[:, g, 0:CT], ident, h1[:, cs(g)], start=True, stop=False, skip_group_check=True)
                for b in range(g * CI, g * CI + CI):
                    last = mm(PS[:, g, tile4(b)], Yb[:, b, :], selG[:, g, tile4(b)], start=False,
                              stop=b % CI == CI - 1, skip_group_check=True)
                last.then_inc(s["h2_ps"], 1)

            for c in range(NC):
                pe.wait_ge(s["h2s"], c + 1)
                centre(2, c, h2)
                if c:
                    variance(2, c - 1)
            variance(2, NC - 1)
            pe.wait_ge(s["xnr"], 12)
            for b in range(NI):
                last = tr(PS[0:T, b // CI, tok4(b)], xn[:, im(b)], ident)
                if b % CI == CI - 1:
                    last.then_inc(s["xs_ps"], 1)
            for b in range(NI):
                last = tr(PS[0:T, 4 + b // CI, tok4(b)], h2[:, im(b)], ident)
                if b % CI == CI - 1:
                    last.then_inc(s["h2t_ps"], 1)
            pe.wait_ge(s["xss"], 4)
            pe.wait_ge(s["toep_in"], 16)
            for h in range(D):
                last = mm(PS[0:T, h // 32, (h % 32) * NI:(h % 32 + 1) * NI], toep[0:T, h, :], xs[:, :, h],
                          start=True, stop=True)
                if h % 32 == 31:
                    last.then_inc(s["cv_ps"], 1)

            pe.wait_ge(s["moe_in"], 16 * 2)
            for b in range(NI):
                if b % CI == 0:
                    pe.wait_ge(s["yn5s"], b // CI + 1)
                    pe.wait_ge(s["yn5a"], b // CI + 1)
                last = tr(PS[:, 4 + b // CI, tile4(b)], yn5[0:T, b, :], ident[0:T, 0:T])
                if b % CI == CI - 1:
                    last.then_inc(s["h5_ps"], 1)
            mm(PS[:, 3, 0:E1], wrT, cbT, start=True, stop=True).then_inc(s["wc_ps"], 1)
            pe.wait_ge(s["h5s"], NC)
            pe.wait_ge(s["wcs"], 1)
            for g in range(NG):
                last = mm(PS[:, 4 + g // 8, (g % 8) * E1:(g % 8 + 1) * E1], h5[:, g * 128:(g + 1) * 128], wc[:, :],
                          start=True, stop=True)
            last.then_inc(s["lg_ps"], 1)
            for k in range(2 * NC):
                if k >= 2:
                    pe.wait_ge(s["s1s"], k - 1)
                mm(PS[:, 6 + k % 2, 0:CT], ws1[:, k % 2:FS:2], h5[:, cs(k // 2)], start=True, stop=True)\
                    .then_inc(s["s1_ps"], 1)
            pe.wait_ge(s["ohss"], 1)
            for g in range(NG):
                r = rows(g)
                last = tr(PS[0:E1, g // 4, (g % 4) * 128:(g % 4) * 128 + r], ohs[0:r, g * E1:(g + 1) * E1], ident[0:r, 0:r])
                if g % 4 == 3 or g == NG - 1:
                    last.then_inc(s["ohs_ps"], 1)
            pe.wait_ge(s["s1s"], 8)
            pe.wait_ge(s["nblks"], 1)
            mm(PS[0:E1, 6, 0:1], cst[0:E1, C_TRI:C_TRI + E1], esm[:, 1:2], start=True, stop=True)
            mm(PS[0:1, 6, 8:9], esm[:, 1:2], vec(V_ONE, E1), start=True, stop=True).then_inc(s["base_ps"], 1)
            pe.wait_ge(s["slts"], 1)
            for g in range(NG):
                last = tr(PS[:, 4 + g // 8, (g % 8) * E1:(g % 8 + 1) * E1], slT[0:E1, g * 128:(g + 1) * 128], ident[0:E1, 0:E1])
            last.then_inc(s["slt_ps"], 1)
            mm(PS[0:1, 6, 16:16 + NCOL], vec(V_E, E1), obk[:, 1, :], start=True, stop=True)
            for c in range(4):
                last = mm(PS[:, 7, c * NCOL:(c + 1) * NCOL], b1all[:, c:F1:4], obk[:, 1, :], start=True, stop=True)
            last.then_inc(s["blk_ps"], 1)
            pe.wait_ge(s["cmbs"], 1)
            pe.wait_ge(s["ohts"], 3)
            for g in range(NG):
                r = rows(g)
                last = tr(PS[0:E1, g // 4, (g % 4) * 128:(g % 4) * 128 + r], cmb[0:r, g, :], ident[0:r, 0:r])
                if g % 4 == 3 or g == NG - 1:
                    last.then_inc(s["cmb_ps"], 1)
            pe.wait_ge(s["cmb_sb"], 3)
            for g in range(NG):
                bank = PS[0:rows(g), g // 4, (g % 4) * 128:(g % 4 + 1) * 128]
                for c in range(2):
                    mm(bank, s1[:, c, gc(g)], ws2[:, c, :], start=c == 0, stop=False)
                last = mm(bank, cmbT[0:E1, gc(g)], b2all[:, :], start=False, stop=True)
                if g % 4 == 3 or g == NG - 1:
                    last.then_inc(s["sh_ps"], 1)
            pe.wait_ge(s["tabs_in"], 1)
            for j in range(NJ):
                r = rows(j % NG)
                last = mm(PS[:, 5, 0:3 * NCOL], ohA[0:r, :, j], ohB[0:r, :, :, j].rearrange("p q i -> p (q i)"),
                          start=j == 0, stop=j == NJ - 1)
            last.then_inc(s["tab_ps"], 1)

            def turn(j):
                tr(PS[:, U + j, 0:CAP], xg[:, j, :], ident).then_inc(s["t_ps"], 1)

            def second(j):
                for c in range(4):
                    last = mm(PS[:, U + j, 128:256], hs[:, j, c * CAP:(c + 1) * CAP], w2r[:, j, c * D:(c + 1) * D],
                              start=c == 0, stop=c == 3)
                last.then_inc(s["y_ps"], 1)

            pe.wait_ge(s["b2s"], 3)
            pe.wait_ge(s["tabs"], 1)
            pe.wait_ge(s["p_io"], 1)
            pe.wait_ge(s["blks"], 2)
            pe_trips = pe.value_load(trips[0:1, 0:1], min_val=1, max_val=NCOL // U - 1)
            pe.wait_ge(s["g_in0"], 16)
            turn(0)

            def pe_body(it, first):
                for j in range(U):
                    nxt, prev = (j + 1) % U, (j - 1) % U
                    pe.wait_ge(s[f"g_in{nxt}"], it * 16 + (16 if j < U - 1 else 32))
                    if not (first and j < 2):
                        pe.wait_ge(s["ysbs"], it * U + (j - 1))
                    turn(nxt)
                    pe.wait_ge(s[f"w1_in{j}"], it * 16 + 16)
                    pe.wait_ge(s["t_sb"], it * U + (j + 1))
                    for c in range(4):
                        last = mm(PS[:, j, c * CAP:(c + 1) * CAP], w1r[:, j, c:F1:4], xsr[:, j, :], start=True, stop=True)
                    last.then_inc(s["h_ps"], 1)
                    pe.wait_ge(s["hss"], it * U + (j + U))
                    if not (first and j == 0):
                        pe.wait_ge(s[f"w2_in{prev}"], it * 16 + (16 if j else 0))
                    second(prev)

            pe_body(0, True)
            with pe.Fori(1, pe_trips) as it:
                pe_body(it, False)
            pe.wait_ge(s["hss"], pe_trips * U + U)
            pe.wait_ge(s[f"w2_in{U - 1}"], pe_trips * 16)
            second(U - 1)

            pe.wait_ge(s["moe2_in"], 32)
            pe.wait_ge(s["ysbs"], pe_trips * U + 1)

            def turn_back(c):
                lo, hi = TAIL[c]
                pe.wait_ge(s["xfs"], c + 1)
                if c >= 2:
                    pe.wait_ge(s["ffs"], c - 1)
                for g in range(lo, hi):
                    r = rows(g)
                    last = tr(PS[:, c % 2, (g - lo) * 128:(g - lo) * 128 + r], xf[0:r, g, :], ident[0:r, 0:r])
                last.then_inc(s["xf_ps"], 1)

            turn_back(0)
            for c, (lo, hi) in enumerate(TAIL):
                cols_c = slice(128 * lo, min(N, 128 * hi))
                pe.wait_ge(s["ffs"], c + 1)
                for f in range(4):
                    if c:
                        pe.wait_ge(s["fss"], 4 * (c - 1) + f + 1)
                    mm(PS[:, 2 + f, 0:cols_c.stop - cols_c.start], wf1[:, f:F1:4], ff[:, cols_c], start=True, stop=True)\
                        .then_inc(s["f1_ps"], 1)
                if c + 1 < len(TAIL):
                    turn_back(c + 1)
                if c >= 2:
                    pe.wait_ge(s["fins"], c - 1)
                for g in range(lo, hi):
                    for f in range(4):
                        if g == lo:
                            pe.wait_ge(s["fss"], 4 * c + f + 1)
                        last = mm(PS[0:rows(g), 6 + c % 2, (g - lo) * 128:(g - lo + 1) * 128], fs[:, f, gc(g)], wf2[:, f, :],
                                  start=f == 0, stop=f == 3)
                last.then_inc(s["f2_ps"], 1)

        @block.scalar
        def _(act):
            act.dma_start(tokw, a["tok_weights"]).then_inc(s["tokw_in"], 16)
            act.dma_start(attw, a["attn_weights"]).then_inc(s["attw_in"], 16)
            act.dma_start(small, a["small"]).then_inc(s["small_in"], 16)
            act.dma_start(ssm, a["ssm"]).then_inc(s["ssm_in"], 16)

            n_link = [0]

            def link(ins):
                n_link[0] += 1
                ins.then_inc(s["a_ch"], 1)
                act.wait_ge(s["a_ch"], n_link[0])

            act.wait_ge(s["eps_in"], 16)
            link(nc.scalar.activation(fabs, feps[:, 0:262], ACT.Abs))
            nc.scalar.activation(fabs, fabs, ACT.Sqrt)
            nc.scalar.activation(fsgn, feps[:, 0:262], ACT.Sign).then_inc(s["feps_f"], 1)
            nc.scalar.preload_act_table_set("natural_log_exp_and_others")
            act.wait_ge(s["small_in"], 16)
            nc.scalar.activation(dt[:, :], col(LDT), ACT.Exp).then_inc(s["mexp"], 1)
            for n in range(2):
                act.wait_ge(s["gmn"], n + 1)
                nc.scalar.activation(emis[:, n * 512:(n + 1) * 512], gmin[:, n * 512:(n + 1) * 512], ACT.Exp)\
                    .then_inc(s["mexp"], 1)
            for n in range(2):
                h = slice(n * 512, (n + 1) * 512)
                act.wait_ge(s["numer"], n + 1)
                link(nc.scalar.activation(emis[:, h], gate[:, h], ACT.Ln, bias=two[:, :]))
                nc.scalar.activation(emis[:, h], emis[:, h], ACT.Exp, scale=-1.0).then_inc(s["mexp"], 1)
            act.wait_ge(s["args"], 2)
            nc.scalar.activation(pE, pAR, ACT.Exp).then_inc(s["trg"], 1)

            def squares(k, c):
                act.wait_ge(s["xc"], 4 * k + c + 1)
                if k:
                    act.wait_ge(s["var"], 4 * k)
                nc.scalar.activation(sq[:, cs(c)], PS[:, LN_XC[k][c], 0:CT], ACT.Square).then_inc(s["sqr"], 1)

            def deviation(k, c):
                act.wait_ge(s["var"], 4 * k + c + 1)
                if k:
                    act.wait_ge(s["xnr"], 4 * k)
                link(nc.scalar.activation(sd[:, cs(c)], PS[:, LN_VAR[k][c], 0:CT], ACT.Ln, bias=vec(V_EPS)))
                nc.scalar.activation(sd[:, cs(c)], sd[:, cs(c)], ACT.Exp, scale=-0.5).then_inc(s["sdv"], 1)

            for c in range(NC):
                squares(0, c)
                if c:
                    deviation(0, c - 1)
            deviation(0, NC - 1)

            nc.scalar.preload_act_table_set("silu_and_others")
            act.wait_ge(s["fracs"], 1)
            link(nc.scalar.activation(pC, pTI, ACT.Abs))
            nc.scalar.activation(pS, pTI, ACT.Sin, scale=TWO_PI).then_inc(s["trg"], 1)
            nc.scalar.activation(pC, pC, ACT.Sin, scale=-TWO_PI, bias=vec(V_HPI)).then_inc(s["trg"], 1)

            def decay(c):
                act.wait_ge(s["pj_ps"], c + 1)
                if c >= 2:
                    act.wait_ge(s["decs"], c - 1)
                nc.scalar.activation(ring4[c % 2][:, TD], PS[:, PJ[c % 2][1], 0:CT], ACT.Tanh, scale=0.5,
                                     bias=col(BDEC)).then_inc(s["tdec"], 1)

            def sincos(c):
                r = ring4[c % 2]
                act.wait_ge(s["frac"], c + 1)
                link(nc.scalar.activation(r[:, AF], r[:, FR], ACT.Abs))
                nc.scalar.activation(r[:, SN], r[:, FR], ACT.Sin, scale=TWO_PI)
                nc.scalar.activation(r[:, CS_], r[:, AF], ACT.Sin, scale=-TWO_PI, bias=vec(V_HPI)).then_inc(s["sc"], 1)

            def residual1(c):
                act.wait_ge(s["out_ps"], c + 1)
                nc.scalar.activation(h1[:, cs(c)], PS[:, PJ[c % 2][0], 0:CT], ACT.Copy).then_inc(s["h1s"], 1)

            act.wait_ge(s["attw"], 1)
            for c in range(NC):
                decay(c)
                sincos(c)
                if c:
                    residual1(c - 1)
            residual1(NC - 1)

            nc.scalar.preload_act_table_set("natural_log_exp_and_others")
            for c in range(NC):
                squares(1, c)
                if c:
                    deviation(1, c - 1)
            deviation(1, NC - 1)

            act.wait_ge(s["smx"], 1)
            nc.scalar.activation(sm[:, 1, :], sm[:, 0, :], ACT.Exp).then_inc(s["smx_e"], 1)
            for g in range(NC):
                act.wait_ge(s["xtm_ps"], g + 1)
                nc.scalar.activation(xtm[0:T, CI * g:CI * g + CI, :],
                                     PS[0:T, g, :].rearrange("p (b d) -> p b d", b=CI), ACT.Copy).then_inc(s["xtms"], 1)
            for g in range(NC):
                act.wait_ge(s["gx_ps"], g + 1)
                nc.scalar.activation(gxs[:, g, :], PS[:, 4 + g, 0:CT], ACT.Copy).then_inc(s["gxc"], 1)
            for g in range(NC):
                act.wait_ge(s["ga_ps"], g + 1)
                nc.scalar.activation(exT[:, :, CI * g:CI * g + CI, :].rearrange("p e b k -> p b e k"),
                                     PS[:, g, :].rearrange("p (b e k) -> p b e k", b=CI, e=E0), ACT.Copy)\
                    .then_inc(s["exts"], 1)
            for e in range(E0):
                act.wait_ge(s["hid_ps"], e + 1)
                if e >= 2:
                    act.wait_ge(s["y0_ps"], e - 1)
                for c in range(2):
                    last = nc.scalar.activation(hid[:, e % 2, c * SL:(c + 1) * SL], PS[:, e % 2, c * SL:(c + 1) * SL],
                                                ACT.Gelu, bias=bT[:, c, e:e + 1])
                last.then_inc(s["gelu"], 1)
            nc.scalar.preload_act_table_set("natural_log_exp_and_others")
            for g in (0, 2):
                act.wait_ge(s["yt_ps"], g + 1)
                nc.scalar.activation(Yb[:, CI * g:CI * g + CI, :], PS[:, 4 + g, :].rearrange("p (b d) -> p b d", b=CI),
                                     ACT.Copy).then_inc(s["ybs"], 1)
            for g in range(NC):
                act.wait_ge(s["h2_ps"], g + 1)
                nc.scalar.activation(h2[:, cs(g)], PS[:, g, 0:CT], ACT.Copy).then_inc(s["h2s"], 1)
                squares(2, g)
                if g:
                    deviation(2, g - 1)
            deviation(2, NC - 1)
            for g in range(NC):
                act.wait_ge(s["xs_ps"], g + 1)
                nc.scalar.activation(xs[:, CI * g:CI * g + CI, :], PS[0:T, g, :].rearrange("p (b d) -> p b d", b=CI),
                                     ACT.Copy).then_inc(s["xss"], 1)
            act.wait_ge(s["st4"], 1)
            link(nc.scalar.activation(lnv[:, 1, :], mv[:, :, 1], ACT.Ln, bias=vec(V_EPS, T)))
            nc.scalar.activation(lnv[:, 2, :], lnv[:, 1, :], ACT.Exp, scale=-0.5).then_inc(s["sdv4"], 1)
            act.wait_ge(s["st4"], 2)
            link(nc.scalar.activation(lnv[:, 1, :], lnv[:, 3, :], ACT.Ln, bias=vec(V_EPS, T)))
            nc.scalar.activation(lnv[:, 5, :], lnv[:, 1, :], ACT.Exp, scale=-0.5).then_inc(s["sdv4"], 1)
            act.wait_ge(s["st4"], 4)
            for c in range(NC):
                for b in (c * CI + 2, c * CI + 3):
                    last = nc.scalar.activation(yn5[0:T, b, :], h3[:, b, :], ACT.Identity, scale=lnv[:, 6, b:b + 1],
                                                bias=lnv[:, 7, b:b + 1])
                last.then_inc(s["yn5a"], 1)
            act.wait_ge(s["h1s"], 4)
            for k in range(2 * NC):
                act.wait_ge(s["s1_ps"], k + 1)
                nc.scalar.activation(s1[:, k % 2, cs(k // 2)], PS[:, 6 + k % 2, 0:CT], ACT.Silu,
                                     bias=bs1[:, k % 2:k % 2 + 1]).then_inc(s["s1s"], 1)
            act.wait_ge(s["w12a"], 1)
            nc.scalar.activation(wk[:, 1, :], wk[:, 0, :], ACT.Tanh, scale=0.5 / 0.7).then_inc(s["w12e"], 1)
            for g in range(3):
                part = slice(512 * g, min(N, 512 * g + 512))
                act.wait_ge(s["ohs_ps"], g + 1)
                nc.scalar.activation(ohT[0:E1, part], PS[0:E1, g, 0:part.stop - part.start], ACT.Copy).then_inc(s["ohts"], 1)
            act.wait_ge(s["blk_ps"], 1)
            nc.scalar.activation(b1blk[:, :, :].rearrange("p c i -> p (c i)"), PS[:, 7, 0:4 * NCOL], ACT.Copy)
            nc.scalar.activation(bexp[:, :], PS[0:1, 6, 16:16 + NCOL], ACT.Copy).then_inc(s["blks"], 1)
            for g in range(3):
                part = slice(512 * g, min(N, 512 * g + 512))
                act.wait_ge(s["cmb_ps"], g + 1)
                nc.scalar.activation(cmbT[0:E1, part], PS[0:E1, g, 0:part.stop - part.start], ACT.Copy).then_inc(s["cmb_sb"], 1)

            act.wait_ge(s["blks"], 2)
            act_trips = act.value_load(trips[0:1, 0:1], min_val=1, max_val=NCOL // U - 1)
            act.wait_ge(s["p_io"], 1)

            act.wait_ge(s["y_clear"], 16)
            y_blocks = yrow_dram.rearrange("(n p) d -> n p d", p=CAP)

            def leave(j, seen, at):
                act.wait_ge(s["y_ps"], seen)
                nc.scalar.activation(ysb[:, j, :], PS[:, U + j, 128:256], ACT.Copy).then_inc(s["ysbs"], 1)
                act.wait_ge(s["ysbs"], seen)
                act.dma_start(y_blocks[bass.ds(at, 1)].rearrange("o p d -> (o p) d"), ysb[:, j, :])\
                    .then_inc(s[f"yr_out{j}"], 16)

            def act_body(it, first):
                for j in range(U):
                    act.wait_ge(s["hps"], it * U + (j + 1))
                    nc.scalar.activation(hs[:, j, :], hpre[:, j, :], ACT.Silu).then_inc(s["hss"], 1)
                    if not first:
                        act.wait_ge(s[f"yr_out{(j - 1) % U}"], it * 16)
                    leave((j - 1) % U, it * U + (j + 1), it * U + j)

            act_body(0, True)
            with act.Fori(1, act_trips) as it:
                act_body(it, False)
            act.wait_ge(s[f"yr_out{U - 1}"], act_trips * 16)
            leave(U - 1, act_trips * U + 1, act_trips * U)

            for c, (lo, hi) in enumerate(TAIL):
                cols_c = slice(128 * lo, min(N, 128 * hi))
                for f in range(4):
                    act.wait_ge(s["f1_ps"], 4 * c + f + 1)
                    nc.scalar.activation(fs[:, f, cols_c], PS[:, 2 + f, 0:cols_c.stop - cols_c.start], ACT.Silu,
                                         bias=bf1[:, f:f + 1]).then_inc(s["fss"], 1)

        @block.vector
        def _(dve):
            v = nc.vector
            n_link = [0]

            def link(ins):
                n_link[0] += 1
                ins.then_inc(s["d_ch"], 1)
                dve.wait_ge(s["d_ch"], n_link[0])

            v.memset(kpad[:, 0:T - 1], 0.0)
            link(v.memset(mask[:, :, :], 1.0))
            link(v.memset(mask[:, :, 0:1], 0.0))
            v.memset(two[:, :], 2.0)
            dve.wait_ge(s["feps_f"], 1)
            link(v.tensor_tensor(feps[:, 0:262], fabs, fsgn, ALU.mult))
            v.tensor_tensor(feps[:, 264:266], feps[:, 264:266], feps[:, 260:262], ALU.mult)
            dve.wait_ge(s["tokw_in"], 16)
            sw = tokw[:, 4:8, :].rearrange("p (k h) o -> p k h o", k=2)
            eps_out = feps[:, 4:260].rearrange("p (k o) -> p k o", k=2)
            link(v.tensor_tensor(sw, sw, spread(eps_out, 2, 2), ALU.mult))
            for q in range(4):
                last = v.scalar_tensor_tensor(tokw[:, q, :], tokw[:, 4 + q, :], feps[:, q:q + 1], tokw[:, q, :],
                                              ALU.mult, ALU.add)
            last.then_inc(s["wn"], 1)
            link(v.tensor_tensor(bcol[:, :], feps[:, 262:264], feps[:, 264:266], ALU.add))

            hf = [slice(0, 512), slice(512, 1024)]
            for n in range(2):
                dve.wait_ge(s["gi_ps"], n + 1)
                v.tensor_scalar(gmin[:, hf[n]], PS[:, 4 + 2 * n, :], bcol[:, 0:1], 20.0, ALU.add, ALU.min)\
                    .then_inc(s["gmn"], 1)
            for n in range(2):
                h = hf[n]
                dve.wait_ge(s["mexp"], n + 2)
                v.scalar_tensor_tensor(gate[:, h], emis[:, h], 2.0, emis[:, h], ALU.add, ALU.mult).then_inc(s["numer"], 1)
            dve.wait_ge(s["small_in"], 16)
            dve.wait_ge(s["attw_in"], 16)
            dve.wait_ge(s["ssm_in"], 16)
            dve.wait_ge(s["mexp"], 1)
            v.tensor_scalar(q64[:, 0, :], lam[:, 0, :], dt[:, :], None, ALU.mult)
            v.tensor_scalar(q64[:, 1, :], lam[:, 1, :], dt[:, :], 1.0 / (2.0 * math.pi), ALU.mult, ALU.mult)\
                .then_inc(s["dtl"], 1)
            dve.wait_ge(s["cst_in"], 16)
            v.tensor_scalar(winsw[:, 64:128], winsw[:, 64:128], -1.0, None, ALU.mult)
            v.tensor_scalar(col(BANG), col(BANG), 1.0 / (2.0 * math.pi), None, ALU.mult)
            v.tensor_scalar(col(BDEC), col(BDEC), 0.5, None, ALU.mult)
            v.tensor_tensor(col(BISW), col(BISW), vec(V_SGN), ALU.mult).then_inc(s["attw"], 1)
            v.tensor_scalar(peb[:, :], cst[:, C_PE:C_PE + L], col(B3), None, ALU.add)
            h0v = h0.rearrange("p (b t) -> p b t", b=NI)
            link(v.tensor_copy(h0v[:, :, 0], col(CLS).to_broadcast([128, NI])))
            for n in range(2):
                h = hf[n]
                dve.wait_ge(s["mexp"], n + 4)
                link(v.tensor_tensor(gate[:, h], gate[:, h], emis[:, h], ALU.mult))
                link(v.scalar_tensor_tensor(gate[:, h], PS[:, 4 + 2 * n, :], bcol[:, 0:1], gate[:, h], ALU.add, ALU.mult))
                v.scalar_tensor_tensor(gate[:, h], PS[:, 5 + 2 * n, :], bcol[:, 1:2], gate[:, h], ALU.add, ALU.mult)\
                    .then_inc(s["gated"], 1)
            for n in range(2):
                dve.wait_ge(s["tok_ps"], n + 1)
                v.tensor_tensor(h0v[:, 8 * n:8 * n + 8, 1:T], PS[:, n, :].rearrange("p (b l) -> p b l", b=8),
                                spread(peb[:, :], 1, 8), ALU.add).then_inc(s["h0s"], 1)

            dve.wait_ge(s["args"], 2)
            link(v.tensor_scalar(pS, pTI, MAGIC, -MAGIC, ALU.add, ALU.add))
            v.tensor_tensor(pTI, pTI, pS, ALU.subtract).then_inc(s["fracs"], 1)

            def normalise(k, c):
                dve.wait_ge(s["sdv"], 4 * k + c + 1)
                dst, xc, rec = xn[:, cs(c)], PS[:, LN_XC[k][c], 0:CT], sd[:, cs(c)]
                if k == 2:
                    dst, xc, rec = [z.rearrange("p (b t) -> p b t", b=CI) for z in (dst, xc, rec)]
                    dst = dst[:, :, ::-1]
                v.tensor_tensor(dst, xc, rec, ALU.mult).then_inc(s["xnr"], 1)

            for c in range(NC):
                normalise(0, c)

            flat_mask = mask[:, :, :].rearrange("p a b -> p (a b)")

            def phases(c):
                r = ring4[c % 2]
                dve.wait_ge(s["pj_ps"], c + 1)
                if c >= 2:
                    dve.wait_ge(s["out_ps"], c - 1)
                link(v.tensor_scalar(r[:, AN], PS[:, PJ[c % 2][0], 0:CT], 1.0 / (2.0 * math.pi), col(BANG), ALU.mult, ALU.add))
                link(v.tensor_tensor_scan(r[:, TH], flat_mask, r[:, AN], 0.0, ALU.mult, ALU.add))
                link(v.tensor_scalar(r[:, RM], r[:, TH], MAGIC, -MAGIC, ALU.add, ALU.add))
                v.tensor_tensor(r[:, FR], r[:, TH], r[:, RM], ALU.subtract).then_inc(s["frac"], 1)

            def recur(c):
                r = ring4[c % 2]
                dve.wait_ge(s["sc"], c + 1)
                v.scalar_tensor_tensor(r[:, CU], PS[:, PJ[c % 2][2], 0:CT], col(BI), r[:, CS_], ALU.add, ALU.mult)
                link(v.scalar_tensor_tensor(r[:, SU], PS[:, PJ[c % 2][3], 0:CT], col(BISW), r[:, SN], ALU.add, ALU.mult))
                link(v.tensor_tensor(r[:, GI], r[:, CU], r[:, SU], ALU.add))
                dve.wait_ge(s["decs"], c + 1)
                link(v.tensor_tensor_scan(r[:, GS], r[:, DEC], r[:, GI], 0.0, ALU.mult, ALU.add))
                v.tensor_tensor(r[:, RM], r[:, CS_], r[:, GS], ALU.mult)
                v.tensor_tensor(r[:, AN], r[:, SN], r[:, GS], ALU.mult).then_inc(s["rot"], 1)

            phases(0)
            phases(1)
            recur(0)
            phases(2)
            recur(1)
            phases(3)
            recur(2)
            recur(3)

            def q(k):
                return q64[:, k, :]

            def tt(o, x, y, op):
                link(v.tensor_tensor(o, x, y, op))

            dve.wait_ge(s["vv"], 1)
            v1r, v1i = VV[:, 1, 0, :], VV[:, 1, 1, :]
            v.tensor_scalar(q(0), v1r, -1.0, None, ALU.add)
            link(v.tensor_scalar(q(2), lam[:, 0, :], 1e-8, None, ALU.add))
            tt(q(3), q(2), q(2), ALU.mult)
            tt(q(4), lam[:, 1, :], lam[:, 1, :], ALU.mult)
            tt(q(3), q(3), q(4), ALU.add)
            link(v.reciprocal(q(3), q(3)))
            tt(q(4), q(0), q(2), ALU.mult)
            tt(q(5), v1i, lam[:, 1, :], ALU.mult)
            tt(q(4), q(4), q(5), ALU.add)
            tt(q(4), q(4), q(3), ALU.mult)
            tt(q(5), v1i, q(2), ALU.mult)
            tt(q(6), q(0), lam[:, 1, :], ALU.mult)
            tt(q(5), q(5), q(6), ALU.subtract)
            tt(q(5), q(5), q(3), ALU.mult)

            def cmul(re, im_, ar, ai, br, bi, t):
                tt(t, ai, bi, ALU.mult)
                tt(re, ar, br, ALU.mult)
                tt(re, re, t, ALU.subtract)
                tt(t, ar, bi, ALU.mult)
                tt(im_, ai, br, ALU.mult)
                tt(im_, im_, t, ALU.add)

            cmul(q(6), q(7), bc4[:, 0, :], bc4[:, 1, :], q(4), q(5), q(10))
            cmul(q(8), q(9), bc4[:, 2, :], bc4[:, 3, :], q(6), q(7), q(10))
            v.tensor_scalar(q(10), q(8), -1.0, None, ALU.mult).then_inc(s["qrec"], 1)

            for c in range(NC):
                normalise(1, c)

            dve.wait_ge(s["lg0_ps"], 1)
            lg0 = PS[0:T, 4, 0:128].rearrange("p (b e) -> p b e", b=NI)
            smv = [sm[:, k, :].rearrange("p (b e) -> p b e", b=NI) for k in range(3)]
            link(v.tensor_reduce(smr[:, 0, :], lg0, AX, ALU.max))
            v.tensor_tensor(smv[0], lg0, spread(smr[:, 0, :], 2, E0), ALU.subtract).then_inc(s["smx"], 1)
            dve.wait_ge(s["smx_e"], 1)
            link(v.tensor_reduce(smr[:, 1, :], smv[1], AX, ALU.add))
            link(v.reciprocal(smr[:, 1, :], smr[:, 1, :]))
            v.tensor_tensor(smv[2], smv[1], spread(smr[:, 1, :], 2, E0), ALU.mult).then_inc(s["sms"], 1)
            dve.wait_ge(s["st_ps"], 1)
            link(v.tensor_copy(rt0[:, 0, :], PS[:, 5, 0:T]))
            link(v.max(top8[:, 0, :], rt0[:, 0, :]))
            link(v.match_replace(rt0[:, 1, :], top8[:, 0, :], rt0[:, 0, :], -1.0))
            link(v.max(top8[:, 1, :], rt0[:, 1, :]))
            link(v.match_replace(rt0[:, 2, :], top8[:, 1, :], rt0[:, 1, :], -1.0))
            link(v.tensor_scalar(rt0[:, 3, :], rt0[:, 2, :], 0.0, None, ALU.is_lt))
            link(v.tensor_tensor_scan(rt0[:, 4, :], rt0[:, 3, :], rt0[:, 3, :], 0.0, ALU.add, ALU.max))
            v.tensor_tensor(rt0[:, 5, :], rt0[:, 4, :], rt0[:, 3, :], ALU.mult)
            v.tensor_tensor(rt0[:, 1, :], rt0[:, 0, :], rt0[:, 3, :], ALU.mult).then_inc(s["route0"], 1)
            dve.wait_ge(s["pt_ps"], 1)
            v.tensor_tensor(sel[0:T], spread(PS[0:T, 0, 0:128], 2, K0),
                            spread(cst[0:T, C_K16:C_K16 + K0], 1, 128), ALU.is_equal).then_inc(s["sels"], 1)
            for g in range(NC):
                dve.wait_ge(s["px_ps"], g + 1)
                v.scalar_tensor_tensor(selG[:, g, :], PS[:, 4 + g, 0:CT], vec(V_SLOT), gxs[:, g, :], ALU.is_equal, ALU.mult)\
                    .then_inc(s["selg"], 1)
            dve.wait_ge(s["prods"], 1)
            link(v.tensor_reduce(kpad[:, T - 1:2 * T - 1], prod, AX, ALU.add))
            v.tensor_tensor(kpad[:, T - 1:T], kpad[:, T - 1:T], col(DD), ALU.add).then_inc(s["kpads"], 1)
            for e in range(E0):
                dve.wait_ge(s["y0_ps"], e + 1)
                v.tensor_scalar(yT[:, :, e, :], PS[:, 2 + e % 2, 0:SL].rearrange("p (b k) -> p b k", b=NI),
                                bT[:, 2, e:e + 1], None, ALU.add).then_inc(s["y0s"], 1)
            for g in (1, 3):
                dve.wait_ge(s["yt_ps"], g + 1)
                v.tensor_copy(Yb[:, CI * g:CI * g + CI, :], PS[:, 4 + g, :].rearrange("p (b d) -> p b d", b=CI))\
                    .then_inc(s["ybs"], 1)
            for c in range(NC):
                normalise(2, c)
            for g in range(NC):
                dve.wait_ge(s["h2t_ps"], g + 1)
                link(v.tensor_copy(h2t[:, CI * g:CI * g + CI, :], PS[0:T, 4 + g, :].rearrange("p (b d) -> p b d", b=CI)))
            for g in range(NC):
                dve.wait_ge(s["cv_ps"], g + 1)
                v.tensor_tensor(h3[:, :, 32 * g:32 * g + 32], PS[0:T, g, :].rearrange("p (h b) -> p b h", b=NI),
                                h2t[:, :, 32 * g:32 * g + 32], ALU.add).then_inc(s["h3s"], 1)
            dve.wait_ge(s["h3s"], 4)

            for b in range(NI):
                last = v.bn_stats(lnst[:, b, :], h3[:, b, :])
            link(last)
            for b in range(NI):
                last = v.bn_aggr(mv[:, b, :], lnst[:, b, :])
            last.then_inc(s["st4"], 1)
            dve.wait_ge(s["sdv4"], 1)
            link(v.tensor_tensor(lnv[:, 3, :], lnv[:, 2, :], lnv[:, 2, :], ALU.mult))
            v.tensor_tensor(lnv[:, 3, :], lnv[:, 3, :], mv[:, :, 1], ALU.mult).then_inc(s["st4"], 1)
            v.tensor_scalar(lnv[:, 0, :], lnv[:, 2, :], 1.0, None, ALU.add)
            v.scalar_tensor_tensor(lnv[:, 4, :], mv[:, :, 0], -1.0, lnv[:, 2, :], ALU.mult, ALU.mult).then_inc(s["st4"], 1)
            dve.wait_ge(s["sdv4"], 2)
            link(v.tensor_tensor(lnv[:, 6, :], lnv[:, 5, :], lnv[:, 2, :], ALU.mult))
            v.scalar_tensor_tensor(lnv[:, 7, :], mv[:, :, 0], -1.0, lnv[:, 6, :], ALU.mult, ALU.mult).then_inc(s["st4"], 1)
            for c in range(NC):
                for b in (c * CI, c * CI + 1):
                    last = v.tensor_scalar(yn5[0:T, b, :], h3[:, b, :], mv[:, b, 0:1], lnv[:, 6, b:b + 1], ALU.subtract, ALU.mult)
                last.then_inc(s["yn5s"], 1)
            dve.wait_ge(s["moe_in"], 16 * 2)
            v.memset(h5[:, N:NP], 0.0)
            v.memset(slT[0:E1, N:NP], 0.0)
            for c in range(NC):
                dve.wait_ge(s["h5_ps"], c + 1)
                v.tensor_scalar(h5[:, cs(c)], PS[:, 4 + c, 0:CT], col(G1), col(B1), ALU.mult, ALU.add).then_inc(s["h5s"], 1)
            dve.wait_ge(s["wc_ps"], 1)
            v.tensor_copy(wc[:, :], PS[:, 3, 0:E1]).then_inc(s["wcs"], 1)
            v.tensor_scalar(ws2, ws2, 0.25, None, ALU.mult)
            link(v.tensor_scalar(bs2, bs2, 0.25, None, ALU.mult))
            dve.wait_ge(s["lg_ps"], 1)

            def scores(b):
                return PS[:, 4 + b // 8, (b % 8) * E1:(b % 8 + 1) * E1]

            for b in range(NG):
                last = v.max(mx8[:, b, :], scores(b))
            link(last)
            for b in range(NG):
                last = v.max_index(ix8[:, b, :], mx8[:, b, :], scores(b))
            link(last)
            v.tensor_tensor(wk[:, 0, :], mx8[:, :, 1], mx8[:, :, 0], ALU.subtract).then_inc(s["w12a"], 1)
            link(v.tensor_copy(ef[:, :, :].rearrange("p k b -> p b k"), ix8[:, :, 0:2]))
            for k in range(2):
                last = v.tensor_tensor(oh[:, k, :].rearrange("p (g e) -> p g e", g=NG), spread(cst[:, C_IOTA:C_IOTA + E1], 1, NG),
                                       spread(ef[:, k, :], 2, E1), ALU.is_equal)
            link(last)
            v.tensor_tensor(ohs, oh[:, 0, :], oh[:, 1, :], ALU.add).then_inc(s["ohss"], 1)
            dve.wait_ge(s["w12e"], 1)
            v.tensor_scalar(wts[:, 0, :], wk[:, 1, :], -0.5, 0.5, ALU.mult, ALU.add)
            v.tensor_scalar(wts[:, 1, :], wk[:, 1, :], 0.5, 0.5, ALU.mult, ALU.add).then_inc(s["w12"], 1)
            dve.wait_ge(s["ohts"], 3)
            link(v.tensor_tensor_scan(inc[0:E1, :], ohT[0:E1, :], ohT[0:E1, :], 0.0, ALU.add, ALU.max))
            cnt = inc[0:E1, N - 1:N]
            link(v.tensor_scalar(esm[:, 0:1], cnt, 1.0 / CAP, (CAP - 1.0) / CAP - 0.498, ALU.mult, ALU.add))
            v.tensor_scalar(esm[:, 1:2], esm[:, 0:1], MAGIC, -MAGIC, ALU.add, ALU.add).then_inc(s["nblks"], 1)
            dve.wait_ge(s["base_ps"], 1)
            v.tensor_scalar(esm[:, 3:4], PS[0:E1, 6, 0:1], float(CAP), -1.0, ALU.mult, ALU.add)
            v.tensor_scalar(esm[0:1, 6:7], PS[0:1, 6, 8:9], 1.0 / U, (U - 1.0) / U - 0.4, ALU.mult, ALU.add)
            v.tensor_tensor(esm[:, 4:5], PS[0:E1, 6, 0:1], esm[:, 1:2], ALU.add)
            link(v.tensor_copy(esm[:, 2:3], PS[0:E1, 6, 0:1]))
            v.tensor_scalar(trips[:, :], esm[0:1, 6:7], MAGIC, -MAGIC, ALU.add, ALU.add).then_inc(s["blks"], 1)
            link(v.tensor_scalar(obk[:, 0, :], cst[0:E1, C_IOTA:C_IOTA + NCOL], esm[:, 4:5], None, ALU.is_lt))
            v.scalar_tensor_tensor(obk[:, 1, :], cst[0:E1, C_IOTA:C_IOTA + NCOL], esm[:, 2:3], obk[:, 0, :], ALU.is_ge, ALU.mult)
            v.tensor_scalar(slT[0:E1, 0:N], inc[0:E1, :], esm[:, 3:4], None, ALU.add).then_inc(s["slts"], 1)
            dve.wait_ge(s["slt_ps"], 1)
            slt = PS[:, 4:6, :].rearrange("p a b -> p (a b)")[:, 0:NG * E1]
            for k in range(2):
                last = v.tensor_tensor(sprod[:, k, :], oh[:, k, :], slt, ALU.mult)
            link(last)
            link(v.tensor_reduce(slot[:, 0, :], sprod.rearrange("p k (b e) -> p (k b) e", e=E1), AX, ALU.add))
            v.tensor_scalar(yix[:, :], slot[:, 0, :], float(CAP), None, ALU.add)
            link(v.tensor_scalar(slot[:, 1, :], slot[:, 0, :], 1.0 / CAP, -0.498, ALU.mult, ALU.add))
            link(v.tensor_scalar(slot[:, 2, :], slot[:, 1, :], MAGIC, -MAGIC, ALU.add, ALU.add))
            v.tensor_copy(slotb[:, 1, :], slot[:, 2, :])
            link(v.scalar_tensor_tensor(slotb[:, 0, :], slot[:, 2, :], -float(CAP), slot[:, 0, :], ALU.mult, ALU.add))
            dve.wait_ge(s["iots"], 2)
            v.tensor_tensor(ohA, iotb, spread(slotb[:, 0, :], 1, CAP), ALU.is_equal)
            link(v.tensor_tensor(ohB[:, 0], iotb[:, 0:NCOL, :], spread(slotb[:, 1, :], 1, NCOL), ALU.is_equal))
            v.tensor_scalar(ohB[:, 1], ohB[:, 0], vec(V_T), None, ALU.mult)
            v.tensor_tensor(ohB[:, 2], ohB[:, 0], spread(cvb[:, :], 1, NCOL), ALU.mult).then_inc(s["tabs_in"], 1)
            dve.wait_ge(s["tab_ps"], 1)
            link(v.tensor_copy(tabf[:, 0:3, :].rearrange("p a b -> p (a b)"), PS[:, 5, 0:3 * NCOL]))
            v.scalar_tensor_tensor(tabf[:, 3, :], tabf[:, 2, :], 128.0, tabf[:, 1, :], ALU.mult, ALU.add)
            link(v.tensor_scalar(tabf[:, 4, :], tabf[:, 0, :], -BIG, BIG, ALU.mult, ALU.add))
            v.tensor_tensor(tabx[:, :], tabf[:, 3, :], tabf[:, 4, :], ALU.add).then_inc(s["tabs"], 1)
            dve.wait_ge(s["x_out"], 16)
            for g in range(3):
                lo, hi = 4 * g, min(4 * g + 4, NG)
                r = rows(hi - 1)
                dve.wait_ge(s["sh_ps"], g + 1)
                v.tensor_tensor(base2[0:r, lo:hi, :], PS[0:r, g, 0:(hi - lo) * D].rearrange("p (b d) -> p b d", d=D),
                                spread(bs2[0:r, :], 1, hi - lo), ALU.add).then_inc(s["b2s"], 1)

            dve.wait_ge(s["blks"], 2)
            dve_trips = dve.value_load(trips[0:1, 0:1], min_val=1, max_val=NCOL // U - 1)
            dve.wait_ge(s["p_io"], 1)

            def tokens(j, seen):
                dve.wait_ge(s["t_ps"], seen)
                v.tensor_scalar(xsr[:, j, :], PS[:, U + j, 0:CAP], col(G1), col(B1), ALU.mult, ALU.add).then_inc(s["t_sb"], 1)

            tokens(0, 1)
            with dve.Fori(0, dve_trips) as it:
                for j in range(U):
                    tokens((j + 1) % U, it * U + (j + 2))
                    dve.wait_ge(s["hss"], it * U + (j + 1))
                    dve.wait_ge(s["h_ps"], it * U + (j + 1))
                    bias = b1blk[:, :, bass.ds(it * U + j, 1)].to_broadcast([128, 4, CAP])
                    v.tensor_tensor(hpre[:, j, :].rearrange("p (c q) -> p c q", c=4),
                                    PS[:, j, :].rearrange("p (c q) -> p c q", c=4), bias, ALU.add).then_inc(s["hps"], 1)

            dve.wait_ge(s["rr_in"], 32)
            link(v.tensor_tensor(resg[:, 0:NG - 1, :], resg[:, 0:NG - 1, :], spread(bf2[:, :], 1, NG - 1), ALU.add))
            v.tensor_tensor(resg[0:rows(NG - 1), NG - 1, :], resg[0:rows(NG - 1), NG - 1, :], bf2[0:rows(NG - 1), :],
                            ALU.add).then_inc(s["resb"], 1)
            dve.wait_ge(s["w12"], 1)
            dve.wait_ge(s["b2s"], 3)

            def combine(c):
                lo, hi = TAIL[c]
                r = rows(hi - 1)
                dve.wait_ge(s[f"yl_in{c}"], 32 * (hi - lo))
                for k in range(2):
                    for g in range(lo, hi):
                        last = v.scalar_tensor_tensor(base2[0:r, g, :], yl[0:r, k * NG + g, :], wts[0:r, k, g:g + 1],
                                                      base2[0:r, g, :], ALU.mult, ALU.add)
                    if k == 0:
                        link(last)
                last.then_inc(s["hms"], 1)
                dve.wait_ge(s["hms"], c + 1)
                for g in range(lo, hi):
                    last = v.bn_stats(st6[0:r, g, :], base2[0:r, g, :])
                link(last)
                for g in range(lo, hi):
                    last = v.bn_aggr(mv6[0:r, g, :], st6[0:r, g, :])
                link(last)
                ve, half, y, w = [nw[0:r, k, lo:hi] for k in range(4)]
                link(v.tensor_scalar(ve, mv6[0:r, lo:hi, 1], EPS, None, ALU.add))
                v.tensor_scalar(half, ve, -0.5, None, ALU.mult)
                link(v.tensor_copy(w, ve.bitcast(I32)))
                link(v.tensor_scalar(nwi[0:r, lo:hi], w, -0.5, SQRT_GUESS, ALU.mult, ALU.add))
                guess = nwi[0:r, lo:hi].bitcast(F32)
                for k in range(4):
                    z = guess if k == 0 else y
                    link(v.tensor_tensor(w, z, z, ALU.mult))
                    link(v.tensor_tensor(w, w, half, ALU.mult))
                    link(v.scalar_tensor_tensor(y, w, 1.5, z, ALU.add, ALU.mult))
                for g in range(lo, hi):
                    last = v.tensor_scalar(xf[0:r, g, :], base2[0:r, g, :], mv6[0:r, g, 0:1], nw[0:r, 2, g:g + 1],
                                           ALU.subtract, ALU.mult)
                last.then_inc(s["xfs"], 1)

            def rescale(c):
                lo, hi = TAIL[c]
                cols_c = slice(128 * lo, min(N, 128 * hi))
                dve.wait_ge(s["xf_ps"], c + 1)
                v.tensor_scalar(ff[:, cols_c], PS[:, c % 2, 0:cols_c.stop - cols_c.start], col(GF), col(BF), ALU.mult, ALU.add)\
                    .then_inc(s["ffs"], 1)

            def finish(c):
                lo, hi = TAIL[c]
                r = rows(hi - 1)
                dve.wait_ge(s["f2_ps"], c + 1)
                dve.wait_ge(s["res"], c + 2)
                v.tensor_tensor(resg[0:r, lo:hi, :], PS[0:r, 6 + c % 2, 0:(hi - lo) * D].rearrange("p (b d) -> p b d", d=D),
                                resg[0:r, lo:hi, :], ALU.add).then_inc(s["fins"], 1)

            for c in range(len(TAIL)):
                combine(c)
                rescale(c)
                if c >= 2:
                    finish(c - 2)
            finish(len(TAIL) - 2)
            finish(len(TAIL) - 1)

        @block.gpsimd
        def _(pool):
            p = nc.gpsimd
            n_link = [0]

            def link(ins):
                n_link[0] += 1
                ins.then_inc(s["p_ch"], 1)
                pool.wait_ge(s["p_ch"], n_link[0])

            p.memset(zeros[:, :], 0.0).then_inc(s["zero"], 1)
            pool.wait_ge(s["cst_in"], 16)
            pool.wait_ge(s["dtl"], 1)
            powers = spread(cst[:, C_PWR:C_PWR + NPW], 2, NS)
            for k, dst in enumerate((pAR, pTI)):
                p.tensor_tensor(dst, powers, spread(q64[:, k, :], 1, NPW), ALU.mult).then_inc(s["args"], 1)
            pool.wait_ge(s["trg"], 3)
            p.tensor_tensor(VV[:, :, 0, :], pE, pC, ALU.mult)
            p.tensor_tensor(VV[:, :, 1, :], pE, pS, ALU.mult).then_inc(s["vv"], 1)

            def decays(c):
                r = ring4[c % 2]
                if c < 2:
                    link(p.memset(r[:, DEC], 0.0))
                else:
                    pool.wait_ge(s["rot"], c - 1)
                pool.wait_ge(s["tdec"], c + 1)
                td = r[:, TD].rearrange("p (b t) -> p b t", b=CI)[:, :, 1:T]
                de = r[:, DEC].rearrange("p (b t) -> p b t", b=CI)[:, :, 1:T]
                p.tensor_scalar(de, td, 0.5, 0.5, ALU.mult, ALU.add).then_inc(s["decs"], 1)

            for c in range(NC):
                decays(c)

            pool.wait_ge(s["vv"], 1)
            pool.wait_ge(s["qrec"], 1)
            va = [VV[:, PB:NPW, k, :] for k in range(2)]
            t0, t1 = pE[:, 0:PA, :], pS[:, 0:PA, :]

            def fac(k):
                return spread(q64[:, k, :], 1, PA)

            p.tensor_tensor(t0, va[0], fac(8), ALU.mult)
            link(p.tensor_tensor(t1, va[1], fac(9), ALU.mult))
            link(p.tensor_tensor(UU[:, :, 0, :], t0, t1, ALU.subtract))
            p.tensor_tensor(t0, va[1], fac(10), ALU.mult)
            link(p.tensor_tensor(t1, va[0], fac(9), ALU.mult))
            link(p.tensor_tensor(UU[:, :, 1, :], t0, t1, ALU.subtract))
            uf = UU.rearrange("p a c n -> p a (c n)")
            vf = VV.rearrange("p a c n -> p a (c n)")
            for q in range(PA - 1):
                p.tensor_tensor(prod[:, PB * q:PB * q + PB, :], spread(uf[:, q, :], 1, PB), vf[:, 0:PB, :], ALU.mult)
            p.tensor_tensor(prod[:, T - 1, :], uf[:, PA - 1, :], vf[:, 0, :], ALU.mult).then_inc(s["prods"], 1)

            pool.wait_ge(s["cv_ps"], 4)
            p.iota(iotb, [[1, CAP], [0, NJ]], base=0, channel_multiplier=0, allow_small_or_imprecise_dtypes=True)\
                .then_inc(s["iots"], 1)
            p.iota(cvb[:, :].rearrange("p (k g) -> p k g", k=2), [[0, 2], [1, NG]], base=0, channel_multiplier=0, allow_small_or_imprecise_dtypes=True)\
                .then_inc(s["iots"], 1)
            pool.wait_ge(s["st4"], 3)
            for b in range(NI):
                last = p.tensor_scalar(hres[:, b, :], h3[:, b, :], lnv[:, 0, b:b + 1], lnv[:, 4, b:b + 1], ALU.mult, ALU.add)
            last.then_inc(s["res"], 1)
            pool.wait_ge(s["w12"], 1)
            ohv = [oh[:, k, :].rearrange("p (b e) -> p b e", b=NG) for k in range(2)]
            tmp = carve(h2, [[NG, E1]])[0]
            p.tensor_tensor(cmb, ohv[0], spread(wts[:, 0, :], 2, E1), ALU.mult)
            link(p.tensor_tensor(tmp, ohv[1], spread(wts[:, 1, :], 2, E1), ALU.mult))
            p.tensor_tensor(cmb, cmb, tmp, ALU.add).then_inc(s["cmbs"], 1)
            p.memset(xg, 0.0)
            p.memset(hs[:, U - 1, :], 0.0).then_inc(s["hss"], U)
            p.memset(w2r[:, U - 1, :], 0.0).then_inc(s["p_io"], 1)

            pool.wait_ge(s["blks"], 2)
            pool_trips = pool.value_load(trips[0:1, 0:1], min_val=1, max_val=NCOL // U - 1)
            last_x = pool.to_reg(N - 1)
            last_y = pool.to_reg(NOUT * CAP - 1)
            pool.wait_ge(s["tabs"], 1)
            pool.wait_ge(s["x_out"], 16)
            pool.wait_ge(s["p_io"], 1)

            def gather(j):
                pool.indirect_dma_start(out=xg[:, j, :], out_offset=None, in_=xrow_dram,
                                        in_offset=bass.IndirectOffsetOnAxis(ap=ixg[:, j:j + 1], axis=0),
                                        bounds_check=last_x, oob_is_err=False).then_inc(s[f"g_in{j}"], 16)

            p.tensor_copy(ixg[:, 0:U - 1], tabx[:, 0:U - 1]).then_inc(s["ix_cp"], 1)
            pool.wait_ge(s["ix_cp"], 1)
            for j in range(U - 1):
                gather(j)

            def pool_body(it, first):
                for j in range(U):
                    far = (j + U - 1) % U
                    if not (first and j == 0):
                        pool.wait_ge(s["t_ps"], it * U + j)
                        pool.sem_inc(s["p_rd"], 1)
                    p.tensor_copy(ixg[:, far:far + 1], tabx[:, bass.ds(it * U + (j + U - 1), 1)]).then_inc(s["ix_cp"], 1)
                    pool.wait_ge(s["ix_cp"], it * U + (j + 2))
                    pool.sem_inc(s["p_rd"], 1)
                    gather(far)

            pool_body(0, True)
            with pool.Fori(1, pool_trips) as it:
                pool_body(it, False)
            for j in range(U):
                pool.wait_ge(s[f"yr_out{j}"], pool_trips * 16 + (16 if j == U - 1 else 0))
                pool.sem_inc(s["p_rd"], 1)
            for c, (lo, hi) in enumerate(TAIL):
                for g in range(lo, hi):
                    for q in (g, NG + g):
                        r = rows(g)
                        pool.indirect_dma_start(out=yl[0:r, q, :], out_offset=None, in_=yrow_dram,
                                                in_offset=bass.IndirectOffsetOnAxis(ap=yix[0:r, q:q + 1], axis=0),
                                                bounds_check=last_y, oob_is_err=False).then_inc(s[f"yl_in{c}"], 16)
            pool.wait_ge(s["resb"], 1)
            for c, (lo, hi) in enumerate(TAIL):
                r = rows(hi - 1)
                pool.wait_ge(s["hms"], c + 1)
                p.tensor_tensor(resg[0:r, lo:hi, :], resg[0:r, lo:hi, :], base2[0:r, lo:hi, :], ALU.add).then_inc(s["res"], 1)


def kernel(**inputs):
    import concourse.bacc as _bacc
    from concourse.bass_utils import run_bass_kernel_spmd as _run

    nc = _bacc.Bacc("TRN2", target_bir_lowering=False, num_devices=1)
    arrays, args = {}, {}
    for name, value in packed(inputs).items():
        v = np.ascontiguousarray(value)
        arrays[f"in_{name}"] = v
        args[name] = nc.dram_tensor(f"in_{name}", v.shape, mybir.dt.from_np(v.dtype), kind="ExternalInput").ap()
    out = nc.dram_tensor("out", (NI, T, D), F32, kind="ExternalOutput").ap()
    build(nc, args, out)
    r = _run(nc, [arrays], core_ids=[0])
    return r.results[0]["out"]
```

```python
from contextlib import ExitStack
import math

import numpy as np

import concourse.bass as bass
from concourse import mybir

F32 = mybir.dt.float32
BF16 = mybir.dt.bfloat16
I32 = mybir.dt.int32
U32 = mybir.dt.uint32
ALU = mybir.AluOpType
ACT = mybir.ActivationFunctionType
AX = mybir.AxisListType.X

NI, GP, PW, D = 16, 8, 16, 128
L = GP * GP
T = L + 1
N = NI * T
CI = 4
NC = NI // CI
CT = CI * T
CL = CI * L
E0, K0, F0 = 8, 2 * T // 8, 256
SL = NI * K0
NS = 64
KSUM = (0, 13, 26, 39, 52, T)
PB, PA = 8, 9
E1, F1, FS = 64, 512, 256
SH_SPLIT = 3
SH_EARLY = 5
CAP = 128
NBLK = E1 + 2 * N // CAP
U = 4
NCOL = (NBLK // U + 2) * U
NOUT = (NBLK // U + 1) * U + 1
BIG = 1.0e6
MAGIC = 12582912.0
TWO_PI = 6.2831850
EPS = 1e-5
NG = -(-N // 128)
NP = NG * 128
NJ = 2 * NG
TAIL = [(0, 2), (2, 4), (4, 6), (6, NG)]
LOADS = [(0, 2), (2, 4), (4, 6), (6, 8), (8, NG)]
SQRT_GUESS = 1597463007.0 - 2.0 ** 22 - 2.0 ** 30

C_ID, C_CEN, C_ONE, C_PA, C_PB = 0, 128, 256, 384, 512
C_PE = 640
C_TRI = C_PE + L
C_UPP = C_TRI + E1
C_IOTA = C_UPP + 128
C_K16 = C_IOTA + 128
C_PWR = C_K16 + K0
C_VEC = C_PWR + PA + PB
V_SLOT, V_E, V_EPS, V_HPI, V_SGN, V_T, V_ONE = range(7)
C_ALL = C_VEC + 7


def shape_constants():
    c = np.zeros((128, C_ALL), np.float32)
    eye = np.eye(128, dtype=np.float32)
    c[:, C_ID:C_ID + 128] = eye
    c[:, C_CEN:C_CEN + 128] = eye - 1.0 / D
    c[:, C_ONE:C_ONE + 128] = 1.0 / D
    for p in range(64):
        c[p, C_PA + 2 * p] = 1.0
        c[64 + p, C_PA + 2 * p + 1] = 1.0
        c[64 + p, C_PB + 2 * p] = -1.0
        c[p, C_PB + 2 * p + 1] = 1.0
    pos = np.arange(L, dtype=np.float32)[:, None]
    div = np.exp(np.arange(0, D, 2, dtype=np.float32) * np.float32(-math.log(10000.0) / D)).astype(np.float32)
    ang = pos * div
    c[:, C_PE:C_PE + L] = np.stack([np.sin(ang), np.cos(ang)], axis=-1).reshape(L, D).T
    c[:E1, C_TRI:C_TRI + E1] = np.triu(np.ones((E1, E1), np.float32), 1)
    c[:, C_UPP:C_UPP + 128] = np.triu(np.ones((128, 128), np.float32), 1)
    c[:, C_IOTA:C_IOTA + 128] = np.arange(128)
    c[:, C_K16:C_K16 + K0] = np.arange(1, K0 + 1)
    c[:, C_PWR:C_PWR + PB] = np.arange(PB)
    c[:, C_PWR + PB:C_PWR + PB + PA] = PB * np.arange(PA)
    c[:, C_VEC + V_SLOT] = np.arange(128) % K0 + 1
    c[:, C_VEC + V_E] = np.arange(128)
    c[:, C_VEC + V_EPS] = EPS
    c[:, C_VEC + V_HPI] = math.pi / 2
    c[:, C_VEC + V_SGN] = np.where(np.arange(128) < 64, 1.0, -1.0)
    c[:, C_VEC + V_T] = np.arange(128)
    c[:, C_VEC + V_ONE] = 1.0
    return c

(B3, CLS, BANG, BDEC, BI, BISW, LDT, DD, G1, B1, GF, BF) = range(12)
S_B1 = 12
S_WG = S_B1 + 3 * E0
S_BS1 = S_WG + E0
S_BF1 = S_BS1 + FS // 128
S_ALL = S_BF1 + F1 // 128


def packed(a):
    f = {k: np.asarray(v) for k, v in a.items()}

    def wide(v):
        return np.broadcast_to(v, (128, v.size))

    tok = [f[f"L0_tok_{n}"] for n in ("eps_in1", "eps_in2", "eps_out1", "eps_out2")]
    eps = [e.reshape(2, 128).T for e in tok[:2]] + [wide(e) for e in tok[2:]] + [e[:, None] for e in tok[2:]]
    eps += [f[f"L0_tok_W{k}_{n}"][:, None] for n in ("b", "sb") for k in (1, 2)]
    weights = np.stack([np.stack([f[f"L0_tok_W{k}_{n}"] for k in (1, 2)]) for n in ("w", "sw")])
    patches = f["x"].reshape(NI, GP, PW, GP, PW).transpose(0, 1, 3, 2, 4).reshape(2, NI * L // 2, 2, 128)
    w_in, b_in = f["L0_attn_W_input"], f["L0_attn_b_input"]
    attw = [f["L0_tok_W3_w"].T, f["L0_attn_W_angle"], f["L0_attn_W_angle"],
            np.broadcast_to(f["L0_attn_W_decay"], (D, 128)), w_in[:, 0::2], w_in[:, 1::2], w_in[:, 1::2], w_in[:, 0::2]]
    small = [f["L0_tok_W3_b"], f["cls_tok"].reshape(D), np.tile(f["L0_attn_b_angle"], 2), wide(f["L0_attn_b_decay"])[:, 0],
             np.concatenate([b_in[0::2], b_in[1::2]]), np.concatenate([b_in[1::2], b_in[0::2]]), f["L1_attn_log_dt"],
             f["L1_attn_D"], f["L1_ffn_ln1_g"], f["L1_ffn_ln1_b"], f["L1_ffn_ffln_g"], f["L1_ffn_ffln_b"]]
    b1 = f["L0_ffn_b1"].reshape(E0, 128, 2)
    small = [v[:, None] for v in small] + [b1[:, :, 0].T, b1[:, :, 1].T, f["L0_ffn_b2"].T, f["L0_ffn_Wg"],
                                           f["L1_ffn_bs1"].reshape(128, -1), f["L1_ffn_bf1"].reshape(128, -1)]
    ssm = [wide(f[f"L1_attn_Lambda_{n}"]) for n in ("real", "imag")]
    ssm += [f[f"L1_attn_{n}"] for n in ("B_real", "B_imag", "C_real", "C_imag")]
    moe = [f["L1_ffn_Ws1"], f["L1_ffn_Ws2"].reshape(128, -1), wide(f["L1_ffn_bs2"]), wide(f["L1_ffn_bf2"])]
    rest = ("L0_ffn_W1", "L0_ffn_W2", "L1_ffn_W1", "L1_ffn_W2", "L1_ffn_Wf1", "L1_ffn_Wf2")
    return {
        "eps": np.concatenate(eps, 1),
        "tok_weights": weights.reshape(2, 2, 128, 2, 128).transpose(4, 0, 1, 3, 2).reshape(128, 8, 128),
        "patches": patches.transpose(0, 3, 2, 1),
        "attn_weights": np.concatenate(attw, 1),
        "small": np.concatenate(small, 1),
        "ssm": np.concatenate(ssm, 1),
        "moe": np.concatenate(moe, 1),
        "experts_b": np.concatenate([f["L1_ffn_b1"], f["L1_ffn_b2"], f["L1_ffn_codebook"].T, f["L1_ffn_Wr"].T], 1),
        "constants": shape_constants(),
        **{k: f[k] for k in rest},
    }


SEMAPHORES = """
zero y_clear cst_in x_in0 x_in1 eps_in tokw_in attw_in small_in ssm_in ffn0_in moe_in moe2_in
feps_f wn wc_ps wcs gi_ps gmn mexp numer inv gated tok_ps h0s
xc sqr var sdv xnr pj_ps uv_ps attw tdec decs frac sc rot out_ps h1s
lg0_ps smx smx_e sms st_ps route0 pt_ps sels xtm_ps xtms ga_ps exts selw sg_ps selg
hid_ps gelu y0_ps y0s yt_ps ybs h2_ps h2s xs_ps xss h2t_ps cv_ps h3s
dtl args fracs trg lam2 prods kpads kp_out toep_in
st4 sdv4 yn5s x_out yn5a yn5p h5_ps h5s lg_ps w12a w12e w12 ohss cnt_ps nblks obks slt_ps bfc rr_out rr_in
s1_ps s1s cmbs cmb_ps cmb_sb sh_ps b2s tabs_in blk_ps blks tab_ps tabs iots
w1_in0 w1_in1 w1_in2 w1_in3 w2_in0 w2_in1 w2_in2 w2_in3
g_in0 g_in1 g_in2 g_in3 yr_out0 yr_out1 yr_out2 yr_out3 t_ps t_sb h_ps hps hss y_ps ysbs resb ix_cp p_rd sp_rd p_io
yl_in0 yl_in1 yl_in2 yl_in3 yl_in4 hms nrm xfs xf_ps ffs f1_ps fss f2_ps fins out_in res
a_ch d_ch p_ch
""".split()


def build(nc, a, out):
    xrow_dram = nc.dram_tensor("moe_rows", [N, D], F32, kind="Internal").ap()
    yrow_dram = nc.dram_tensor("moe_out_rows", [NOUT * CAP, D], F32, kind="Internal").ap()
    rrow_dram = nc.dram_tensor("residual_rows", [N, D], F32, kind="Internal").ap()
    kpad_dram = nc.dram_tensor("ssm_kernel", [128, 2 * T - 1], F32, kind="Internal").ap()

    ctx = ExitStack()
    with ctx:
        def sb(name, shape, dt=F32):
            return ctx.enter_context(nc.sbuf_tensor(name, shape, dt))[:]

        s = {n: ctx.enter_context(nc.semaphore(n)) for n in SEMAPHORES}
        PS = ctx.enter_context(nc.psum_tensor("PS", [128, 8, 512], F32))[:]

        def carve(region, shapes):
            views, at = [], 0
            for shape in shapes:
                n = math.prod(shape)
                v = region[:, at:at + n]
                if len(shape) == 2:
                    v = v.rearrange("p (a b) -> p a b", a=shape[0])
                elif len(shape) == 3:
                    v = v.rearrange("p (a b c) -> p a b c", a=shape[0], b=shape[1])
                views.append(v)
                at += n
            assert at <= region.shape[1], (at, region.shape)
            return views

        R1 = sb("R1", [128, 8448])
        R2 = sb("R2", [128, 12400])
        R3 = sb("R3", [128, 7680])
        R4 = sb("R4", [128, 26 * CT])
        R5 = sb("R5", [128, 4096])
        RF = sb("RF", [128, 6 * N])

        cst = sb("cst", [128, C_ALL])
        ident = cst[:, C_ID:C_ID + 128]
        cen = cst[:, C_CEN:C_CEN + 128]
        onesd = cst[:, C_ONE:C_ONE + 128]
        perm_a = cst[:, C_PA:C_PA + 128]
        perm_b = cst[:, C_PB:C_PB + 128]

        def vec(k, rows=128):
            return cst[0:rows, C_VEC + k:C_VEC + k + 1]

        h0, h1, h2, xn, sq, sd = carve(RF, [[N]] * 6)

        xT, gmin, emis, gate = carve(R2, [[2, 2, 512], [1024], [1024], [1024]])
        feps, fabs, fsgn, tokw = carve(R4, [[266], [262], [262], [8, 128]])
        bcol = sb("bcol", [128, 2])
        peb = sb("peb", [128, L])
        two, dt = sb("two", [128, 1]), sb("dt", [128, 1])
        small = sb("small", [128, S_ALL])
        attw = sb("attw", [128, 5, 128])
        w3T, wang, wdec, winp, winsw = [attw[:, k, :] for k in range(5)]

        def col(k):
            return small[:, k:k + 1]

        mask = sb("mask", [128, CI, T])
        ring4 = carve(R4, [[13, CT]] * 2) + carve(R1, [[13, CT]] * 2)
        wg = small[:, S_WG:S_WG + E0]
        w1a, w2a = carve(R5, [[E0, F0], [E0, 2, D]])
        bT = small[:, S_B1:S_B1 + 3 * E0].rearrange("p (c e) -> p c e", c=3)
        xtm, sel, exT, yT, Yb, selG = carve(
            R2, [[NI, D], [128, K0], [E0, NI, K0], [NI, E0, K0], [NI, D], [NC, CT]])
        sm = sb("sm", [T, 4, 128])
        smr = sb("smr", [T, 2, NI])
        rt0 = sb("rt0", [128, 6, T])
        selw, = carve(R4, [[128, K0]])
        top8 = sb("top8", [128, 2, 8])
        ssm = sb("ssm", [128, 6, NS])
        lam, bc4 = ssm[:, 0:2, :], ssm[:, 2:6, :]
        NPW = PB + PA
        pAR, pTI, pE, pS, pC, UU, q64 = carve(R3, [[NPW, NS]] * 5 + [[PA, 2, NS], [14, NS]])
        VV, = carve(R3, [[NPW, 2, NS]])
        prod, = carve(R1, [[T, 2 * NS]])
        kpad = sb("kpad", [128, 2 * T - 1])
        toep, = carve(R1, [[D, T]])
        xs, h2t, h3 = carve(R4[0:T, :], [[NI, D]] * 3)
        hres = h2t
        lnst, = carve(R2[0:T, 8192:], [[NI, NC, 6]])
        mv = sb("mv", [T, NI, 2])
        lnv = sb("lnv", [T, 8, NI])
        yn5, h5, oh = carve(R2, [[NI, D], [NP], [2, NG * E1]])
        ohs = sb("ohs", [128, NG * E1], BF16)
        before, ones_b = sb("before", [128, 128], BF16), sb("ones_b", [128, 128], BF16)
        tri_cap, nblk_b = sb("tri_cap", [E1, E1], BF16), sb("nblk_b", [E1, 128], BF16)
        base2 = carve(R2, [[NG, D]])[0]
        wc = sb("wc", [128, E1])
        mx8, ix8 = sb("mx8", [128, NG, 8]), sb("ix8", [128, NG, 8], U32)
        ef = sb("ef", [128, 2, NG])
        wk = sb("wk", [128, 2, NG])
        wts = sb("wts", [128, 2, NG])
        esm = sb("esm", [E1, 8])
        obk = sb("obk", [E1, 2, NCOL])
        experts_b = sb("experts_b", [E1, F1 + D + E1 + D])
        b1all, b2all = experts_b[:, 0:F1], experts_b[:, F1:F1 + D]
        cbT, wrT = experts_b[:, F1 + D:F1 + D + E1], experts_b[:, F1 + D + E1:F1 + D + E1 + D]
        moe = sb("moe", [128, 2 * FS + 2 * D])
        ws1, ws2 = moe[:, 0:FS], moe[:, FS:2 * FS].rearrange("p (c d) -> p c d", c=2)
        bs2, bf2 = moe[:, 2 * FS:2 * FS + D], moe[:, 2 * FS + D:2 * FS + 2 * D]
        bs1, bf1 = small[:, S_BS1:S_BF1], small[:, S_BF1:S_ALL]
        s1, = carve(RF, [[2, N]])
        cmb, cmbT = carve(sq, [[NG, E1]])[0], sd
        sprod, ohAf, ohBf = carve(R1, [[2, NG * E1], [CAP * NJ // 2], [3 * NCOL * NJ // 2]])
        ohA = ohAf.bitcast(BF16).rearrange("p (a j) -> p a j", a=CAP)
        ohB = ohBf.bitcast(BF16).rearrange("p (q i j) -> p q i j", q=3, i=NCOL)
        iotb = R4[:, 0:CAP * NJ // 2].bitcast(BF16).rearrange("p (a j) -> p a j", a=CAP)
        slot = sb("slot", [128, 3, NJ])
        slotb = sb("slotb", [128, 2, NJ], BF16)
        cvb = sb("cvb", [128, NJ], BF16)
        tabf, = carve(xn, [[5, NCOL]])
        tabx, yix = sb("tabx", [128, NCOL], U32), sb("yix", [128, NJ], U32)
        bexp, trips = sb("bexp", [1, NCOL], I32), sb("trips", [1, 1], I32)
        b1blk = sb("b1blk", [128, 4, NCOL])
        zeros = sb("zeros", [128, D])
        w1r, w2r, hs = carve(R3, [[U, F1], [U, 4 * D], [U, 4 * CAP]])
        hpre, xg, xsr, ysb = carve(R5, [[U, 4 * CAP], [U, D], [U, CAP], [U, D]])
        ixg = sb("ixg", [128, U], U32)
        yl, xf, fs = carve(R2[:, 2048:], [[NJ, D], [NG, D], [4, N]])
        resg, = carve(R4, [[NG, D]])
        st6, mv6 = sb("st6", [128, NG, 6]), sb("mv6", [128, NG, 2])
        nw = sb("nw", [128, 4, NG])
        nwi = sb("nwi", [128, NG], I32)
        wf1, wf2 = carve(h2, [[F1], [4, D]])
        ff = xn
        hid, = carve(R2, [[2, 2 * SL]])
        y_dst = yT

        def cs(c):
            return slice(c * CT, (c + 1) * CT)

        def im(b):
            return slice(b * T, (b + 1) * T)

        def tile4(b):
            return slice((b % CI) * T, (b % CI + 1) * T)

        def tok4(b):
            return slice((b % CI) * D, (b % CI + 1) * D)

        def rows(g):
            return min(128, N - 128 * g)

        def gc(g):
            return slice(128 * g, 128 * g + rows(g))

        def in_chunk(g):
            return -(-min(N, 128 * g + 128) // CT) - 1

        def scores(g):
            return PS[:, in_chunk(g), (g % 3) * E1:(g % 3 + 1) * E1]

        def even(lo, hi):
            full = min(hi, N // 128)
            return [(a_, b_, rows(a_)) for a_, b_ in ((lo, full), (full, hi)) if a_ < b_]

        def spread(ap, axis, n):
            shape = list(ap.shape)
            return ap.unsqueeze(axis).to_broadcast(shape[:axis] + [n] + shape[axis:])

        LN_XC = [[2, 3, 0, 1], [0, 1, 2, 3], [4, 5, 6, 7]]
        LN_VAR = [[4, 5, 6, 7], [4, 5, 6, 7], [0, 1, 2, 3]]
        PJ = [[2, 3, 4, 5], [0, 1, 6, 7]]
        TD, DEC, AN, TH, RM, FR, AF, SN, CS_, CU, SU, GI, GS = range(13)

        block = ctx.enter_context(nc.Block())

        @block.sync
        def _(sp):
            sp.dma_start(feps, a["eps"]).then_inc(s["eps_in"], 16)
            sp.dma_start(xT[:, 0], a["patches"][0]).then_inc(s["x_in0"], 16)
            sp.dma_start(xT[:, 1], a["patches"][1]).then_inc(s["x_in1"], 16)
            sp.dma_start(cst, a["constants"]).then_inc(s["cst_in"], 16)
            sp.dma_start(w1a, a["L0_ffn_W1"].rearrange("e h f -> h e f")).then_inc(s["ffn0_in"], 16)
            sp.dma_start(w2a, a["L0_ffn_W2"].rearrange("e (p c) h -> p e c h", c=2)).then_inc(s["ffn0_in"], 16)
            sp.dma_start(experts_b, a["experts_b"]).then_inc(s["moe_in"], 16)
            sp.dma_start(moe, a["moe"]).then_inc(s["moe_in"], 16)
            sp.wait_ge(s["zero"], 1)
            sp.dma_start(yrow_dram.rearrange("(n p) d -> p n d", p=CAP), spread(zeros[:, :], 1, NOUT)).then_inc(s["y_clear"], 16)
            sp.wait_ge(s["kpads"], 1)
            sp.dma_start(kpad_dram, kpad[:, :]).then_inc(s["kp_out"], 16)
            sp.wait_ge(s["kp_out"], 16)
            skewed = bass.AP(kpad_dram.tensor, 0, [[1, T], [2 * T - 1, D], [1, T]])
            sp.dma_start(toep[0:T], skewed).then_inc(s["toep_in"], 16)
            sp.wait_ge(s["yn5s"], NC)
            sp.wait_ge(s["yn5a"], NC)
            sp.wait_ge(s["yn5p"], NC)
            sp.dma_start(xrow_dram.rearrange("(b t) d -> t b d", b=NI), yn5[0:T]).then_inc(s["x_out"], 16)
            sp.wait_ge(s["res"], 1)
            sp.dma_start(rrow_dram.rearrange("(b t) d -> t b d", b=NI), hres).then_inc(s["rr_out"], 16)
            sp.wait_ge(s["cmbs"], 1)
            sp.dma_start(wf1, a["L1_ffn_Wf1"]).then_inc(s["moe2_in"], 16)
            sp.dma_start(wf2, a["L1_ffn_Wf2"].rearrange("(p c) d -> p c d", p=128)).then_inc(s["moe2_in"], 16)

            sp.wait_ge(s["rr_out"], 16)
            sp.wait_ge(s["tabs_in"], 1)
            full = NG - 1 if rows(NG - 1) < 128 else NG
            sp.dma_start(resg[:, 0:full, :], rrow_dram[0:128 * full].rearrange("(g p) d -> p g d", p=128)).then_inc(s["rr_in"], 16)
            if full < NG:
                sp.dma_start(resg[0:rows(full), full, :], rrow_dram[128 * full:N]).then_inc(s["rr_in"], 16)

            sp.wait_ge(s["blks"], 2)
            n_trips = sp.value_load(trips[0:1, 0:1], min_val=1, max_val=NCOL // U - 1)

            def expert(at):
                return sp.value_load(bexp[0:1, at], min_val=0, max_val=E1 - 1)

            def load_first(j, e):
                sp.dma_start(w1r[:, j, :], a["L1_ffn_W1"][bass.ds(e, 1)].rearrange("o h f -> (o h) f"))\
                    .then_inc(s[f"w1_in{j}"], 16)

            def load_second(j, e):
                sp.dma_start(w2r[:, j, :], a["L1_ffn_W2"][bass.ds(e, 1)].rearrange("o (p c) d -> (o p) (c d)", p=128))\
                    .then_inc(s[f"w2_in{j}"], 16)

            sp.wait_ge(s["p_io"], 1)
            for j in range(U):
                e = expert(slice(j, j + 1))
                load_first(j, e)
                if j == U - 1:
                    sp.wait_ge(s["y_ps"], 1)
                load_second(j, e)
            with sp.Fori(1, n_trips) as it:
                for j in range(U):
                    sp.wait_ge(s["h_ps"], it * U + (j - U + 1))
                    sp.sem_inc(s["sp_rd"], 1)
                    e = expert(bass.ds(it * U + j, 1))
                    load_first(j, e)
                    sp.wait_ge(s["y_ps"], it * U + (j - U + 2))
                    load_second(j, e)
            result = out.rearrange("b t d -> (b t) d")
            for c, (lo, hi) in enumerate(TAIL):
                sp.wait_ge(s["fins"], c + 1)
                for g, end, r in even(lo, hi):
                    dst = result[128 * g:128 * (end - 1) + r].rearrange("(g p) d -> p g d", p=r)
                    sp.dma_start(dst, resg[0:r, g:end, :]).then_inc(s["out_in"], 16)
            sp.wait_ge(s["out_in"], 16 * sum(len(even(lo, hi)) for lo, hi in TAIL))

        @block.tensor
        def _(pe):
            mm, tr = nc.tensor.matmul, nc.tensor.transpose

            def keep_warm(bank, n, at=0, src=cst, width=256):
                for _ in range(n):
                    mm(PS[:, bank, at:at + width], src[:, 0:128], src[:, 0:width], start=True, stop=True)

            pe.wait_ge(s["zero"], 1)
            keep_warm(0, 24, src=zeros, width=128)
            for c in range(NC):
                if c % 2 == 0:
                    pe.wait_ge(s[f"x_in{c // 2}"], 16)
                for k in range(2):
                    pe.wait_ge(s["wn"], 2 * k + 2)
                    for h in range(2):
                        last = mm(PS[:, (LN_XC[0][c], 4 + c)[k], 0:CL], tokw[:, 2 * k + h, :],
                                  xT[:, c // 2, h, c % 2 * CL:(c % 2 + 1) * CL], start=h == 0, stop=h == 1)
                last.then_inc(s["gi_ps"], 1)
            pe.wait_ge(s["attw_in"], 16)
            pe.wait_ge(s["cst_in"], 16)
            for c in range(NC):
                if c:
                    keep_warm(2, 2)
                pe.wait_ge(s["gated"], c + 1)
                mm(PS[:, 4 + c, 0:CL], w3T, gate[:, c * CL:(c + 1) * CL], start=True, stop=True).then_inc(s["tok_ps"], 1)
            keep_warm(2, 2)

            def centre(k, c, src):
                mm(PS[:, LN_XC[k][c], 0:CT], cen, src[:, cs(c)], start=True, stop=True).then_inc(s["xc"], 1)

            def variance(k, c):
                pe.wait_ge(s["sqr"], 4 * k + c + 1)
                mm(PS[:, LN_VAR[k][c], 0:CT], onesd, sq[:, cs(c)], start=True, stop=True).then_inc(s["var"], 1)

            for c in range(NC):
                pe.wait_ge(s["h0s"], c + 1)
                centre(0, c, h0)
                if c:
                    variance(0, c - 1)
            variance(0, NC - 1)

            def project_turns(c):
                bk = PJ[c % 2]
                pe.wait_ge(s["xnr"], 2 if c == 0 else 4)
                if c >= 2:
                    pe.wait_ge(s["frac"], c - 1)
                    pe.wait_ge(s["tdec"], c - 1)
                mm(PS[:, bk[0], 0:CT], wang, xn[:, cs(c)], start=True, stop=True)
                mm(PS[:, bk[1], 0:CT], wdec, xn[:, cs(c)], start=True, stop=True).then_inc(s["pj_ps"], 1)

            def project_inputs(c):
                bk = PJ[c % 2]
                if c >= 2:
                    pe.wait_ge(s["h1s"], c - 1)
                mm(PS[:, bk[2], 0:CT], winp, xn[:, cs(c)], start=True, stop=True)
                mm(PS[:, bk[3], 0:CT], winsw, xn[:, cs(c)], start=True, stop=True).then_inc(s["uv_ps"], 1)

            def rotate_back(c):
                r = ring4[c]
                pe.wait_ge(s["rot"], c + 1)
                bank = PS[:, PJ[c % 2][2], 0:CT]
                mm(bank, ident, h0[:, cs(c)], start=True, stop=False)
                mm(bank, perm_a, r[:, RM], start=False, stop=False)
                mm(bank, perm_b, r[:, AN], start=False, stop=True).then_inc(s["out_ps"], 1)

            pe.wait_ge(s["attw"], 1)
            project_turns(0)
            project_inputs(0)
            project_turns(1)
            project_inputs(1)
            project_turns(2)
            rotate_back(0)
            project_turns(3)
            project_inputs(2)
            rotate_back(1)
            project_inputs(3)
            rotate_back(2)

            for c in range(NC):
                pe.wait_ge(s["h1s"], c + 1)
                centre(1, c, h1)
                if c == 0:
                    rotate_back(3)
                else:
                    pe.wait_ge(s["h1s"], min(NC, c + 2))
                    if c < NC - 1:
                        keep_warm(7, 0)
                    variance(1, c - 1)
            variance(1, NC - 1)

            pe.wait_ge(s["ffn0_in"], 32)
            for c in range(NC):
                pe.wait_ge(s["xnr"], 4 + c + 1)
                for b in range(c * CI, c * CI + CI):
                    last = mm(PS[0:T, 4, b * E0:(b + 1) * E0], xn[:, im(b)], wg, start=True, stop=True)
                if c == NC - 1:
                    last.then_inc(s["lg0_ps"], 1)
                for b in range(c * CI, c * CI + CI):
                    last = tr(PS[0:T, c, tok4(b)], xn[:, im(b)], ident)
                last.then_inc(s["xtm_ps"], 1)
                if c < NC - 1:
                    keep_warm(4, 0, at=256)
            pe.wait_ge(s["sms"], 1)
            tr(PS[:, 5, 0:T], sm[:, 2, :], ident[0:T, 0:T]).then_inc(s["st_ps"], 1)
            keep_warm(7, 3)
            pe.wait_ge(s["route0"], 1)
            pe.wait_ge(s["xtms"], 4)
            tr(PS[0:T, 4, 0:128], rt0[:, 5, :], ident).then_inc(s["pt_ps"], 1)
            keep_warm(7, 4)
            for b in range(NI):
                if b % CI == 0:
                    pe.wait_ge(s["sels"], b // CI + 1)
                last = mm(PS[:, b // CI, tok4(b)], xtm[0:T, b, :],
                          sel[0:T, b * E0:(b + 1) * E0, :].rearrange("p e k -> p (e k)"), start=True, stop=True)
                if b % CI == CI - 1:
                    last.then_inc(s["ga_ps"], 1)
            pe.wait_ge(s["selw"], 1)
            for b in range(NI):
                last = tr(PS[:, 4 + b // CI, tile4(b)], selw[0:T, b * E0:(b + 1) * E0, :].rearrange("p e k -> p (e k)"),
                          ident[0:T, 0:T])
                if b % CI == CI - 1:
                    last.then_inc(s["sg_ps"], 1)

            def hidden0(e):
                if e == 0:
                    pe.wait_ge(s["exts"], 4)
                if e >= 2:
                    pe.wait_ge(s["gelu"], e - 1)
                for c in range(2):
                    last = mm(PS[:, e % 2, c * SL:(c + 1) * SL], w1a[:, e, c:F0:2],
                              exT[:, e].rearrange("p b k -> p (b k)"), start=True, stop=True)
                last.then_inc(s["hid_ps"], 1)

            hidden0(0)
            for e in range(E0):
                if e + 1 < E0:
                    hidden0(e + 1)
                pe.wait_ge(s["gelu"], e + 1)
                if e >= 2:
                    pe.wait_ge(s["y0s"], e - 1)
                for c in range(2):
                    last = mm(PS[:, 2 + e % 2, 0:SL], w2a[:, e, c, :], hid[:, e % 2, c * SL:(c + 1) * SL],
                              start=c == 0, stop=c == 1)
                last.then_inc(s["y0_ps"], 1)
            pe.wait_ge(s["selg"], 4)
            keep_warm(0, 4)
            pe.wait_ge(s["y0s"], 8)
            for b in range(NI):
                last = tr(PS[:, 4 + b // CI, tok4(b)], yT[:, b].rearrange("p e k -> p (e k)"), ident)
                if b % CI == CI - 1:
                    last.then_inc(s["yt_ps"], 1)
            keep_warm(0, 4)
            pe.wait_ge(s["ybs"], 4)

            def behind_choice(g):
                mm(PS[:, g, 0:CT], ident, h1[:, cs(g)], start=True, stop=False, skip_group_check=True)
                for b in range(g * CI, g * CI + CI):
                    last = mm(PS[:, g, tile4(b)], Yb[:, b, :], selG[:, g, tile4(b)], start=False,
                              stop=b % CI == CI - 1, skip_group_check=True)
                last.then_inc(s["h2_ps"], 1)

            behind_choice(0)
            behind_choice(1)
            for c in range(NC):
                pe.wait_ge(s["h2s"], c + 1)
                centre(2, c, h2)
                if c:
                    variance(2, c - 1)
                if c + 2 < NC:
                    behind_choice(c + 2)
            variance(2, NC - 1)
            for c in range(NC):
                pe.wait_ge(s["xnr"], 8 + c + 1)
                for b in range(c * CI, c * CI + CI):
                    last = tr(PS[0:T, c, tok4(b)], xn[:, im(b)], ident)
                last.then_inc(s["xs_ps"], 1)
                for b in range(c * CI, c * CI + CI):
                    last = tr(PS[0:T, 4 + c, tok4(b)], h2[:, im(b)], ident)
                last.then_inc(s["h2t_ps"], 1)
            pe.wait_ge(s["xss"], 4)
            pe.wait_ge(s["toep_in"], 16)
            for h in range(D):
                n = min(4, 32 - h % 32)
                last = mm(PS[0:T, h // 32, (h % 32) * NI:(h % 32 + n) * NI], toep[0:T, h, :],
                          xs[:, :, h:h + n].rearrange("p b h -> p h b"), start=True, stop=True)
                if h % 32 == 31:
                    last.then_inc(s["cv_ps"], 1)

            pe.wait_ge(s["h3s"], 4)
            pe.wait_ge(s["moe_in"], 16 * 2)
            mm(PS[:, 3, 0:E1], wrT, cbT, start=True, stop=True).then_inc(s["wc_ps"], 1)
            keep_warm(6, 10)

            def turn_rows(c):
                pe.wait_ge(s["yn5s"], c + 1)
                pe.wait_ge(s["yn5a"], c + 1)
                pe.wait_ge(s["yn5p"], c + 1)
                for b in range(c * CI, c * CI + CI):
                    last = tr(PS[:, 4 + c, tile4(b)], yn5[0:T, b, :], ident[0:T, 0:T])
                last.then_inc(s["h5_ps"], 1)

            def logits(c):
                pe.wait_ge(s["h5s"], c + 1)
                for g in range(NG):
                    if in_chunk(g) == c:
                        last = mm(scores(g), h5[:, g * 128:(g + 1) * 128], wc[:, :], start=True, stop=True)
                last.then_inc(s["lg_ps"], 1)

            for c in range(NC):
                turn_rows(c)
            pe.wait_ge(s["wcs"], 1)
            for c in range(NC):
                logits(c)

            def shared_hidden(k):
                if k >= 2:
                    pe.wait_ge(s["s1s"], k - 1)
                mm(PS[:, 6 + k % 2, 0:CT], ws1[:, k % 2:FS:2], h5[:, cs(k // 2)], start=True, stop=True)\
                    .then_inc(s["s1_ps"], 1)

            for k in range(SH_EARLY):
                shared_hidden(k)
            pe.wait_ge(s["bfc"], 1)
            pe.wait_ge(s["ohss"], 1)
            for g in range(NG):
                r = rows(g)
                last = mm(PS[0:E1, 0, 0:1], ohs[0:r, g * E1:(g + 1) * E1], ones_b[0:r, 0:1], start=g == 0, stop=g == NG - 1)
            last.then_inc(s["cnt_ps"], 1)
            head, tail = PS[:, 4, 0:8 * E1], PS[:, 5, 0:E1]
            mm(head, before[:, :], ohs[:, 0:8 * E1], start=True, stop=False, skip_group_check=True)
            mm(tail, before[0:rows(8), :], ohs[0:rows(8), 8 * E1:9 * E1], start=True, stop=False, skip_group_check=True)
            for g in range(8):
                one = ohs[:, g * E1:(g + 1) * E1]
                if g < 7:
                    mm(head[:, (g + 1) * E1:8 * E1], ones_b[:, :], spread(one, 1, 7 - g), start=False, stop=False,
                       skip_group_check=True)
                mm(tail, ones_b[:, :], one, start=False, stop=False, skip_group_check=True)
                if g == 4:
                    pe.wait_ge(s["nblks"], 1)
                    mm(PS[0:E1, 0, 0:1], cst[0:E1, C_TRI:C_TRI + E1], esm[:, 1:2], start=True, stop=True)
                    mm(PS[0:1, 0, 8:9], esm[:, 1:2], vec(V_ONE, E1), start=True, stop=True).then_inc(s["cnt_ps"], 1)
            mm(head, nblk_b[:, :], spread(tri_cap[:, :], 1, 8), start=False, stop=True, skip_group_check=True)
            mm(tail, nblk_b[:, :], tri_cap[:, :], start=False, stop=True, skip_group_check=True).then_inc(s["slt_ps"], 1)
            pe.wait_ge(s["obks"], 1)
            mm(PS[0:1, 3, 400:400 + NCOL], vec(V_E, E1), obk[:, 1, :], start=True, stop=True)
            for c in range(4):
                last = mm(PS[:, 3, c * NCOL:(c + 1) * NCOL], b1all[:, c:F1:4], obk[:, 1, :], start=True, stop=True)
            last.then_inc(s["blk_ps"], 1)
            for k in range(SH_EARLY, 2 * NC):
                shared_hidden(k)
            pe.wait_ge(s["cmbs"], 1)
            for g in range(NG):
                r = rows(g)
                last = tr(PS[0:E1, g // 4, (g % 4) * 128:(g % 4) * 128 + r], cmb[0:r, g, :], ident[0:r, 0:r])
                if g % 4 == 3 or g == NG - 1:
                    last.then_inc(s["cmb_ps"], 1)
            pe.wait_ge(s["cmb_sb"], 3)
            pe.wait_ge(s["s1s"], 8)
            for g in range(NG):
                bank = PS[0:rows(g), g // 4, (g % 4) * 128:(g % 4 + 1) * 128]
                for c in range(2):
                    mm(bank, s1[:, c, gc(g)], ws2[:, c, :], start=c == 0, stop=False)
                last = mm(bank, cmbT[0:E1, gc(g)], b2all[:, :], start=False, stop=True)
                if g % 4 == 3 or g == NG - 1:
                    last.then_inc(s["sh_ps"], 1)
                if g == SH_SPLIT:
                    pe.wait_ge(s["tabs_in"], 1)
                    for j in range(NJ):
                        r = rows(j % NG)
                        last = mm(PS[:, 5, 0:3 * NCOL], ohA[0:r, :, j], ohB[0:r, :, :, j].rearrange("p q i -> p (q i)"),
                                  start=j == 0, stop=j == NJ - 1)
                    last.then_inc(s["tab_ps"], 1)

            def turn(j):
                tr(PS[:, U + j, 0:CAP], xg[:, j, :], ident).then_inc(s["t_ps"], 1)

            def second(j):
                for c in range(4):
                    last = mm(PS[:, U + j, 128:256], hs[:, j, c * CAP:(c + 1) * CAP], w2r[:, j, c * D:(c + 1) * D],
                              start=c == 0, stop=c == 3)
                last.then_inc(s["y_ps"], 1)

            pe.wait_ge(s["tabs"], 1)
            pe.wait_ge(s["p_io"], 1)
            pe.wait_ge(s["blks"], 2)
            pe_trips = pe.value_load(trips[0:1, 0:1], min_val=1, max_val=NCOL // U - 1)
            pe.wait_ge(s["g_in0"], 16)
            turn(0)
            pe.wait_ge(s["b2s"], 3)

            def pe_body(it, first):
                for j in range(U):
                    nxt, prev = (j + 1) % U, (j - 1) % U
                    pe.wait_ge(s[f"g_in{nxt}"], it * 16 + (16 if j < U - 1 else 32))
                    if not (first and j + 3 <= U):
                        pe.wait_ge(s["ysbs"], it * U + (j + 3 - U))
                    turn(nxt)
                    pe.wait_ge(s[f"w1_in{j}"], it * 16 + 16)
                    pe.wait_ge(s["t_sb"], it * U + (j + 1))
                    for c in range(4):
                        last = mm(PS[:, j, c * CAP:(c + 1) * CAP], w1r[:, j, c:F1:4], xsr[:, j, :], start=True, stop=True)
                    last.then_inc(s["h_ps"], 1)
                    pe.wait_ge(s["hss"], it * U + (j + U))
                    if not (first and j == 0):
                        pe.wait_ge(s[f"w2_in{prev}"], it * 16 + (16 if j else 0))
                    second(prev)

            pe_body(0, True)
            with pe.Fori(1, pe_trips) as it:
                pe_body(it, False)
            pe.wait_ge(s["hss"], pe_trips * U + U)
            pe.wait_ge(s[f"w2_in{U - 1}"], pe_trips * 16)
            second(U - 1)

            pe.wait_ge(s["moe2_in"], 32)
            pe.wait_ge(s["ysbs"], pe_trips * U + 1)

            keep_warm(7, 34)

            def turn_back(c):
                lo, hi = TAIL[c]
                pe.wait_ge(s["xfs"], c + 1)
                if c >= 2:
                    pe.wait_ge(s["ffs"], c - 1)
                for g in range(lo, hi):
                    r = rows(g)
                    last = tr(PS[:, c % 2, (g - lo) * 128:(g - lo) * 128 + r], xf[0:r, g, :], ident[0:r, 0:r])
                last.then_inc(s["xf_ps"], 1)

            turn_back(0)
            for c, (lo, hi) in enumerate(TAIL):
                cols_c = slice(128 * lo, min(N, 128 * hi))
                pe.wait_ge(s["ffs"], c + 1)
                for f in range(4):
                    if c:
                        pe.wait_ge(s["fss"], 4 * (c - 1) + f + 1)
                    mm(PS[:, 2 + f, 0:cols_c.stop - cols_c.start], wf1[:, f:F1:4], ff[:, cols_c], start=True, stop=True)\
                        .then_inc(s["f1_ps"], 1)
                if c >= 2:
                    pe.wait_ge(s["fins"], c - 1)
                for g in range(lo, hi):
                    for f in range(4):
                        if g == lo:
                            pe.wait_ge(s["fss"], 4 * c + f + 1)
                        last = mm(PS[0:rows(g), 6 + c % 2, (g - lo) * 128:(g - lo + 1) * 128], fs[:, f, gc(g)], wf2[:, f, :],
                                  start=f == 0, stop=f == 3)
                last.then_inc(s["f2_ps"], 1)
                if c + 1 < len(TAIL):
                    turn_back(c + 1)

        @block.scalar
        def _(act):
            act.dma_start(tokw, a["tok_weights"]).then_inc(s["tokw_in"], 16)
            act.dma_start(attw, a["attn_weights"]).then_inc(s["attw_in"], 16)
            act.dma_start(small, a["small"]).then_inc(s["small_in"], 16)
            act.dma_start(ssm, a["ssm"]).then_inc(s["ssm_in"], 16)

            n_link = [0]

            def link(ins):
                n_link[0] += 1
                ins.then_inc(s["a_ch"], 1)
                act.wait_ge(s["a_ch"], n_link[0])

            nc.scalar.preload_act_table_set("sqrt_and_others")
            act.wait_ge(s["eps_in"], 16)
            nc.scalar.activation(fabs, feps[:, 0:262], ACT.Abs)
            link(nc.scalar.activation(fsgn, feps[:, 0:262], ACT.Sign))
            nc.scalar.activation(fabs, fabs, ACT.Sqrt).then_inc(s["feps_f"], 1)
            nc.scalar.preload_act_table_set("natural_log_exp_and_others")
            act.wait_ge(s["small_in"], 16)
            nc.scalar.activation(dt[:, :], col(LDT), ACT.Exp).then_inc(s["mexp"], 1)

            def exponential(c):
                h = slice(c * CL, (c + 1) * CL)
                act.wait_ge(s["gmn"], c + 1)
                nc.scalar.activation(emis[:, h], gmin[:, h], ACT.Exp).then_inc(s["mexp"], 1)

            exponential(0)
            for c in range(NC):
                if c + 1 < NC:
                    exponential(c + 1)
                h = slice(c * CL, (c + 1) * CL)
                act.wait_ge(s["numer"], c + 1)
                link(nc.scalar.activation(emis[:, h], gate[:, h], ACT.Ln, bias=two[:, :]))
                nc.scalar.activation(emis[:, h], emis[:, h], ACT.Exp, scale=-1.0).then_inc(s["inv"], 1)
            act.wait_ge(s["args"], 2)
            nc.scalar.activation(pE, pAR, ACT.Exp).then_inc(s["trg"], 1)

            def squares(k, c):
                act.wait_ge(s["xc"], 4 * k + c + 1)
                if k:
                    act.wait_ge(s["var"], 4 * k)
                nc.scalar.activation(sq[:, cs(c)], PS[:, LN_XC[k][c], 0:CT], ACT.Square).then_inc(s["sqr"], 1)

            def deviation(k, c):
                act.wait_ge(s["var"], 4 * k + c + 1)
                if k:
                    act.wait_ge(s["xnr"], 4 * k)
                link(nc.scalar.activation(sd[:, cs(c)], PS[:, LN_VAR[k][c], 0:CT], ACT.Ln, bias=vec(V_EPS)))
                nc.scalar.activation(sd[:, cs(c)], sd[:, cs(c)], ACT.Exp, scale=-0.5).then_inc(s["sdv"], 1)

            for c in range(NC):
                squares(0, c)
                if c:
                    deviation(0, c - 1)
            deviation(0, NC - 1)

            nc.scalar.preload_act_table_set("silu_and_others")

            def decay(c):
                act.wait_ge(s["pj_ps"], c + 1)
                nc.scalar.activation(ring4[c][:, TD], PS[:, PJ[c % 2][1], 0:CT], ACT.Tanh, scale=0.5,
                                     bias=col(BDEC)).then_inc(s["tdec"], 1)

            def sincos(c):
                r = ring4[c]
                act.wait_ge(s["frac"], c + 1)
                link(nc.scalar.activation(r[:, AF], r[:, FR], ACT.Abs))
                nc.scalar.activation(r[:, SN], r[:, FR], ACT.Sin, scale=TWO_PI)
                nc.scalar.activation(r[:, CS_], r[:, AF], ACT.Sin, scale=-TWO_PI, bias=vec(V_HPI)).then_inc(s["sc"], 1)

            def residual1(c):
                act.wait_ge(s["out_ps"], c + 1)
                nc.scalar.activation(h1[:, cs(c)], PS[:, PJ[c % 2][2], 0:CT], ACT.Copy).then_inc(s["h1s"], 1)

            act.wait_ge(s["attw"], 1)
            for c in range(NC):
                decay(c)
                sincos(c)
                if c >= 2:
                    residual1(c - 2)
            act.wait_ge(s["fracs"], 1)
            link(nc.scalar.activation(pC, pTI, ACT.Abs))
            nc.scalar.activation(pS, pTI, ACT.Sin, scale=TWO_PI).then_inc(s["trg"], 1)
            residual1(NC - 2)
            nc.scalar.activation(pC, pC, ACT.Sin, scale=-TWO_PI, bias=vec(V_HPI)).then_inc(s["trg"], 1)
            residual1(NC - 1)

            nc.scalar.preload_act_table_set("natural_log_exp_and_others")
            for c in range(NC):
                squares(1, c)
                if c:
                    deviation(1, c - 1)
            deviation(1, NC - 1)

            act.wait_ge(s["smx"], 1)
            nc.scalar.activation(sm[:, 1, :], sm[:, 0, :], ACT.Exp).then_inc(s["smx_e"], 1)
            for g in range(NC):
                act.wait_ge(s["xtm_ps"], g + 1)
                nc.scalar.activation(xtm[0:T, CI * g:CI * g + CI, :],
                                     PS[0:T, g, :].rearrange("p (b d) -> p b d", b=CI), ACT.Copy).then_inc(s["xtms"], 1)
            for g in range(NC):
                act.wait_ge(s["ga_ps"], g + 1)
                nc.scalar.activation(exT[:, :, CI * g:CI * g + CI, :].rearrange("p e b k -> p b e k"),
                                     PS[:, g, :].rearrange("p (b e k) -> p b e k", b=CI, e=E0), ACT.Copy)\
                    .then_inc(s["exts"], 1)
            for e in range(E0):
                act.wait_ge(s["hid_ps"], e + 1)
                if e >= 2:
                    act.wait_ge(s["y0_ps"], e - 1)
                for c in range(2):
                    last = nc.scalar.activation(hid[:, e % 2, c * SL:(c + 1) * SL], PS[:, e % 2, c * SL:(c + 1) * SL],
                                                ACT.Gelu, bias=bT[:, c, e:e + 1])
                last.then_inc(s["gelu"], 1)
            nc.scalar.preload_act_table_set("natural_log_exp_and_others")
            for g in (0, 2):
                act.wait_ge(s["yt_ps"], g + 1)
                nc.scalar.activation(Yb[:, CI * g:CI * g + CI, :], PS[:, 4 + g, :].rearrange("p (b d) -> p b d", b=CI),
                                     ACT.Copy).then_inc(s["ybs"], 1)
            for g in range(NC):
                squares(2, g)
                if g:
                    deviation(2, g - 1)
            deviation(2, NC - 1)
            for g in range(NC):
                act.wait_ge(s["xs_ps"], g + 1)
                nc.scalar.activation(xs[:, CI * g:CI * g + CI, :], PS[0:T, g, :].rearrange("p (b d) -> p b d", b=CI),
                                     ACT.Copy).then_inc(s["xss"], 1)
            act.wait_ge(s["st4"], 1)
            link(nc.scalar.activation(lnv[:, 1, :], mv[:, :, 1], ACT.Ln, bias=vec(V_EPS, T)))
            nc.scalar.activation(lnv[:, 2, :], lnv[:, 1, :], ACT.Exp, scale=-0.5).then_inc(s["sdv4"], 1)
            act.wait_ge(s["st4"], 2)
            link(nc.scalar.activation(lnv[:, 1, :], lnv[:, 3, :], ACT.Ln, bias=vec(V_EPS, T)))
            nc.scalar.activation(lnv[:, 5, :], lnv[:, 1, :], ACT.Exp, scale=-0.5).then_inc(s["sdv4"], 1)
            act.wait_ge(s["st4"], 4)
            for c in range(NC):
                b = c * CI + 2
                nc.scalar.activation(yn5[0:T, b, :], h3[:, b, :], ACT.Identity, scale=lnv[:, 6, b:b + 1],
                                     bias=lnv[:, 7, b:b + 1]).then_inc(s["yn5a"], 1)
            nc.scalar.preload_act_table_set("silu_and_others")

            def shared_silu(k):
                act.wait_ge(s["s1_ps"], k + 1)
                nc.scalar.activation(s1[:, k % 2, cs(k // 2)], PS[:, 6 + k % 2, 0:CT], ACT.Silu,
                                     bias=bs1[:, k % 2:k % 2 + 1]).then_inc(s["s1s"], 1)

            for k in range(3):
                shared_silu(k)
            act.wait_ge(s["w12a"], 1)
            nc.scalar.activation(wk[:, 1, :], wk[:, 0, :], ACT.Tanh, scale=0.5 / 0.7).then_inc(s["w12e"], 1)
            for k in range(3, SH_EARLY):
                shared_silu(k)
            act.wait_ge(s["blk_ps"], 1)
            nc.scalar.activation(bexp[:, :], PS[0:1, 3, 400:400 + NCOL], ACT.Copy).then_inc(s["blks"], 1)
            nc.scalar.activation(b1blk[:, :, :].rearrange("p c i -> p (c i)"), PS[:, 3, 0:4 * NCOL], ACT.Copy)
            for k in range(SH_EARLY, 2 * NC):
                shared_silu(k)
            for g in range(3):
                part = slice(512 * g, min(N, 512 * g + 512))
                act.wait_ge(s["cmb_ps"], g + 1)
                nc.scalar.activation(cmbT[0:E1, part], PS[0:E1, g, 0:part.stop - part.start], ACT.Copy).then_inc(s["cmb_sb"], 1)

            act.wait_ge(s["blks"], 2)
            act_trips = act.value_load(trips[0:1, 0:1], min_val=1, max_val=NCOL // U - 1)
            act.wait_ge(s["p_io"], 1)

            act.wait_ge(s["y_clear"], 16)
            y_blocks = yrow_dram.rearrange("(n p) d -> n p d", p=CAP)

            def leave(j, seen, at):
                act.wait_ge(s["y_ps"], seen)
                nc.scalar.activation(ysb[:, j, :], PS[:, U + j, 128:256], ACT.Copy).then_inc(s["ysbs"], 1)
                act.wait_ge(s["ysbs"], seen)
                act.dma_start(y_blocks[bass.ds(at, 1)].rearrange("o p d -> (o p) d"), ysb[:, j, :])\
                    .then_inc(s[f"yr_out{j}"], 16)

            def act_body(it, first):
                for j in range(U):
                    act.wait_ge(s["hps"], it * U + (j + 1))
                    nc.scalar.activation(hs[:, j, :], hpre[:, j, :], ACT.Silu).then_inc(s["hss"], 1)
                    if not first:
                        act.wait_ge(s[f"yr_out{(j - 1) % U}"], it * 16)
                    leave((j - 1) % U, it * U + (j + 1), it * U + j)

            act_body(0, True)
            with act.Fori(1, act_trips) as it:
                act_body(it, False)
            act.wait_ge(s[f"yr_out{U - 1}"], act_trips * 16)
            leave(U - 1, act_trips * U + 1, act_trips * U)

            def normalise(c):
                lo, hi = TAIL[c]
                act.wait_ge(s["nrm"], c + 1)
                for g in range(lo, hi):
                    r = rows(g)
                    last = nc.scalar.activation(xf[0:r, g, :], base2[0:r, g, :], ACT.Identity, scale=nw[0:r, 1, g:g + 1],
                                                bias=nw[0:r, 3, g:g + 1])
                last.then_inc(s["xfs"], 1)

            for c, (lo, hi) in enumerate(TAIL):
                cols_c = slice(128 * lo, min(N, 128 * hi))
                normalise(c)
                act.wait_ge(s["xf_ps"], c + 1)
                nc.scalar.activation(ff[:, cols_c], PS[:, c % 2, 0:cols_c.stop - cols_c.start], ACT.Identity,
                                     scale=col(GF), bias=col(BF)).then_inc(s["ffs"], 1)
                for f in range(4):
                    act.wait_ge(s["f1_ps"], 4 * c + f + 1)
                    nc.scalar.activation(fs[:, f, cols_c], PS[:, 2 + f, 0:cols_c.stop - cols_c.start], ACT.Silu,
                                         bias=bf1[:, f:f + 1]).then_inc(s["fss"], 1)
        @block.vector
        def _(dve):
            v = nc.vector
            n_link = [0]

            def link(ins):
                n_link[0] += 1
                ins.then_inc(s["d_ch"], 1)
                dve.wait_ge(s["d_ch"], n_link[0])

            v.memset(kpad[:, 0:T - 1], 0.0)
            link(v.memset(mask[:, :, :], 1.0))
            link(v.memset(mask[:, :, 0:1], 0.0))
            v.memset(two[:, :], 2.0)
            v.memset(ones_b[:, :], 1.0)
            dve.wait_ge(s["feps_f"], 1)
            link(v.tensor_tensor(feps[:, 0:262], fabs, fsgn, ALU.mult))
            v.tensor_tensor(feps[:, 264:266], feps[:, 264:266], feps[:, 260:262], ALU.mult)
            dve.wait_ge(s["tokw_in"], 16)
            sw = tokw[:, 4:8, :].rearrange("p (k h) o -> p k h o", k=2)
            eps_out = feps[:, 4:260].rearrange("p (k o) -> p k o", k=2)
            link(v.tensor_tensor(sw, sw, spread(eps_out, 2, 2), ALU.mult))
            for q in range(4):
                v.scalar_tensor_tensor(tokw[:, q, :], tokw[:, 4 + q, :], feps[:, q:q + 1], tokw[:, q, :],
                                       ALU.mult, ALU.add).then_inc(s["wn"], 1)
            link(v.tensor_tensor(bcol[:, :], feps[:, 262:264], feps[:, 264:266], ALU.add))

            dve.wait_ge(s["ssm_in"], 16)
            link(v.tensor_scalar(q64[:, 2, :], lam[:, 0, :], 1e-8, None, ALU.add))
            v.tensor_tensor(q64[:, 3, :], q64[:, 2, :], q64[:, 2, :], ALU.mult)
            link(v.tensor_tensor(q64[:, 4, :], lam[:, 1, :], lam[:, 1, :], ALU.mult))
            link(v.tensor_tensor(q64[:, 3, :], q64[:, 3, :], q64[:, 4, :], ALU.add))
            v.reciprocal(q64[:, 3, :], q64[:, 3, :]).then_inc(s["lam2"], 1)

            hf = [slice(c * CL, (c + 1) * CL) for c in range(NC)]

            def gated(c):
                h = hf[c]
                dve.wait_ge(s["inv"], c + 1)
                link(v.tensor_tensor(gate[:, h], gate[:, h], emis[:, h], ALU.mult))
                link(v.scalar_tensor_tensor(gate[:, h], PS[:, LN_XC[0][c], 0:CL], bcol[:, 0:1], gate[:, h], ALU.add, ALU.mult))
                v.scalar_tensor_tensor(gate[:, h], PS[:, 4 + c, 0:CL], bcol[:, 1:2], gate[:, h], ALU.add, ALU.mult)\
                    .then_inc(s["gated"], 1)

            def embedded(c):
                dve.wait_ge(s["tok_ps"], c + 1)
                v.tensor_tensor(h0v[:, CI * c:CI * c + CI, 1:T], PS[:, 4 + c, 0:CL].rearrange("p (b l) -> p b l", b=CI),
                                spread(peb[:, :], 1, CI), ALU.add).then_inc(s["h0s"], 1)

            dve.wait_ge(s["small_in"], 16)
            dve.wait_ge(s["attw_in"], 16)
            dve.wait_ge(s["ssm_in"], 16)
            dve.wait_ge(s["mexp"], 1)
            v.tensor_scalar(q64[:, 0, :], lam[:, 0, :], dt[:, :], None, ALU.mult)
            v.tensor_scalar(q64[:, 1, :], lam[:, 1, :], dt[:, :], 1.0 / (2.0 * math.pi), ALU.mult, ALU.mult)\
                .then_inc(s["dtl"], 1)
            dve.wait_ge(s["cst_in"], 16)
            v.tensor_scalar(winsw[:, 64:128], winsw[:, 64:128], -1.0, None, ALU.mult)
            v.tensor_scalar(col(BANG), col(BANG), 1.0 / (2.0 * math.pi), None, ALU.mult)
            v.tensor_scalar(col(BDEC), col(BDEC), 0.5, None, ALU.mult)
            v.tensor_tensor(col(BISW), col(BISW), vec(V_SGN), ALU.mult).then_inc(s["attw"], 1)
            v.tensor_scalar(peb[:, :], cst[:, C_PE:C_PE + L], col(B3), None, ALU.add)
            h0v = h0.rearrange("p (b t) -> p b t", b=NI)
            link(v.tensor_copy(h0v[:, :, 0], col(CLS).to_broadcast([128, NI])))
            def bounded(c):
                dve.wait_ge(s["gi_ps"], c + 1)
                v.tensor_scalar(gmin[:, hf[c]], PS[:, LN_XC[0][c], 0:CL], bcol[:, 0:1], 20.0, ALU.add, ALU.min)\
                    .then_inc(s["gmn"], 1)

            bounded(0)
            for c in range(NC):
                if c + 1 < NC:
                    bounded(c + 1)
                dve.wait_ge(s["mexp"], c + 2)
                h = hf[c]
                v.scalar_tensor_tensor(gate[:, h], emis[:, h], 2.0, emis[:, h], ALU.add, ALU.mult).then_inc(s["numer"], 1)
                if c:
                    gated(c - 1)
                if c >= 2:
                    embedded(c - 2)
            gated(NC - 1)
            embedded(NC - 2)
            embedded(NC - 1)

            dve.wait_ge(s["args"], 2)
            link(v.tensor_scalar(pS, pTI, MAGIC, -MAGIC, ALU.add, ALU.add))
            v.tensor_tensor(pTI, pTI, pS, ALU.subtract).then_inc(s["fracs"], 1)

            def normalise(k, c):
                dve.wait_ge(s["sdv"], 4 * k + c + 1)
                dst, xc, rec = xn[:, cs(c)], PS[:, LN_XC[k][c], 0:CT], sd[:, cs(c)]
                if k == 2:
                    dst, xc, rec = [z.rearrange("p (b t) -> p b t", b=CI) for z in (dst, xc, rec)]
                    dst = dst[:, :, ::-1]
                v.tensor_tensor(dst, xc, rec, ALU.mult).then_inc(s["xnr"], 1)

            for c in range(NC):
                normalise(0, c)

            flat_mask = mask[:, :, :].rearrange("p a b -> p (a b)")

            def phases(c):
                r = ring4[c]
                dve.wait_ge(s["pj_ps"], c + 1)
                link(v.tensor_scalar(r[:, AN], PS[:, PJ[c % 2][0], 0:CT], 1.0 / (2.0 * math.pi), col(BANG), ALU.mult, ALU.add))
                link(v.tensor_tensor_scan(r[:, TH], flat_mask, r[:, AN], 0.0, ALU.mult, ALU.add))
                link(v.tensor_scalar(r[:, RM], r[:, TH], MAGIC, -MAGIC, ALU.add, ALU.add))
                v.tensor_tensor(r[:, FR], r[:, TH], r[:, RM], ALU.subtract).then_inc(s["frac"], 1)

            def recur(c):
                r = ring4[c]
                dve.wait_ge(s["sc"], c + 1)
                dve.wait_ge(s["uv_ps"], c + 1)
                v.scalar_tensor_tensor(r[:, CU], PS[:, PJ[c % 2][2], 0:CT], col(BI), r[:, CS_], ALU.add, ALU.mult)
                link(v.scalar_tensor_tensor(r[:, SU], PS[:, PJ[c % 2][3], 0:CT], col(BISW), r[:, SN], ALU.add, ALU.mult))
                link(v.tensor_tensor(r[:, GI], r[:, CU], r[:, SU], ALU.add))
                dve.wait_ge(s["decs"], c + 1)
                link(v.tensor_tensor_scan(r[:, GS], r[:, DEC], r[:, GI], 0.0, ALU.mult, ALU.add))
                v.tensor_tensor(r[:, RM], r[:, CS_], r[:, GS], ALU.mult)
                v.tensor_tensor(r[:, AN], r[:, SN], r[:, GS], ALU.mult).then_inc(s["rot"], 1)

            phases(0)
            phases(1)
            recur(0)
            phases(2)
            recur(1)
            phases(3)
            recur(2)
            recur(3)

            for c in range(NC):
                normalise(1, c)

            dve.wait_ge(s["lg0_ps"], 1)
            lg0 = PS[0:T, 4, 0:128].rearrange("p (b e) -> p b e", b=NI)
            smv = [sm[:, k, :].rearrange("p (b e) -> p b e", b=NI) for k in range(3)]
            link(v.tensor_reduce(smr[:, 0, :], lg0, AX, ALU.max))
            v.tensor_tensor(smv[0], lg0, spread(smr[:, 0, :], 2, E0), ALU.subtract).then_inc(s["smx"], 1)
            dve.wait_ge(s["smx_e"], 1)
            link(v.tensor_reduce(smr[:, 1, :], smv[1], AX, ALU.add))
            link(v.reciprocal(smr[:, 1, :], smr[:, 1, :]))
            v.tensor_tensor(smv[2], smv[1], spread(smr[:, 1, :], 2, E0), ALU.mult).then_inc(s["sms"], 1)
            dve.wait_ge(s["st_ps"], 1)
            link(v.tensor_copy(rt0[:, 0, :], PS[:, 5, 0:T]))
            link(v.max(top8[:, 0, :], rt0[:, 0, :]))
            link(v.match_replace(rt0[:, 1, :], top8[:, 0, :], rt0[:, 0, :], -1.0))
            link(v.max(top8[:, 1, :], rt0[:, 1, :]))
            link(v.match_replace(rt0[:, 2, :], top8[:, 1, :], rt0[:, 1, :], -1.0))
            link(v.tensor_scalar(rt0[:, 3, :], rt0[:, 2, :], 0.0, None, ALU.is_lt))
            link(v.tensor_tensor_scan(rt0[:, 4, :], rt0[:, 3, :], rt0[:, 3, :], 0.0, ALU.add, ALU.max))
            v.tensor_tensor(rt0[:, 5, :], rt0[:, 4, :], rt0[:, 3, :], ALU.mult).then_inc(s["route0"], 1)
            dve.wait_ge(s["pt_ps"], 1)
            for c in range(NC):
                ce = slice(c * CI * E0, (c + 1) * CI * E0)
                v.tensor_tensor(sel[0:T, ce], spread(PS[0:T, 4, ce], 2, K0),
                                spread(cst[0:T, C_K16:C_K16 + K0], 1, CI * E0), ALU.is_equal).then_inc(s["sels"], 1)
            dve.wait_ge(s["sels"], NC)
            v.tensor_tensor(selw[0:T], sel[0:T], spread(sm[:, 2, :], 2, K0), ALU.mult).then_inc(s["selw"], 1)
            for g in range(NC):
                dve.wait_ge(s["sg_ps"], g + 1)
                v.tensor_copy(selG[:, g, :], PS[:, 4 + g, 0:CT]).then_inc(s["selg"], 1)

            def outputs(e):
                dve.wait_ge(s["y0_ps"], e + 1)
                v.tensor_scalar(yT[:, :, e, :], PS[:, 2 + e % 2, 0:SL].rearrange("p (b k) -> p b k", b=NI),
                                bT[:, 2, e:e + 1], None, ALU.add).then_inc(s["y0s"], 1)

            for e in range(E0):
                outputs(e)
                if 1 <= e <= 5:
                    lo, hi = KSUM[e - 1], KSUM[e]
                    dve.wait_ge(s["prods"], -(-hi // PB))
                    last = v.tensor_reduce(kpad[:, T - 1 + lo:T - 1 + hi], prod[:, lo:hi, :], AX, ALU.add)
                    if e == 5:
                        link(last)
                        v.tensor_tensor(kpad[:, T - 1:T], kpad[:, T - 1:T], col(DD), ALU.add).then_inc(s["kpads"], 1)
            for g in (1, 3):
                dve.wait_ge(s["yt_ps"], g + 1)
                v.tensor_copy(Yb[:, CI * g:CI * g + CI, :], PS[:, 4 + g, :].rearrange("p (b d) -> p b d", b=CI))\
                    .then_inc(s["ybs"], 1)
            def h2_copy(c):
                dve.wait_ge(s["h2_ps"], c + 1)
                v.tensor_copy(h2[:, cs(c)], PS[:, c, 0:CT]).then_inc(s["h2s"], 1)

            h2_copy(0)
            h2_copy(1)
            for c in range(NC):
                if c + 2 < NC:
                    h2_copy(c + 2)
                normalise(2, c)
            for g in range(NC):
                dve.wait_ge(s["h2t_ps"], g + 1)
                link(v.tensor_copy(h2t[:, CI * g:CI * g + CI, :], PS[0:T, 4 + g, :].rearrange("p (b d) -> p b d", b=CI)))
            for g in range(NC):
                dve.wait_ge(s["cv_ps"], g + 1)
                v.tensor_tensor(h3[:, :, 32 * g:32 * g + 32], PS[0:T, g, :].rearrange("p (h b) -> p b h", b=NI),
                                h2t[:, :, 32 * g:32 * g + 32], ALU.add).then_inc(s["h3s"], 1)
                dve.wait_ge(s["h3s"], g + 1)
                for b in range(NI):
                    last = v.bn_stats(lnst[:, b, g, :], h3[:, b, 32 * g:32 * g + 32])
            link(last)
            for b in range(NI):
                last = v.bn_aggr(mv[:, b, :], lnst[:, b, :, :].rearrange("p q k -> p (q k)"))
            last.then_inc(s["st4"], 1)
            dve.wait_ge(s["wc_ps"], 1)
            v.tensor_copy(wc[:, :], PS[:, 3, 0:E1]).then_inc(s["wcs"], 1)
            dve.wait_ge(s["sdv4"], 1)
            link(v.tensor_tensor(lnv[:, 3, :], lnv[:, 2, :], lnv[:, 2, :], ALU.mult))
            v.tensor_tensor(lnv[:, 3, :], lnv[:, 3, :], mv[:, :, 1], ALU.mult).then_inc(s["st4"], 1)
            v.tensor_scalar(lnv[:, 0, :], lnv[:, 2, :], 1.0, None, ALU.add)
            v.scalar_tensor_tensor(lnv[:, 4, :], mv[:, :, 0], -1.0, lnv[:, 2, :], ALU.mult, ALU.mult).then_inc(s["st4"], 1)
            v.memset(h5[:, N:NP], 0.0)
            v.tensor_scalar(bs2, bs2, 0.25, None, ALU.mult)
            v.tensor_copy(before[:, :], cst[:, C_UPP:C_UPP + 128])
            dve.wait_ge(s["sdv4"], 2)
            link(v.tensor_tensor(lnv[:, 6, :], lnv[:, 5, :], lnv[:, 2, :], ALU.mult))
            v.scalar_tensor_tensor(lnv[:, 7, :], mv[:, :, 0], -1.0, lnv[:, 6, :], ALU.mult, ALU.mult).then_inc(s["st4"], 1)
            for c in range(NC):
                for b in (c * CI, c * CI + 1):
                    last = v.tensor_scalar(yn5[0:T, b, :], h3[:, b, :], mv[:, b, 0:1], lnv[:, 6, b:b + 1], ALU.subtract, ALU.mult)
                last.then_inc(s["yn5s"], 1)
            for c in range(NC):
                dve.wait_ge(s["h5_ps"], c + 1)
                v.tensor_scalar(h5[:, cs(c)], PS[:, 4 + c, 0:CT], col(G1), col(B1), ALU.mult, ALU.add).then_inc(s["h5s"], 1)
            v.tensor_scalar(ws2, ws2, 0.25, None, ALU.mult)
            v.tensor_scalar(tri_cap[:, :], cst[0:E1, C_TRI:C_TRI + E1], float(CAP), None, ALU.mult).then_inc(s["bfc"], 1)

            for b in range(NG):
                dve.wait_ge(s["lg_ps"], in_chunk(b) + 1)
                last = v.max(mx8[:, b, :], scores(b))
            link(last)
            for b in range(NG):
                last = v.max_index(ix8[:, b, :], mx8[:, b, :], scores(b))
            link(last)
            v.tensor_tensor(wk[:, 0, :], mx8[:, :, 1], mx8[:, :, 0], ALU.subtract).then_inc(s["w12a"], 1)
            link(v.tensor_copy(ef[:, :, :].rearrange("p k b -> p b k"), ix8[:, :, 0:2]))
            for k in range(2):
                last = v.tensor_tensor(oh[:, k, :].rearrange("p (g e) -> p g e", g=NG), spread(cst[:, C_IOTA:C_IOTA + E1], 1, NG),
                                       spread(ef[:, k, :], 2, E1), ALU.is_equal)
            link(last)
            v.tensor_tensor(ohs[:, :], oh[:, 0, :], oh[:, 1, :], ALU.add).then_inc(s["ohss"], 1)
            dve.wait_ge(s["w12e"], 1)
            v.tensor_scalar(wts[:, 0, :], wk[:, 1, :], -0.5, 0.5, ALU.mult, ALU.add)
            v.tensor_scalar(wts[:, 1, :], wk[:, 1, :], 0.5, 0.5, ALU.mult, ALU.add).then_inc(s["w12"], 1)
            dve.wait_ge(s["cnt_ps"], 1)
            link(v.tensor_scalar(esm[:, 0:1], PS[0:E1, 0, 0:1], 1.0 / CAP, (CAP - 1.0) / CAP - 0.498, ALU.mult, ALU.add))
            link(v.tensor_scalar(esm[:, 1:2], esm[:, 0:1], MAGIC, -MAGIC, ALU.add, ALU.add))
            v.tensor_copy(nblk_b[:, :], esm[:, 1:2].to_broadcast([E1, 128])).then_inc(s["nblks"], 1)
            dve.wait_ge(s["cnt_ps"], 2)
            v.tensor_scalar(esm[0:1, 6:7], PS[0:1, 0, 8:9], 1.0 / U, (U - 1.0) / U - 0.4, ALU.mult, ALU.add)
            v.tensor_tensor(esm[:, 4:5], PS[0:E1, 0, 0:1], esm[:, 1:2], ALU.add)
            link(v.tensor_copy(esm[:, 2:3], PS[0:E1, 0, 0:1]))
            v.tensor_scalar(trips[:, :], esm[0:1, 6:7], MAGIC, -MAGIC, ALU.add, ALU.add).then_inc(s["blks"], 1)
            link(v.tensor_scalar(obk[:, 0, :], cst[0:E1, C_IOTA:C_IOTA + NCOL], esm[:, 4:5], None, ALU.is_lt))
            v.scalar_tensor_tensor(obk[:, 1, :], cst[0:E1, C_IOTA:C_IOTA + NCOL], esm[:, 2:3], obk[:, 0, :], ALU.is_ge, ALU.mult)\
                .then_inc(s["obks"], 1)
            dve.wait_ge(s["slt_ps"], 1)
            slt = PS[:, 4:6, :].rearrange("p a b -> p (a b)")[:, 0:NG * E1]
            for k in range(2):
                last = v.tensor_tensor(sprod[:, k, :], oh[:, k, :], slt, ALU.mult)
            link(last)
            link(v.tensor_reduce(slot[:, 0, :], sprod.rearrange("p k (b e) -> p (k b) e", e=E1), AX, ALU.add))
            v.tensor_scalar(yix[:, :], slot[:, 0, :], float(CAP), None, ALU.add)
            link(v.tensor_scalar(slot[:, 1, :], slot[:, 0, :], 1.0 / CAP, -0.498, ALU.mult, ALU.add))
            link(v.tensor_scalar(slot[:, 2, :], slot[:, 1, :], MAGIC, -MAGIC, ALU.add, ALU.add))
            v.tensor_copy(slotb[:, 1, :], slot[:, 2, :])
            link(v.scalar_tensor_tensor(slotb[:, 0, :], slot[:, 2, :], -float(CAP), slot[:, 0, :], ALU.mult, ALU.add))
            dve.wait_ge(s["iots"], 2)
            v.tensor_tensor(ohA, iotb, spread(slotb[:, 0, :], 1, CAP), ALU.is_equal)
            link(v.tensor_tensor(ohB[:, 0], iotb[:, 0:NCOL, :], spread(slotb[:, 1, :], 1, NCOL), ALU.is_equal))
            v.tensor_scalar(ohB[:, 1], ohB[:, 0], vec(V_T), None, ALU.mult)
            v.tensor_tensor(ohB[:, 2], ohB[:, 0], spread(cvb[:, :], 1, NCOL), ALU.mult).then_inc(s["tabs_in"], 1)
            dve.wait_ge(s["tab_ps"], 1)
            link(v.tensor_copy(tabf[:, 0:3, :].rearrange("p a b -> p (a b)"), PS[:, 5, 0:3 * NCOL]))
            v.scalar_tensor_tensor(tabf[:, 3, :], tabf[:, 2, :], 128.0, tabf[:, 1, :], ALU.mult, ALU.add)
            link(v.tensor_scalar(tabf[:, 4, :], tabf[:, 0, :], -BIG, BIG, ALU.mult, ALU.add))
            v.tensor_tensor(tabx[:, :], tabf[:, 3, :], tabf[:, 4, :], ALU.add).then_inc(s["tabs"], 1)
            dve.wait_ge(s["x_out"], 16)
            for g in range(3):
                lo, hi = 4 * g, min(4 * g + 4, NG)
                r = rows(hi - 1)
                dve.wait_ge(s["sh_ps"], g + 1)
                v.tensor_tensor(base2[0:r, lo:hi, :], PS[0:r, g, 0:(hi - lo) * D].rearrange("p (b d) -> p b d", d=D),
                                spread(bs2[0:r, :], 1, hi - lo), ALU.add).then_inc(s["b2s"], 1)

            dve.wait_ge(s["blks"], 2)
            dve_trips = dve.value_load(trips[0:1, 0:1], min_val=1, max_val=NCOL // U - 1)
            dve.wait_ge(s["p_io"], 1)

            def tokens(j, seen):
                dve.wait_ge(s["t_ps"], seen)
                v.tensor_scalar(xsr[:, j, :], PS[:, U + j, 0:CAP], col(G1), col(B1), ALU.mult, ALU.add).then_inc(s["t_sb"], 1)

            tokens(0, 1)
            with dve.Fori(0, dve_trips) as it:
                for j in range(U):
                    tokens((j + 1) % U, it * U + (j + 2))
                    dve.wait_ge(s["hss"], it * U + (j + 1))
                    dve.wait_ge(s["h_ps"], it * U + (j + 1))
                    bias = b1blk[:, :, bass.ds(it * U + j, 1)].to_broadcast([128, 4, CAP])
                    v.tensor_tensor(hpre[:, j, :].rearrange("p (c q) -> p c q", c=4),
                                    PS[:, j, :].rearrange("p (c q) -> p c q", c=4), bias, ALU.add).then_inc(s["hps"], 1)

            v.memset(mv6[:, :, :], 1.0)
            dve.wait_ge(s["rr_in"], 32)
            link(v.tensor_tensor(resg[:, 0:NG - 1, :], resg[:, 0:NG - 1, :], spread(bf2[:, :], 1, NG - 1), ALU.add))
            v.tensor_tensor(resg[0:rows(NG - 1), NG - 1, :], resg[0:rows(NG - 1), NG - 1, :], bf2[0:rows(NG - 1), :],
                            ALU.add).then_inc(s["resb"], 1)
            dve.wait_ge(s["w12"], 1)
            dve.wait_ge(s["b2s"], 3)

            def combine(c):
                for part, (lo, hi) in enumerate(LOADS):
                    if not TAIL[c][0] <= lo < TAIL[c][1]:
                        continue
                    dve.wait_ge(s[f"yl_in{part}"], 32 * (hi - lo))
                    for k in range(2):
                        for g in range(lo, hi):
                            r = rows(g)
                            last = v.scalar_tensor_tensor(base2[0:r, g, :], yl[0:r, k * NG + g, :], wts[0:r, k, g:g + 1],
                                                          base2[0:r, g, :], ALU.mult, ALU.add)
                        if k == 0:
                            link(last)
                    if hi < TAIL[c][1]:
                        link(last)
                last.then_inc(s["hms"], 1)

            def moments(c):
                lo, hi = TAIL[c]
                r = 128
                dve.wait_ge(s["hms"], c + 1)
                for g in range(lo, hi):
                    last = v.bn_stats(st6[0:rows(g), g, :], base2[0:rows(g), g, :])
                link(last)
                for g in range(lo, hi):
                    last = v.bn_aggr(mv6[0:rows(g), g, :], st6[0:rows(g), g, :])
                link(last)
                half, y, w, off = [nw[0:r, k, lo:hi] for k in range(4)]
                link(v.tensor_scalar(half, mv6[0:r, lo:hi, 1], EPS, -0.5, ALU.add, ALU.mult))
                link(v.tensor_scalar(nwi[0:r, lo:hi], half.bitcast(I32), -0.5, SQRT_GUESS, ALU.mult, ALU.add))
                guess = nwi[0:r, lo:hi].bitcast(F32)
                for k in range(3):
                    z = guess if k == 0 else y
                    for g in range(hi - lo):
                        last = v.scalar_tensor_tensor(w[:, g:g + 1], z[:, g:g + 1], half[:, g:g + 1], z[:, g:g + 1],
                                                      ALU.mult, ALU.mult)
                    link(last)
                    link(v.scalar_tensor_tensor(y, w, 1.5, z, ALU.add, ALU.mult))
                v.scalar_tensor_tensor(off, mv6[0:r, lo:hi, 0], -1.0, y, ALU.mult, ALU.mult).then_inc(s["nrm"], 1)

            def finish(c):
                lo, hi = TAIL[c]
                dve.wait_ge(s["f2_ps"], c + 1)
                dve.wait_ge(s["res"], c + 2)
                for g, end, r in even(lo, hi):
                    bank = PS[0:r, 6 + c % 2, (g - lo) * D:(end - lo) * D]
                    last = v.tensor_tensor(resg[0:r, g:end, :], bank.rearrange("p (b d) -> p b d", d=D),
                                           resg[0:r, g:end, :], ALU.add)
                last.then_inc(s["fins"], 1)

            for c in range(len(TAIL)):
                combine(c)
                moments(c)
                if c >= 2:
                    finish(c - 2)
            for c in range(len(TAIL) - 2, len(TAIL)):
                finish(c)

        @block.gpsimd
        def _(pool):
            p = nc.gpsimd
            n_link = [0]

            def link(ins):
                n_link[0] += 1
                ins.then_inc(s["p_ch"], 1)
                pool.wait_ge(s["p_ch"], n_link[0])

            p.memset(zeros[:, :], 0.0).then_inc(s["zero"], 1)
            def q(k):
                return q64[:, k, :]

            def tt(o, x, y, op):
                link(p.tensor_tensor(o, x, y, op))

            def cmul(re, im_, ar, ai, br, bi, z):
                p.tensor_tensor(z, ai, bi, ALU.mult)
                tt(re, ar, br, ALU.mult)
                tt(re, re, z, ALU.subtract)
                p.tensor_tensor(z, ar, bi, ALU.mult)
                tt(im_, ai, br, ALU.mult)
                tt(im_, im_, z, ALU.add)

            pool.wait_ge(s["ssm_in"], 16)
            cmul(q(6), q(7), bc4[:, 2, :], bc4[:, 3, :], bc4[:, 0, :], bc4[:, 1, :], q(10))
            pool.wait_ge(s["lam2"], 1)
            p.tensor_tensor(q(8), q(6), q(2), ALU.mult)
            p.tensor_tensor(q(9), q(7), q(2), ALU.mult)
            p.tensor_tensor(q(10), q(7), lam[:, 1, :], ALU.mult)
            tt(q(11), q(6), lam[:, 1, :], ALU.mult)
            p.tensor_tensor(q(8), q(8), q(10), ALU.add)
            tt(q(9), q(9), q(11), ALU.subtract)
            p.tensor_tensor(q(8), q(8), q(3), ALU.mult)
            tt(q(9), q(9), q(3), ALU.mult)
            pool.wait_ge(s["cst_in"], 16)
            pool.wait_ge(s["dtl"], 1)
            powers = spread(cst[:, C_PWR:C_PWR + NPW], 2, NS)
            for k, dst in enumerate((pAR, pTI)):
                p.tensor_tensor(dst, powers, spread(q64[:, k, :], 1, NPW), ALU.mult).then_inc(s["args"], 1)

            pool.wait_ge(s["h0s"], 1)
            for c in range(NC):
                last = p.memset(ring4[c][:, DEC], 0.0)
            link(last)
            for c in range(NC):
                r = ring4[c]
                pool.wait_ge(s["tdec"], c + 1)
                td = r[:, TD].rearrange("p (b t) -> p b t", b=CI)[:, :, 1:T]
                de = r[:, DEC].rearrange("p (b t) -> p b t", b=CI)[:, :, 1:T]
                p.tensor_scalar(de, td, 0.5, 0.5, ALU.mult, ALU.add).then_inc(s["decs"], 1)

            pool.wait_ge(s["trg"], 3)
            p.tensor_tensor(VV[:, :, 0, :], pE, pC, ALU.mult)
            link(p.tensor_tensor(VV[:, :, 1, :], pE, pS, ALU.mult))
            link(p.tensor_scalar(q(5), VV[:, 1, 0, :], -1.0, None, ALU.add))
            cmul(q(12), q(13), q(8), q(9), q(5), VV[:, 1, 1, :], q(10))
            link(p.tensor_scalar(q(10), q(12), -1.0, None, ALU.mult))
            va = [VV[:, PB:NPW, k, :] for k in range(2)]
            t0, t1 = pE[:, 0:PA, :], pS[:, 0:PA, :]

            def fac(k):
                return spread(q64[:, k, :], 1, PA)

            p.tensor_tensor(t0, va[0], fac(12), ALU.mult)
            link(p.tensor_tensor(t1, va[1], fac(13), ALU.mult))
            link(p.tensor_tensor(UU[:, :, 0, :], t0, t1, ALU.subtract))
            p.tensor_tensor(t0, va[1], fac(10), ALU.mult)
            link(p.tensor_tensor(t1, va[0], fac(13), ALU.mult))
            link(p.tensor_tensor(UU[:, :, 1, :], t0, t1, ALU.subtract))
            uf = UU.rearrange("p a c n -> p a (c n)")
            vf = VV.rearrange("p a c n -> p a (c n)")
            pool.wait_ge(s["out_ps"], 4)
            for q_ in range(PA - 1):
                p.tensor_tensor(prod[:, PB * q_:PB * q_ + PB, :], spread(uf[:, q_, :], 1, PB), vf[:, 0:PB, :], ALU.mult)\
                    .then_inc(s["prods"], 1)
            p.tensor_tensor(prod[:, T - 1, :], uf[:, PA - 1, :], vf[:, 0, :], ALU.mult).then_inc(s["prods"], 1)

            pool.wait_ge(s["cv_ps"], 4)
            p.iota(iotb, [[1, CAP], [0, NJ]], base=0, channel_multiplier=0, allow_small_or_imprecise_dtypes=True)\
                .then_inc(s["iots"], 1)
            p.iota(cvb[:, :].rearrange("p (k g) -> p k g", k=2), [[0, 2], [1, NG]], base=0, channel_multiplier=0, allow_small_or_imprecise_dtypes=True)\
                .then_inc(s["iots"], 1)
            pool.wait_ge(s["st4"], 4)
            for b in range(3, NI, CI):
                p.tensor_scalar(yn5[0:T, b, :], h3[:, b, :], lnv[:, 6, b:b + 1], lnv[:, 7, b:b + 1], ALU.mult, ALU.add)\
                    .then_inc(s["yn5p"], 1)
            for b in range(NI):
                last = p.tensor_scalar(hres[:, b, :], h3[:, b, :], lnv[:, 0, b:b + 1], lnv[:, 4, b:b + 1], ALU.mult, ALU.add)
            last.then_inc(s["res"], 1)
            pool.wait_ge(s["w12"], 1)
            ohv = [oh[:, k, :].rearrange("p (b e) -> p b e", b=NG) for k in range(2)]
            tmp = carve(h2, [[NG, E1]])[0]
            p.tensor_tensor(cmb, ohv[0], spread(wts[:, 0, :], 2, E1), ALU.mult)
            link(p.tensor_tensor(tmp, ohv[1], spread(wts[:, 1, :], 2, E1), ALU.mult))
            p.tensor_tensor(cmb, cmb, tmp, ALU.add).then_inc(s["cmbs"], 1)
            p.memset(xg, 0.0)
            p.memset(hs[:, U - 1, :], 0.0).then_inc(s["hss"], U)
            p.memset(w2r[:, U - 1, :], 0.0).then_inc(s["p_io"], 1)

            pool.wait_ge(s["blks"], 2)
            pool_trips = pool.value_load(trips[0:1, 0:1], min_val=1, max_val=NCOL // U - 1)
            last_x = pool.to_reg(N - 1)
            last_y = pool.to_reg(NOUT * CAP - 1)
            pool.wait_ge(s["tabs"], 1)
            pool.wait_ge(s["x_out"], 16)
            pool.wait_ge(s["p_io"], 1)

            def gather(j):
                pool.indirect_dma_start(out=xg[:, j, :], out_offset=None, in_=xrow_dram,
                                        in_offset=bass.IndirectOffsetOnAxis(ap=ixg[:, j:j + 1], axis=0),
                                        bounds_check=last_x, oob_is_err=False).then_inc(s[f"g_in{j}"], 16)

            p.tensor_copy(ixg[:, 0:U - 1], tabx[:, 0:U - 1]).then_inc(s["ix_cp"], 1)
            pool.wait_ge(s["ix_cp"], 1)
            for j in range(U - 1):
                gather(j)

            def pool_body(it, first):
                for j in range(U):
                    far = (j + U - 1) % U
                    if not (first and j == 0):
                        pool.wait_ge(s["t_ps"], it * U + j)
                        pool.sem_inc(s["p_rd"], 1)
                    p.tensor_copy(ixg[:, far:far + 1], tabx[:, bass.ds(it * U + (j + U - 1), 1)]).then_inc(s["ix_cp"], 1)
                    pool.wait_ge(s["ix_cp"], it * U + (j + 2))
                    pool.sem_inc(s["p_rd"], 1)
                    gather(far)

            pool_body(0, True)
            with pool.Fori(1, pool_trips) as it:
                pool_body(it, False)
            for j in range(U):
                pool.wait_ge(s[f"yr_out{j}"], pool_trips * 16 + (16 if j == U - 1 else 0))
                pool.sem_inc(s["p_rd"], 1)
            for part, (lo, hi) in enumerate(LOADS):
                for g in range(lo, hi):
                    for q in (g, NG + g):
                        r = rows(g)
                        pool.indirect_dma_start(out=yl[0:r, q, :], out_offset=None, in_=yrow_dram,
                                                in_offset=bass.IndirectOffsetOnAxis(ap=yix[0:r, q:q + 1], axis=0),
                                                bounds_check=last_y, oob_is_err=False).then_inc(s[f"yl_in{part}"], 16)
            pool.wait_ge(s["resb"], 1)
            for c, (lo, hi) in enumerate(TAIL):
                pool.wait_ge(s["hms"], c + 1)
                for g, end, r in even(lo, hi):
                    last = p.tensor_tensor(resg[0:r, g:end, :], resg[0:r, g:end, :], base2[0:r, g:end, :], ALU.add)
                last.then_inc(s["res"], 1)


def kernel(**inputs):
    import concourse.bacc as _bacc
    from concourse.bass_utils import run_bass_kernel_spmd as _run

    nc = _bacc.Bacc("TRN2", target_bir_lowering=False, num_devices=1)
    arrays, args = {}, {}
    for name, value in packed(inputs).items():
        v = np.ascontiguousarray(value)
        arrays[f"in_{name}"] = v
        args[name] = nc.dram_tensor(f"in_{name}", v.shape, mybir.dt.from_np(v.dtype), kind="ExternalInput").ap()
    out = nc.dram_tensor("out", (NI, T, D), F32, kind="ExternalOutput").ap()
    build(nc, args, out)
    r = _run(nc, [arrays], core_ids=[0])
    return r.results[0]["out"]
```
